# Optimizing a Trainium2 kernel written in Bass

```python
import numpy as np
import jax
import jax.numpy as jnp

def _softmax(x, axis=-1):
    return jax.nn.softmax(x, axis=axis)

def _gelu(x):
    return jax.nn.gelu(x, approximate=True)

def _silu(x):
    return jax.nn.silu(x)

def _sigmoid(x):
    return jax.nn.sigmoid(x)

def _layernorm(x, axis=-1, eps=1e-05):
    m = jnp.mean(x, axis=axis, keepdims=True)
    v = jnp.var(x, axis=axis, keepdims=True)
    return (x - m) / jnp.sqrt(v + eps)

def _scatter_add(tgt, idx, src, axis=0):
    return tgt.at[idx].add(src)

def _segment_sum(src, seg, n):
    return jax.ops.segment_sum(src, seg, n)
kernel_name = 'mk_gnn_preln_d4_gnn_r32_c33542'

def setup_inputs(seed: int=0):
    np.random.seed(seed)
    _w = jnp.asarray

    def _rec_inputs():
        import jax
        import jax.numpy as jnp
        _gk = jax.random.key(seed)
        x = -0.000202 + 1 * jax.random.normal(jax.random.fold_in(_gk, 1), (50000, 128), jnp.float32)
        src = jax.random.randint(jax.random.fold_in(_gk, 2), (25000,), 0, 50000, jnp.int32)
        dst = jnp.minimum((50000 * jax.random.uniform(jax.random.fold_in(_gk, 3), (25000,)) ** 2.0).astype(jnp.int32), 49999)
        _o = jnp.argsort(dst, stable=True)
        src = src[_o]
        dst = dst[_o]
        edge_attr_128 = -8.513e-05 + 0.999844 * jax.random.normal(jax.random.fold_in(_gk, 12), (25000, 128), jnp.float32)
        edge_weight = jax.random.uniform(jax.random.fold_in(_gk, 14), (25000,), jnp.float32, 0.0, 0.999999)
        return (x, src, dst, edge_attr_128, edge_weight)
    x, src, dst, edge_attr_128, edge_weight = _rec_inputs()

    def _L0_gnn_setup():
        import jax, jax.numpy as jnp
        import numpy as np
        N = 50000
        E = 18750
        IN_CH = 128
        HEADS = 8
        HEAD_DIM = 16
        OUT_CH = 128
        NEG_SLOPE = 0.2
        LN_EPS = 1e-05
        key = jax.random.key(seed)
        ks = jax.random.split(key, 9)
        x = jax.random.normal(ks[0], (N, IN_CH), dtype=jnp.float32)
        edge_index = jax.random.randint(ks[1], (2, E), 0, N, dtype=jnp.int64)
        lin_w = jax.random.normal(ks[2], (HEADS * HEAD_DIM, IN_CH), dtype=jnp.float32) * 0.05
        att_src = jax.random.normal(ks[3], (1, HEADS, HEAD_DIM), dtype=jnp.float32) * 0.1
        att_dst = jax.random.normal(ks[4], (1, HEADS, HEAD_DIM), dtype=jnp.float32) * 0.1
        gat_bias = jnp.zeros((HEADS * HEAD_DIM,), dtype=jnp.float32)
        proj_w = jax.random.normal(ks[5], (OUT_CH, HEADS * HEAD_DIM), dtype=jnp.float32) * 0.05
        proj_b = jnp.zeros((OUT_CH,), dtype=jnp.float32)
        ln_gamma = jnp.ones((OUT_CH,), dtype=jnp.float32)
        ln_beta = jnp.zeros((OUT_CH,), dtype=jnp.float32)
        return {'x': x, 'edge_index': edge_index, 'lin_w': lin_w, 'att_src': att_src, 'att_dst': att_dst, 'gat_bias': gat_bias, 'proj_w': proj_w, 'proj_b': proj_b, 'ln_gamma': ln_gamma, 'ln_beta': ln_beta}
    _L0_gnn_all = _L0_gnn_setup()
    _L0_gnn_in = {k: v for k, v in _L0_gnn_all.items() if k in ('lin_w', 'att_src', 'att_dst', 'gat_bias', 'proj_w', 'proj_b', 'ln_gamma', 'ln_beta')}
    del _L0_gnn_all

    def _L1_gnn_setup():
        import jax, jax.numpy as jnp
        import numpy as np
        N, E, D, G, H, O = (10000, 20000, 128, 128, 512, 128)

        def mish(x):
            return x * jnp.tanh(jax.nn.softplus(x))
        key = jax.random.key(seed)
        ks = jax.random.split(key, 10)
        nodes = jax.random.normal(ks[0], (N, D), dtype=jnp.float32)
        edges = jax.random.normal(ks[1], (E, D), dtype=jnp.float32)
        globals_g = jax.random.normal(ks[2], (1, G), dtype=jnp.float32)
        senders = jax.random.randint(ks[3], (E,), 0, N)
        receivers = jax.random.randint(ks[4], (E,), 0, N)
        lim_e = np.sqrt(6.0 / (D + D)).astype(np.float32)
        W_e_k = jax.random.uniform(ks[5], (D, D), jnp.float32, -lim_e, lim_e)
        W_e_b = jnp.zeros((D,), jnp.float32)
        eps = jnp.zeros((1, 1), jnp.float32)
        lim1 = np.sqrt(6.0 / (D + G + H)).astype(np.float32)
        W1 = jax.random.uniform(ks[6], (D + G, H), jnp.float32, -lim1, lim1)
        b1 = jnp.zeros((H,), jnp.float32)
        lim2 = np.sqrt(6.0 / (H + O)).astype(np.float32)
        W2 = jax.random.uniform(ks[7], (H, O), jnp.float32, -lim2, lim2)
        b2 = jnp.zeros((O,), jnp.float32)
        return {'nodes': nodes, 'edges': edges, 'globals_g': globals_g, 'W_e_k': W_e_k, 'W_e_b': W_e_b, 'eps': eps, 'W1': W1, 'b1': b1, 'W2': W2, 'b2': b2, 'senders': senders, 'receivers': receivers}
    _L1_gnn_all = _L1_gnn_setup()
    _L1_gnn_in = {k: v for k, v in _L1_gnn_all.items() if k in ('globals_g', 'W_e_k', 'W_e_b', 'eps', 'W1', 'b1', 'W2', 'b2')}
    del _L1_gnn_all

    def _L2_gnn_setup():
        import jax, jax.numpy as jnp
        import numpy as np
        N_VAR, N_FAC, N_EDGE, D = (3125, 50000, 31250, 128)
        key = jax.random.key(seed)
        ks = jax.random.split(key, 8)
        return {'variables': jax.random.normal(ks[0], (N_VAR, D), dtype=jnp.float32), 'factors': jax.random.normal(ks[1], (N_FAC, D), dtype=jnp.float32), 'senders': jax.random.randint(ks[2], (N_EDGE,), 0, N_VAR), 'receivers': jax.random.randint(ks[3], (N_EDGE,), 0, N_FAC), 'Wm': jax.random.normal(ks[4], (2 * D, D), dtype=jnp.float32) * (1.0 / np.sqrt(2 * D)), 'bm': jnp.zeros((D,), dtype=jnp.float32), 'Wc': jax.random.normal(ks[5], (2 * D, D), dtype=jnp.float32) * (1.0 / np.sqrt(2 * D)), 'bc': jnp.zeros((D,), dtype=jnp.float32)}
    _L2_gnn_all = _L2_gnn_setup()
    _L2_gnn_in = {k: v for k, v in _L2_gnn_all.items() if k in ('factors', 'Wm', 'bm', 'Wc', 'bc')}
    del _L2_gnn_all

    def _L3_gnn_setup():
        import jax, jax.numpy as jnp
        import numpy as np
        N = 3125
        E = 50000
        D_IN = 128
        D_OUT = 128
        LN_EPS = 1e-05
        key = jax.random.key(seed)
        ks = jax.random.split(key, 5)
        features = jax.random.normal(ks[0], (N, D_IN), dtype=jnp.float32)
        adj_indices = jax.random.randint(ks[1], (2, E), 0, N, dtype=jnp.int64)
        adj_values = jax.random.uniform(ks[2], (E,), dtype=jnp.float32)
        weight = jax.random.normal(ks[3], (D_IN, D_OUT), dtype=jnp.float32) * (1.0 / np.sqrt(D_IN))
        bias = jax.random.normal(ks[4], (1, D_OUT), dtype=jnp.float32) * 0.1
        ln_gamma = jnp.ones((D_OUT,), dtype=jnp.float32)
        ln_beta = jnp.zeros((D_OUT,), dtype=jnp.float32)
        return {'features': features, 'adj_indices': adj_indices, 'adj_values': adj_values, 'weight': weight, 'bias': bias, 'ln_gamma': ln_gamma, 'ln_beta': ln_beta}
    _L3_gnn_all = _L3_gnn_setup()
    _L3_gnn_in = {k: v for k, v in _L3_gnn_all.items() if k in ('weight', 'bias', 'ln_gamma', 'ln_beta')}
    del _L3_gnn_all
    return {'x': x, 'src': src, 'dst': dst, 'edge_attr_128': edge_attr_128, 'edge_weight': edge_weight, 'L0_gnn_lin_w': _L0_gnn_in['lin_w'], 'L0_gnn_att_src': _L0_gnn_in['att_src'], 'L0_gnn_att_dst': _L0_gnn_in['att_dst'], 'L0_gnn_gat_bias': _L0_gnn_in['gat_bias'], 'L0_gnn_proj_w': _L0_gnn_in['proj_w'], 'L0_gnn_proj_b': _L0_gnn_in['proj_b'], 'L0_gnn_ln_gamma': _L0_gnn_in['ln_gamma'], 'L0_gnn_ln_beta': _L0_gnn_in['ln_beta'], 'L1_gnn_globals_g': _L1_gnn_in['globals_g'], 'L1_gnn_W_e_k': _L1_gnn_in['W_e_k'], 'L1_gnn_W_e_b': _L1_gnn_in['W_e_b'], 'L1_gnn_eps': _L1_gnn_in['eps'], 'L1_gnn_W1': _L1_gnn_in['W1'], 'L1_gnn_b1': _L1_gnn_in['b1'], 'L1_gnn_W2': _L1_gnn_in['W2'], 'L1_gnn_b2': _L1_gnn_in['b2'], 'L2_gnn_factors': _L2_gnn_in['factors'], 'L2_gnn_Wm': _L2_gnn_in['Wm'], 'L2_gnn_bm': _L2_gnn_in['bm'], 'L2_gnn_Wc': _L2_gnn_in['Wc'], 'L2_gnn_bc': _L2_gnn_in['bc'], 'L3_gnn_weight': _L3_gnn_in['weight'], 'L3_gnn_bias': _L3_gnn_in['bias'], 'L3_gnn_ln_gamma': _L3_gnn_in['ln_gamma'], 'L3_gnn_ln_beta': _L3_gnn_in['ln_beta']}

def reference(x, src, dst, edge_attr_128, edge_weight, L0_gnn_lin_w, L0_gnn_att_src, L0_gnn_att_dst, L0_gnn_gat_bias, L0_gnn_proj_w, L0_gnn_proj_b, L0_gnn_ln_gamma, L0_gnn_ln_beta, L1_gnn_globals_g, L1_gnn_W_e_k, L1_gnn_W_e_b, L1_gnn_eps, L1_gnn_W1, L1_gnn_b1, L1_gnn_W2, L1_gnn_b2, L2_gnn_factors, L2_gnn_Wm, L2_gnn_bm, L2_gnn_Wc, L2_gnn_bc, L3_gnn_weight, L3_gnn_bias, L3_gnn_ln_gamma, L3_gnn_ln_beta):
    import jax
    import jax.numpy as jnp

    def _L0_gnn_ref(x, edge_index, lin_w, att_src, att_dst, gat_bias, proj_w, proj_b, ln_gamma, ln_beta):
        import jax, jax.numpy as jnp
        import numpy as np
        N = 50000
        E = 18750
        IN_CH = 128
        HEADS = 8
        HEAD_DIM = 16
        OUT_CH = 128
        NEG_SLOPE = 0.2
        LN_EPS = 1e-05
        n = x.shape[0]
        h = (x @ lin_w.T).reshape(n, HEADS, HEAD_DIM)
        a_src = (h * att_src).sum(-1)
        a_dst = (h * att_dst).sum(-1)
        loops = jnp.arange(n, dtype=edge_index.dtype)
        src = jnp.concatenate([edge_index[0], loops])
        dst = jnp.concatenate([edge_index[1], loops])
        logits = jax.nn.leaky_relu(a_src[src] + a_dst[dst], NEG_SLOPE)
        seg_max = jax.ops.segment_max(logits, dst, num_segments=n)
        e = jnp.exp(logits - seg_max[dst])
        denom = jax.ops.segment_sum(e, dst, num_segments=n)
        alpha = e / denom[dst]
        agg = jax.ops.segment_sum(h[src] * alpha[:, :, None], dst, num_segments=n)
        gat_out = agg.reshape(n, HEADS * HEAD_DIM) + gat_bias
        out = gat_out @ proj_w.T + proj_b
        mu = out.mean(-1, keepdims=True)
        var = ((out - mu) ** 2).mean(-1, keepdims=True)
        out = (out - mu) * jax.lax.rsqrt(var + LN_EPS) * ln_gamma + ln_beta
        return out

    def _L1_gnn_ref(nodes, edges, globals_g, W_e_k, W_e_b, eps, W1, b1, W2, b2, senders, receivers):
        import jax, jax.numpy as jnp
        import numpy as np
        N, E, D, G, H, O = (10000, 20000, 128, 128, 512, 128)

        def mish(x):
            return x * jnp.tanh(jax.nn.softplus(x))
        n = nodes.shape[0]
        sent = nodes[senders]
        e = mish(sent + edges @ W_e_k + W_e_b)
        agg = jax.ops.segment_sum(e, receivers, num_segments=n)
        h = (1.0 + eps) * nodes + agg
        g = jnp.broadcast_to(globals_g, (n, globals_g.shape[-1]))
        h = jnp.concatenate([h, g], axis=-1)
        h = jax.nn.relu(h @ W1 + b1) @ W2 + b2
        return h

    def _L2_gnn_ref(variables, factors, senders, receivers, Wm, bm, Wc, bc):
        import jax, jax.numpy as jnp
        import numpy as np
        N_VAR, N_FAC, N_EDGE, D = (3125, 50000, 31250, 128)
        x_i = variables[senders]
        x_j = factors[receivers]
        x = jnp.concatenate([x_i, x_j], axis=-1)
        msg = jax.nn.relu(x @ Wm + bm)
        agg = jax.ops.segment_sum(msg, senders, num_segments=variables.shape[0])
        h = jnp.concatenate([variables, agg], axis=-1)
        h = jax.nn.relu(h @ Wc + bc)
        return variables + h

    def _L3_gnn_ref(features, adj_indices, adj_values, weight, bias, ln_gamma, ln_beta):
        import jax, jax.numpy as jnp
        import numpy as np
        N = 3125
        E = 50000
        D_IN = 128
        D_OUT = 128
        LN_EPS = 1e-05
        h = features @ weight
        row, col = (adj_indices[0], adj_indices[1])
        msg = adj_values[:, None] * h[col]
        agg = jax.ops.segment_sum(msg, row, num_segments=features.shape[0])
        x = jax.nn.elu(agg + bias)
        mu = jnp.mean(x, axis=-1, keepdims=True)
        var = jnp.mean(jnp.square(x - mu), axis=-1, keepdims=True)
        return (x - mu) * jax.lax.rsqrt(var + LN_EPS) * ln_gamma + ln_beta
    edge_index = jnp.stack([src, dst])
    h = jnp.maximum(_layernorm(x, axis=-1), 0.0)
    x = x + _L0_gnn_ref(h, edge_index, L0_gnn_lin_w, L0_gnn_att_src, L0_gnn_att_dst, L0_gnn_gat_bias, L0_gnn_proj_w, L0_gnn_proj_b, L0_gnn_ln_gamma, L0_gnn_ln_beta)
    h = jnp.maximum(_layernorm(x, axis=-1), 0.0)
    x = x + _L1_gnn_ref(h, edge_attr_128, L1_gnn_globals_g, L1_gnn_W_e_k, L1_gnn_W_e_b, L1_gnn_eps, L1_gnn_W1, L1_gnn_b1, L1_gnn_W2, L1_gnn_b2, src, dst)
    h = jnp.maximum(_layernorm(x, axis=-1), 0.0)
    x = x + _L2_gnn_ref(h, L2_gnn_factors, src, dst, L2_gnn_Wm, L2_gnn_bm, L2_gnn_Wc, L2_gnn_bc)
    h = jnp.maximum(_layernorm(x, axis=-1), 0.0)
    x = x + _L3_gnn_ref(h, edge_index, edge_weight, L3_gnn_weight, L3_gnn_bias, L3_gnn_ln_gamma, L3_gnn_ln_beta)
    return x

_drawn_inputs = setup_inputs


def setup_inputs(seed=0):
    import zlib

    import numpy as np

    out = dict(_drawn_inputs(seed))
    spreads = {'L0_gnn_gat_bias': (0.0, 0.1),
     'L0_gnn_proj_b': (0.0, 0.1),
     'L0_gnn_ln_gamma': (1.0, 0.2),
     'L0_gnn_ln_beta': (0.0, 0.1),
     'L1_gnn_W_e_b': (0.0, 0.384),
     'L1_gnn_b1': (0.0, 0.1),
     'L1_gnn_b2': (0.0, 0.1),
     'L2_gnn_bm': (0.0, 0.8),
     'L2_gnn_bc': (0.0, 0.321),
     'L3_gnn_ln_gamma': (1.0, 0.2),
     'L3_gnn_ln_beta': (0.0, 0.1)}
    factors = {'L0_gnn_att_src': 3.886, 'L0_gnn_att_dst': 8.0}
    for name, (base, spread) in spreads.items():
        noise = np.random.default_rng([zlib.crc32(name.encode()), seed]).standard_normal(out[name].shape)
        drawn = base * np.exp(spread * noise) if base else spread * noise
        out[name] = jnp.asarray(drawn.astype(out[name].dtype))
    for name, factor in factors.items():
        out[name] = (out[name] * factor).astype(out[name].dtype)
    return out
```

```python
import concourse.bass as bass
from concourse import mybir
from contextlib import ExitStack

F32, I32, BF16 = mybir.dt.float32, mybir.dt.int32, mybir.dt.bfloat16
ALU = mybir.AluOpType
ACT = mybir.ActivationFunctionType

P = 128
D = 128
N, E = 50000, 25000
HEADS, HD = 8, 16
HID = 512
SLOTS = 4
BLK = P * SLOTS
NBLK = 98
NPAD = NBLK * BLK
TILES = 196
EPAD = TILES * P
GROUPS = TILES // SLOTS
SROWS = EPAD + 16
PAD_ROWS = SROWS - EPAD
AW = D + 2 * HEADS
XW = D + 2
LO = 256
LN_EPS = 1e-5
SKIP = 1.0e6
LOWEST = -3.0e38


class Tally:

    def __init__(self, eng, sem, per):
        self.eng, self.sem, self.per = eng, sem, per

    def begin(self, turn):
        self.base, self.n = turn * self.per, 0

    def inc(self, instruction):
        self.n += 1
        instruction.then_inc(self.sem, 1)

    def wait(self):
        self.eng.wait_ge(self.sem, self.base + self.n)

    def end(self):
        assert self.n == self.per, f"per must be {self.n}"


def tables(nc):
    def dram(name, rows, cols):
        return nc.dram_tensor(name, (rows, cols), F32).ap()
    return {
        "att": dram("t_att", NPAD, AW), "gat": dram("t_gat", NPAD, D),
        "x1": dram("t_x1", NPAD, XW), "x2": dram("t_x2", NPAD, XW), "x3": dram("t_x3", NPAD, XW),
        "sum_dst": dram("t_sum_dst", NPAD, D), "sum_src": dram("t_sum_src", NPAD, D),
        "by_dst": dram("t_by_dst", SROWS, 4), "by_src": dram("t_by_src", SROWS, 4),
    }


def blocks4(table, row):
    return table[bass.ds(row, BLK), :].rearrange("(p j) d -> p j d", p=P)


def new_block(nc, ctx, sems):
    def zero():
        with nc.Block() as after:
            @after.gpsimd
            def _(pool):
                pool.dma_reset()
                for s in sems:
                    pool.sem_clear(s)
    ctx.callback(zero)
    return ctx.enter_context(nc.Block())


def prepare(nc, a, w):
    with ExitStack() as c:
        loaded, folded, vec, step = (c.enter_context(nc.semaphore(n)) for n in
                                     ("w_loaded", "w_folded", "w_vec", "w_step"))
        ps = c.enter_context(nc.psum_tensor("w_ps", [P, 4, 512], F32))
        att = c.enter_context(nc.sbuf_tensor("w_att", [P, 2], F32))
        attm = c.enter_context(nc.sbuf_tensor("w_attm", [P, 2 * HEADS], F32))
        linw = c.enter_context(nc.sbuf_tensor("w_linw", [P, D], F32))
        gatb = c.enter_context(nc.sbuf_tensor("w_gatb", [P, D], F32))
        projb = c.enter_context(nc.sbuf_tensor("w_projb", [P, D], F32))
        w1b = c.enter_context(nc.sbuf_tensor("w_w1b", [P, HID], F32))
        glob = c.enter_context(nc.sbuf_tensor("w_glob", [P, 1], F32))
        b1 = c.enter_context(nc.sbuf_tensor("w_b1", [P, 4], F32))
        block = new_block(nc, c, [loaded, folded, vec, step])
        loads = [(w["ident"][:, :], a["ident"]), (w["hmask"][:, :], a["hmask"]), (w["expand"][:, :], a["expand"]),
                 (w["wl"][:, 0:D], a["linwT"]), (w["proj"][:, :], a["projT"]), (linw[:, :], a["linw"]),
                 (att[:, :], a["att"]), (gatb[:, :], a["gatb"]), (projb[:, :], a["projb"]),
                 (w["g0"][:, :], a["g0"]), (w["be0"][:, :], a["be0"]), (w["we"][:, :], a["we"]), (w["bee"][:, :], a["bee"]),
                 (w["eps1"][:, :], a["eps1"]), (w["w1"][:, :], a["w1"][0:D, :]), (w1b[:, :], a["w1"][D:2 * D, :]),
                 (glob[:, :], a["glob"]), (b1[:, :], a["b1"]),
                 (w["w2"][:, :, :], a["w2"].rearrange("(c p) o -> p c o", p=P)), (w["b2"][:, :], a["b2"]),
                 (w["wm"][:, :, :], a["wm"].rearrange("(c p) o -> p c o", p=P)), (w["bm"][:, :], a["bm"]),
                 (w["wc"][:, :, :], a["wc"].rearrange("(c p) o -> p c o", p=P)), (w["bc"][:, :], a["bc"]),
                 (w["w3"][:, :], a["w3"]), (w["b3"][:, :], a["b3"]), (w["g3"][:, :], a["g3"]), (w["be3"][:, :], a["be3"])]

        @block.sync
        def _(sp):
            for dst, src in loads:
                sp.dma_start(dst, src).then_inc(loaded, 16)

        @block.vector
        def _(dve):
            nc.vector.memset(w["eps"][:, :], LN_EPS)
            dve.wait_ge(loaded, 16 * len(loads))
            for k in range(2):
                nc.vector.tensor_scalar(attm[:, k * HEADS:(k + 1) * HEADS], w["hmask"][:, :], att[:, k:k + 1], None,
                                        ALU.mult).then_inc(vec, 1)
            nc.vector.tensor_scalar(w["eps1"][:, :], w["eps1"][:, :], 1.0, None, ALU.add).then_inc(step, 1)
            dve.wait_ge(folded, 1)
            nc.vector.tensor_copy(w["wl"][:, D:AW], ps[:, 0, 0:2 * HEADS])
            nc.vector.tensor_tensor(w["c0"][:, :], ps[:, 1, 0:D], projb[:, :], ALU.add)
            nc.vector.tensor_tensor(w["b1"][:, :], ps[:, 2, 0:4], b1[:, :], ALU.add).then_inc(step, 1)
            dve.wait_ge(step, 2)

        @block.tensor
        def _(pe):
            pe.wait_ge(loaded, 16 * len(loads))
            pe.wait_ge(vec, 2)
            nc.tensor.matmul(ps[:, 0, 0:2 * HEADS], linw[:, :], attm[:, :], start=True, stop=True)
            nc.tensor.matmul(ps[:, 1, 0:D], gatb[:, :], w["proj"][:, :], start=True, stop=True)
            for k in range(4):
                last = nc.tensor.matmul(ps[:, 2, k:k + 1], w1b[:, k * D:(k + 1) * D], glob[:, :], start=True, stop=True)
            last.then_inc(folded, 1)


def sort_edges(nc, a, w, t, which):
    col, row = a[which + "_col"], a[which + "_row"]
    out = t["by_dst" if which == "dst" else "by_src"]
    STEPS = TILES // SLOTS
    with ExitStack() as c:
        def sb(name, shape, dt=F32):
            return c.enter_context(nc.sbuf_tensor(f"s{which}_{name}", shape, dt))

        sems = []

        def sem(name):
            sems.append(c.enter_context(nc.semaphore(f"s{which}_{name}")))
            return sems[-1]
        srcc, dstc, keyi = sb("srcc", [P, TILES], I32), sb("dstc", [P, TILES], I32), sb("keyi", [P, 2, TILES], I32)
        rec = sb("rec", [P, TILES, 4])
        hif, lof, keyf = sb("hif", [P, TILES]), sb("lof", [P, TILES]), sb("keyf", [P, TILES])
        iota, iotap, tri, zero = sb("iota", [P, LO]), sb("iotap", [P, 2]), sb("tri", [P, 3, P]), sb("zero", [P, 512], BF16)
        oh_hi, oh_lo = sb("oh_hi", [P, SLOTS, LO], BF16), sb("oh_lo", [P, SLOTS, LO], BF16)
        krow, hrow, oh_t = sb("krow", [P, BLK], I32), sb("hrow", [P, BLK], I32), sb("oh_t", [P, 2, BLK])
        incl, start = sb("incl", [P, 2, LO]), sb("start", [P, 2, LO])
        count = sb("count", [P, 2, 2, LO])
        rowsum, scr = sb("rowsum", [P, 2]), sb("scr", [P, 2, SLOTS, LO], BF16)
        occ, prev, pos, posi = sb("occ", [P, SLOTS]), sb("prev", [P, TILES]), sb("pos", [P, TILES]), sb("posi", [P, TILES], I32)
        occ_all = sb("occ_all", [P, TILES])
        pos4 = sb("pos4", [P, 2, SLOTS], I32)
        rec4 = sb("rec4", [P, 2, SLOTS, 4])
        cnt_ps = c.enter_context(nc.psum_tensor(f"s{which}_cnt", [P, 2, LO], F32))
        look_ps = c.enter_context(nc.psum_tensor(f"s{which}_look", [P, 2, 512], F32))
        base_ps = c.enter_context(nc.psum_tensor(f"s{which}_base", [P, 512], F32))
        loaded, vec, hots, counted, seeded, base_ok = (sem(n) for n in ("loaded", "vec", "hots", "counted", "seeded", "base"))
        rows_in, rows_free, hot_t, updated, copied, looked, picked = (sem(n) for n in
            ("rows_in", "rows_free", "hot_t", "updated", "copied", "looked", "picked"))
        p4_ready, gate, posrdy = (sem(n) for n in ("p4_ready", "gate", "posrdy"))
        sent = w["dma"][0:2]
        sems += sent
        block = new_block(nc, c, sems)

        @block.sync
        def _(sp):
            for dst, src in ((srcc[:, :], a["src_col"]), (dstc[:, :], a["dst_col"]), (rec[:, :, 2:4], a["rec_col"]),
                             (iota[:, :], a["iota"]), (iotap[:, :], a["iotap"]), (tri[:, :, :], a["tri"])):
                sp.dma_start(dst, src).then_inc(loaded, 16)
            sp.dma_start(out[EPAD:SROWS, :], a["sentinel"]).then_inc(loaded, 16)
            sp.sem_inc(rows_free, 1)
            with sp.Fori(0, STEPS) as i:
                sp.wait_ge(rows_free, i + 1)
                sp.dma_start(krow[:, :], row[:, bass.ds(i * BLK, BLK)].to_broadcast([P, BLK])).then_inc(rows_in, 16)
            sp.wait_ge(loaded, 16 * 7)

        @block.gpsimd
        def _(pool):
            limit = pool.to_reg(SROWS - 1)

            def scatter(g, u):
                pool.wait_ge(p4_ready, g + 1)
                pool.sem_inc(gate, 1)
                for j in range(SLOTS):
                    nc.gpsimd.indirect_dma_start(out, bass.IndirectOffsetOnAxis(ap=pos4[:, u, j:j + 1], axis=0),
                                                 rec4[:, u, j, :], None, bounds_check=limit,
                                                 oob_is_err=False).then_inc(sent[u], 16)
            with pool.Fori(0, STEPS // 2) as i:
                for u in range(2):
                    scatter(2 * i + u, u)
            scatter(STEPS - 1, 0)
            pool.wait_ge(sent[0], 16 * SLOTS * (STEPS - STEPS // 2))
            pool.wait_ge(sent[1], 16 * SLOTS * (STEPS // 2))

        @block.vector
        def _(dve):
            own = dve
            nc.vector.memset(zero[:, :], 0.0).then_inc(vec, 1)
            dve.wait_ge(loaded, 16 * 7)
            keys = dstc if which == "dst" else srcc
            nc.vector.tensor_copy(rec[:, :, 0], srcc[:, :])
            nc.vector.tensor_copy(rec[:, :, 1], dstc[:, :])
            nc.vector.tensor_copy(keyf[:, :], keys[:, :])
            nc.vector.tensor_scalar(keyi[:, 0, :], keys[:, :], 8, None, ALU.logical_shift_right)
            nc.vector.tensor_scalar(keyi[:, 1, :], keys[:, :], LO - 1, None, ALU.bitwise_and).then_inc(vec, 1)
            own.wait_ge(vec, 2)
            nc.vector.tensor_copy(hif[:, :], keyi[:, 0, :])
            nc.vector.tensor_copy(lof[:, :], keyi[:, 1, :]).then_inc(vec, 1)
            own.wait_ge(vec, 3)

            def one_hots(i, j):
                nc.vector.tensor_scalar(oh_hi[:, j, :], iota[:, :], hif[:, bass.ds(i * SLOTS + j, 1)], None, ALU.is_equal)
                return nc.vector.tensor_scalar(oh_lo[:, j, :], iota[:, :], lof[:, bass.ds(i * SLOTS + j, 1)], None,
                                               ALU.is_equal)
            with dve.Fori(0, STEPS) as i:
                for j in range(SLOTS):
                    dve.wait_ge(counted, i * SLOTS + j + 1)
                    one_hots(i, j).then_inc(hots, 1)
            dve.wait_ge(counted, SLOTS + TILES)
            for k in range(2):
                nc.vector.tensor_tensor_scan(incl[:, k, :], zero[:, 0:LO], cnt_ps[:, k, :], 0.0, ALU.add, ALU.add)
            nc.vector.tensor_reduce(rowsum[:, :], cnt_ps[:, :, :], mybir.AxisListType.X, ALU.add).then_inc(vec, 1)
            own.wait_ge(vec, 4)
            nc.vector.tensor_tensor(start[:, :, :], incl[:, :, :], cnt_ps[:, :, :], ALU.subtract).then_inc(vec, 1)
            dve.wait_ge(base_ok, 1)
            own.wait_ge(vec, 5)
            for k in range(2):
                last = nc.vector.tensor_scalar(start[:, k, :], start[:, k, :], base_ps[:, k:k + 1], None, ALU.add)
            last.then_inc(vec, 1)
            own.wait_ge(vec, 6)
            with dve.Fori(0, STEPS) as i:
                dve.wait_ge(rows_in, i * 16 + 16)
                nc.vector.tensor_scalar(hrow[:, :], krow[:, :], 8, None, ALU.logical_shift_right).then_inc(vec, 1)
                dve.wait_ge(vec, 6 + i + 1)
                dve.wait_ge(picked, i * SLOTS + 2)
                dve.wait_ge(looked, i * SLOTS + SLOTS)
                for k in range(2):
                    last = nc.vector.tensor_scalar(oh_t[:, k, :], hrow[:, :], iotap[:, k:k + 1], None, ALU.is_equal)
                last.then_inc(hot_t, 1)
                for j in range(SLOTS):
                    dve.wait_ge(updated, i * SLOTS + j + 1)
                    one_hots(i, j).then_inc(hots, 1)
                    last = nc.vector.scalar_tensor_tensor(scr[:, 0, j, 0:P], krow[:, j * P:(j + 1) * P], keyf[:, bass.ds(i * SLOTS + j, 1)],
                                                   tri[:, 0, :], ALU.is_equal, ALU.mult,
                                                   accum_out=occ_all[:, bass.ds(i * SLOTS + j, 1)])
                    if j == SLOTS - 1:
                        last.then_inc(rows_free, 1)
                for j in range(SLOTS):
                    dve.wait_ge(looked, i * SLOTS + SLOTS + j + 1)
                    last = nc.vector.scalar_tensor_tensor(scr[:, 1, j, :], iota[:, :], lof[:, bass.ds(i * SLOTS + j, 1)],
                                                          look_ps[:, j % 2, 0:LO], ALU.is_equal, ALU.mult,
                                                          accum_out=prev[:, bass.ds(i * SLOTS + j, 1)])
                    last.then_inc(picked, 1)
            own.wait_ge(picked, TILES + 2)
            nc.vector.tensor_tensor(pos[:, :], occ_all[:, :], prev[:, :], ALU.add).then_inc(posrdy, 1)
            own.wait_ge(posrdy, 1)
            nc.vector.tensor_copy(posi[:, :], pos[:, :]).then_inc(posrdy, 1)
            own.wait_ge(posrdy, 2)
            def hand(g, u):
                nc.vector.tensor_copy(pos4[:, u, :], posi[:, bass.ds(g * SLOTS, SLOTS)])
                nc.vector.tensor_copy(rec4[:, u, :, :], rec[:, bass.ds(g * SLOTS, SLOTS), :]).then_inc(p4_ready, 1)
            hand(0, 0)
            hand(1, 1)
            with dve.Fori(0, STEPS // 2 - 1) as i:
                for u in range(2):
                    dve.wait_ge(sent[u], (i + 1) * 16 * SLOTS)
                    hand(2 * i + 2 + u, u)
            dve.wait_ge(sent[0], (STEPS // 2) * 16 * SLOTS)
            hand(STEPS - 1, 0)

        @block.scalar
        def _(act):
            with act.Fori(0, TILES, 2) as i:
                for u in range(2):
                    act.wait_ge(updated, SLOTS + i + u)
                    act.wait_ge(seeded, 1)
                    act.wait_ge(looked, SLOTS + i + u - 1)
                    nc.scalar.activation(count[:, u, :, :], cnt_ps[:, :, :], ACT.Copy).then_inc(copied, 1)

        @block.tensor
        def _(pe):
            pe.sem_inc(counted, SLOTS)
            pe.sem_inc(updated, SLOTS)
            pe.sem_inc(looked, SLOTS)
            pe.sem_inc(picked, 2)
            pe.wait_ge(vec, 1)
            nc.tensor.matmul(cnt_ps[:, :, :], zero[:, 0:P], zero[:, :], start=True, stop=True)

            def count_tile(j):
                for k in range(2):
                    last = nc.tensor.matmul(cnt_ps[:, k, :], oh_hi[:, j, k * P:(k + 1) * P], oh_lo[:, j, :],
                                            start=False, stop=True, skip_group_check=True)
                return last
            with pe.Fori(0, STEPS) as i:
                for j in range(SLOTS):
                    pe.wait_ge(hots, i * SLOTS + j + 1)
                    count_tile(j).then_inc(counted, 1)
            pe.wait_ge(vec, 4)
            nc.tensor.matmul(base_ps[:, 0:2], tri[:, 1, :], rowsum[:, :], start=True, stop=True)
            nc.tensor.matmul(base_ps[:, 1:2], tri[:, 2, :], rowsum[:, 0:1], start=False, stop=True,
                             skip_group_check=True).then_inc(base_ok, 1)
            pe.wait_ge(vec, 6)
            nc.tensor.matmul(cnt_ps[:, :, :], w["ident"][:, :], start[:, :, :], start=True, stop=True).then_inc(seeded, 1)
            with pe.Fori(0, STEPS) as i:
                pe.wait_ge(hot_t, i + 1)
                for j in range(SLOTS):
                    pe.wait_ge(copied, i * SLOTS + j + 1)
                    pe.wait_ge(picked, i * SLOTS + j + 1)
                    for k in range(2):
                        last = nc.tensor.matmul(look_ps[:, j % 2, 0:LO], oh_t[:, k, j * P:(j + 1) * P],
                                                count[:, j % 2, k, :], start=(k == 0), stop=(k == 1))
                    last.then_inc(looked, 1)
                    pe.wait_ge(hots, TILES + i * SLOTS + j + 1)
                    count_tile(j).then_inc(updated, 1)

AHEAD = 4


def done(eng, sem, g, before=0):
    eng.wait_ge(sem, g + (AHEAD + 1 - before))


def reused(eng, sem, value):
    if not (isinstance(value, int) and value == 0):
        eng.wait_ge(sem, value)


def pipelined(eng, stages, count, unroll):
    longest = max(lag for _, lag in stages)
    head = longest + unroll
    turns = (count - head) // unroll

    def step(tau, i):
        for stage, lag in stages:
            at = tau - lag
            if i is None:
                if 0 <= at < count:
                    stage(at, at // unroll, at % unroll)
            else:
                stage(i * unroll + at, i + at // unroll, at % unroll)
    for tau in range(head):
        step(tau, None)
    with eng.Fori(0, turns) as i:
        for u in range(unroll):
            step(head + u, i)
    for tau in range(head + turns * unroll, count + longest):
        step(tau, None)


class Phase:

    def __init__(self, nc, ctx, name):
        self.nc, self.ctx, self.name, self.steps, self.all = nc, ctx, name, [], []
        self.gate = self.sem("gate")

    def sb(self, name, shape, dt=F32):
        return self.ctx.enter_context(self.nc.sbuf_tensor(f"{self.name}_{name}", shape, dt))

    def ps(self, name, shape):
        return self.ctx.enter_context(self.nc.psum_tensor(f"{self.name}_{name}", shape, F32))

    def sem(self, name):
        self.all.append(self.ctx.enter_context(self.nc.semaphore(f"{self.name}_{name}")))
        return self.all[-1]

    def dma(self, w, n):
        first = sum(s in w["dma"] for s in self.all)
        self.all += w["dma"][first:first + n]
        return w["dma"][first:first + n]

    def sems(self, name, n):
        return [self.sem(f"{name}{k}") for k in range(n)]

    def step(self, *names):
        made = [self.sem(n) for n in names]
        self.steps += made
        return made

    def apart(self, eng):
        eng.sem_inc(self.gate, 1)

    def start(self, eng):
        for s in self.steps:
            eng.sem_inc(s, AHEAD)


def transposes4(nc, out, src, ident):
    for j in range(SLOTS):
        last = nc.tensor.transpose(out[:, j * P:(j + 1) * P], src[:, j, 0:D], ident[:, :])
    return last


def stats4(ph, tally, src, st, mv):
    nc = ph.nc
    for j in range(SLOTS):
        last = nc.vector.bn_stats(st[:, j, :], src[:, j, 0:D])
    tally.inc(last)
    tally.wait()
    ph.apart(tally.eng)
    for j in range(SLOTS):
        last = nc.vector.bn_aggr(mv[:, j, :], st[:, j, :])
    return last


def normalise4(nc, out, src, scale, shift, func):
    for j in range(SLOTS):
        last = nc.scalar.activation(out[:, j, 0:D], src[:, j, 0:D], func, bias=shift(j), scale=scale(j))
    return last


def attention_inputs(nc, a, w, t):
    with ExitStack() as c:
        ph = Phase(nc, c, "A")
        x, st, mv, sd = ph.sb("x", [P, 4, SLOTS, D]), ph.sb("st", [P, 2, SLOTS, 6]), ph.sb("mv", [P, 2, SLOTS, 2]), ph.sb("sd", [P, 2, SLOTS])
        rs, nm = ph.sb("rs", [P, 2, SLOTS]), ph.sb("nm", [P, 2, SLOTS])
        h, hT, o = ph.sb("h", [P, 2, SLOTS, D]), ph.sb("hT", [P, 2, BLK]), ph.sb("o", [P, 4, SLOTS, AW])
        psT, psO = ph.ps("psT", [P, 2, BLK]), ph.ps("psO", [P, 2, SLOTS, LO])
        loaded, stored = ph.sems("loaded", 4), ph.dma(w, 4)
        s_stat, s_sd, s_rs, s_h, s_tr, s_hT, s_mm, s_o = ph.step("stat", "sd", "rs", "h", "tr", "hT", "mm", "o")
        ch1, ch2 = ph.sems("ch", 2)
        block = new_block(nc, c, ph.all)

        @block.sync
        def _(sp):
            ph.start(sp)

            def load(g, q, m):
                done(sp, s_h, g, 4)
                sp.dma_start(x[:, m], blocks4(a["x"], g * BLK)).then_inc(loaded[m], 16)
            pipelined(sp, [(load, 0)], NBLK, 4)

        @block.gpsimd
        def _(pool):
            def store(g, q, m):
                b = m % 2
                done(pool, s_o, g)
                pool.dma_start(blocks4(t["att"], g * BLK), o[:, m]).then_inc(stored[m], 16)
                pool.dma_start(blocks4(t["gat"], g * BLK), o[:, m, :, 0:D]).then_inc(stored[m], 16)
            pipelined(pool, [(store, 3)], NBLK, 4)
            for m in range(4):
                pool.wait_ge(stored[m], 32 * ((NBLK + 3 - m) // 4))

        @block.vector
        def _(dve):
            c1, c2 = Tally(dve, ch1, 1), Tally(dve, ch2, 1)

            def stats(g, q, m):
                b = m % 2
                dve.wait_ge(loaded[m], q * 16 + 16)
                done(dve, s_rs, g, 2)
                done(dve, s_sd, g, 2)
                c1.begin(g)
                stats4(ph, c1, x[:, m], st[:, b], mv[:, b]).then_inc(s_stat, 1)
                c1.end()

            def scale(g, q, m):
                b = m % 2
                done(dve, s_sd, g)
                done(dve, s_h, g, 2)
                c2.begin(g)
                c2.inc(nc.vector.reciprocal(rs[:, b, :], sd[:, b, :]))
                c2.wait()
                nc.vector.scalar_tensor_tensor(nm[:, b, :], mv[:, b, :, 0], -1.0, rs[:, b, :], ALU.mult, ALU.mult).then_inc(s_rs, 1)
                c2.end()

            def evacuate(g, q, m):
                b = m % 2
                done(dve, s_mm, g)
                reused(dve, stored[m], q * 32)
                nc.vector.tensor_copy(o[:, m], psO[:, b, :, 0:AW]).then_inc(s_o, 1)
            pipelined(dve, [(evacuate, 3), (scale, 1), (stats, 0)], NBLK, 4)

        @block.scalar
        def _(act):
            def deviation(g, q, m):
                b = m % 2
                done(act, s_stat, g)
                done(act, s_rs, g, 2)
                nc.scalar.activation(sd[:, b, :], mv[:, b, :, 1], ACT.Sqrt, bias=w["eps"][:, :]).then_inc(s_sd, 1)

            def relu(g, q, m):
                b = m % 2
                done(act, s_rs, g)
                done(act, s_tr, g, 2)
                normalise4(nc, h[:, b], x[:, m], lambda j: rs[:, b, j:j + 1], lambda j: nm[:, b, j:j + 1], ACT.Relu).then_inc(s_h, 1)

            def evacuate(g, q, m):
                b = m % 2
                done(act, s_tr, g)
                done(act, s_mm, g, 2)
                nc.scalar.activation(hT[:, b], psT[:, b], ACT.Copy).then_inc(s_hT, 1)
            pipelined(act, [(evacuate, 2), (relu, 1), (deviation, 0)], NBLK, 4)

        @block.tensor
        def _(pe):
            def turn(g, q, m):
                b = m % 2
                done(pe, s_h, g)
                done(pe, s_hT, g, 2)
                transposes4(nc, psT[:, b], h[:, b], w["ident"]).then_inc(s_tr, 1)

            def project(g, q, m):
                b = m % 2
                done(pe, s_hT, g)
                done(pe, s_o, g, 2)
                for j in range(SLOTS):
                    last = nc.tensor.matmul(psO[:, b, j, 0:AW], hT[:, b, j * P:(j + 1) * P], w["wl"][:, :], start=True, stop=True)
                last.then_inc(s_mm, 1)
            pipelined(pe, [(project, 2), (turn, 1)], NBLK, 4)


def attention_outputs(nc, a, w, t):
    with ExitStack() as c:
        ph = Phase(nc, c, "B")
        x, ga, xb = ph.sb("x", [P, 4, SLOTS, D]), ph.sb("ga", [P, 4, SLOTS, D]), ph.sb("xb", [P, 2, SLOTS, D])
        gT, o, y, xo = ph.sb("gT", [P, 2, BLK]), ph.sb("o", [P, 2, SLOTS, D]), ph.sb("y", [P, 2, SLOTS, D]), ph.sb("xo", [P, 4, SLOTS, XW])
        st, mv, sd = ph.sb("st", [P, 2, 2, SLOTS, 6]), ph.sb("mv", [P, 2, 2, SLOTS, 2]), ph.sb("sd", [P, 2, 2, SLOTS])
        rs, nm = ph.sb("rs", [P, 2, SLOTS]), ph.sb("nm", [P, 2, SLOTS])
        psT, psO = ph.ps("psT", [P, 2, BLK]), ph.ps("psO", [P, 2, BLK])
        loaded, stored = ph.sems("loaded", 4), ph.dma(w, 4)
        s_xb, s_tr, s_gT, s_mm, s_st1, s_sd1, s_rs1, s_y, s_st2, s_sd2, s_xo = ph.step(
            "xb", "tr", "gT", "mm", "st1", "sd1", "rs1", "y", "st2", "sd2", "xo")
        ch1, ch2, ch3, ch4 = ph.sems("ch", 4)
        block = new_block(nc, c, ph.all)

        @block.sync
        def _(sp):
            ph.start(sp)

            def load(g, q, m):
                done(sp, s_xb, g, 4)
                done(sp, s_tr, g, 4)
                sp.dma_start(ga[:, m], blocks4(t["gat"], g * BLK)).then_inc(loaded[m], 16)
                sp.dma_start(x[:, m], blocks4(a["x"], g * BLK)).then_inc(loaded[m], 16)
            pipelined(sp, [(load, 0)], NBLK, 4)

        @block.gpsimd
        def _(pool):
            def shift(g, q, m):
                b = m % 2
                pool.wait_ge(loaded[m], q * 32 + 32)
                done(pool, s_st2, g, 2)
                nc.gpsimd.tensor_tensor(xb[:, b], x[:, m], w["be0"][:, :].unsqueeze(1).to_broadcast([P, SLOTS, D]), ALU.add).then_inc(s_xb, 1)

            def store(g, q, m):
                b = m % 2
                done(pool, s_xo, g)
                pool.dma_start(blocks4(t["x1"], g * BLK), xo[:, m]).then_inc(stored[m], 16)
            pipelined(pool, [(store, 5), (shift, 3)], NBLK, 4)
            for m in range(4):
                pool.wait_ge(stored[m], 16 * ((NBLK + 3 - m) // 4))

        @block.vector
        def _(dve):
            c1, c2, c3, c4 = Tally(dve, ch1, 2), Tally(dve, ch2, 1), Tally(dve, ch3, 3), Tally(dve, ch4, 1)

            def first(g, q, m):
                b = m % 2
                done(dve, s_mm, g)
                done(dve, s_y, g, 2)
                done(dve, s_rs1, g, 2)
                c1.begin(g)
                c1.inc(nc.vector.tensor_tensor(o[:, b], psO[:, b].rearrange("p (j d) -> p j d", j=SLOTS),
                                        w["c0"][:, :].unsqueeze(1).to_broadcast([P, SLOTS, D]), ALU.add))
                c1.wait()
                stats4(ph, c1, o[:, b], st[:, 0, b], mv[:, 0, b]).then_inc(s_st1, 1)
                c1.end()

            def scale(g, q, m):
                b = m % 2
                done(dve, s_sd1, g)
                c2.begin(g)
                c2.inc(nc.vector.reciprocal(rs[:, b, :], sd[:, 0, b, :]))
                c2.wait()
                nc.vector.scalar_tensor_tensor(nm[:, b, :], mv[:, 0, b, :, 0], -1.0, rs[:, b, :], ALU.mult, ALU.mult).then_inc(s_rs1, 1)
                c2.end()

            def second(g, q, m):
                b = m % 2
                done(dve, s_y, g)
                done(dve, s_xb, g)
                reused(dve, stored[m], q * 16)
                c3.begin(g)
                c3.inc(nc.vector.tensor_tensor(y[:, b], y[:, b], w["g0"][:, :].unsqueeze(1).to_broadcast([P, SLOTS, D]), ALU.mult))
                c3.wait()
                c3.inc(nc.vector.tensor_tensor(xo[:, m, :, 0:D], y[:, b], xb[:, b], ALU.add))
                c3.wait()
                stats4(ph, c3, xo[:, m], st[:, 1, b], mv[:, 1, b]).then_inc(s_st2, 1)
                c3.end()

            def finish(g, q, m):
                b = m % 2
                done(dve, s_sd2, g)
                c4.begin(g)
                c4.inc(nc.vector.reciprocal(xo[:, m, :, D:D + 1], sd[:, 1, b, :].unsqueeze(2)))
                c4.wait()
                nc.vector.scalar_tensor_tensor(xo[:, m, :, D + 1:XW], mv[:, 1, b, :, 0:1], -1.0, xo[:, m, :, D:D + 1], ALU.mult, ALU.mult).then_inc(s_xo, 1)
                c4.end()
            pipelined(dve, [(finish, 5), (second, 4), (scale, 3), (first, 2)], NBLK, 4)

        @block.scalar
        def _(act):
            def evacuate(g, q, m):
                b = m % 2
                done(act, s_tr, g)
                done(act, s_mm, g, 2)
                nc.scalar.activation(gT[:, b], psT[:, b], ACT.Copy).then_inc(s_gT, 1)

            def deviation1(g, q, m):
                b = m % 2
                done(act, s_st1, g)
                nc.scalar.activation(sd[:, 0, b, :], mv[:, 0, b, :, 1], ACT.Sqrt, bias=w["eps"][:, :]).then_inc(s_sd1, 1)

            def normalise(g, q, m):
                b = m % 2
                done(act, s_rs1, g)
                done(act, s_st2, g, 2)
                normalise4(nc, y[:, b], o[:, b], lambda j: rs[:, b, j:j + 1], lambda j: nm[:, b, j:j + 1], ACT.Identity).then_inc(s_y, 1)

            def deviation2(g, q, m):
                b = m % 2
                done(act, s_st2, g)
                nc.scalar.activation(sd[:, 1, b, :], mv[:, 1, b, :, 1], ACT.Sqrt, bias=w["eps"][:, :]).then_inc(s_sd2, 1)
            pipelined(act, [(evacuate, 1), (deviation2, 4), (normalise, 3), (deviation1, 2)], NBLK, 4)

        @block.tensor
        def _(pe):
            def turn(g, q, m):
                b = m % 2
                pe.wait_ge(loaded[m], q * 32 + 32)
                done(pe, s_gT, g, 2)
                transposes4(nc, psT[:, b], ga[:, m], w["ident"]).then_inc(s_tr, 1)

            def project(g, q, m):
                b = m % 2
                done(pe, s_gT, g)
                done(pe, s_st1, g, 2)
                for j in range(SLOTS):
                    last = nc.tensor.matmul(psO[:, b, j * P:(j + 1) * P], gT[:, b, j * P:(j + 1) * P], w["proj"][:, :], start=True, stop=True)
                last.then_inc(s_mm, 1)
            pipelined(pe, [(turn, 0), (project, 1)], NBLK, 4)


def mlp(nc, a, w, t):
    with ExitStack() as c:
        ph = Phase(nc, c, "C")
        x, ag, xb = ph.sb("x", [P, 4, SLOTS, XW]), ph.sb("ag", [P, 4, SLOTS, D]), ph.sb("xb", [P, 2, SLOTS, D])
        h, hh, hT, r, xo = ph.sb("h", [P, 2, SLOTS, D]), ph.sb("hh", [P, 2, SLOTS, D]), ph.sb("hT", [P, 2, BLK]), ph.sb("r", [P, 2, 4, BLK]), ph.sb("xo", [P, 4, SLOTS, XW])
        st, mv, sd = ph.sb("st", [P, 2, SLOTS, 6]), ph.sb("mv", [P, 2, SLOTS, 2]), ph.sb("sd", [P, 2, SLOTS])
        psT, psH, psO = ph.ps("psT", [P, 2, BLK]), ph.ps("psH", [P, 4, BLK]), ph.ps("psO", [P, 2, BLK])
        loaded, stored = ph.sems("loaded", 4), ph.dma(w, 4)
        s_xb, s_h, s_hh, s_tr, s_hT, s_up, s_ra, s_rv, s_mm, s_st, s_sd, s_xo = ph.step(
            "xb", "h", "hh", "tr", "hT", "up", "ra", "rv", "mm", "st", "sd", "xo")
        up2 = ph.sem("up2")
        ch1, ch2 = ph.sems("ch", 2)
        block = new_block(nc, c, ph.all)

        @block.sync
        def _(sp):
            ph.start(sp)

            def load(g, q, m):
                done(sp, s_xb, g, 4)
                done(sp, s_h, g, 4)
                done(sp, s_hh, g, 4)
                sp.dma_start(x[:, m], blocks4(t["x1"], g * BLK)).then_inc(loaded[m], 16)
                sp.dma_start(ag[:, m], blocks4(t["sum_dst"], g * BLK)).then_inc(loaded[m], 16)
            pipelined(sp, [(load, 0)], NBLK, 4)

        @block.gpsimd
        def _(pool):
            def shift(g, q, m):
                b = m % 2
                pool.wait_ge(loaded[m], q * 32 + 32)
                done(pool, s_st, g, 2)
                nc.gpsimd.tensor_tensor(xb[:, b], x[:, m, :, 0:D], w["b2"][:, :].unsqueeze(1).to_broadcast([P, SLOTS, D]), ALU.add).then_inc(s_xb, 1)

            def store(g, q, m):
                b = m % 2
                done(pool, s_xo, g)
                pool.dma_start(blocks4(t["x2"], g * BLK), xo[:, m]).then_inc(stored[m], 16)
            pipelined(pool, [(store, 5), (shift, 3)], NBLK, 4)
            for m in range(4):
                pool.wait_ge(stored[m], 16 * ((NBLK + 3 - m) // 4))

        @block.vector
        def _(dve):
            c1, c2 = Tally(dve, ch1, 2), Tally(dve, ch2, 1)

            def combine(g, q, m):
                b = m % 2
                done(dve, s_h, g)
                done(dve, s_tr, g, 2)
                nc.vector.scalar_tensor_tensor(hh[:, b], h[:, b], w["eps1"][:, :], ag[:, m], ALU.mult, ALU.add).then_inc(s_hh, 1)

            def evacuate(g, q, m):
                b = m % 2
                done(dve, s_tr, g)
                done(dve, s_up, g, 2)
                nc.vector.tensor_copy(hT[:, b], psT[:, b]).then_inc(s_hT, 1)

            def relu(g, q, m):
                b = m % 2
                done(dve, s_up, g)
                done(dve, s_mm, g, 2)
                for k in (2, 3):
                    last = nc.vector.tensor_scalar(r[:, b, k], psH[:, k], w["b1"][:, k:k + 1], 0.0, ALU.add, ALU.max)
                last.then_inc(s_rv, 1)

            def add(g, q, m):
                b = m % 2
                done(dve, s_mm, g)
                done(dve, s_xb, g)
                done(dve, s_sd, g, 2)
                reused(dve, stored[m], q * 16)
                c1.begin(g)
                c1.inc(nc.vector.tensor_tensor(xo[:, m, :, 0:D], psO[:, b].rearrange("p (j d) -> p j d", j=SLOTS), xb[:, b], ALU.add))
                c1.wait()
                stats4(ph, c1, xo[:, m], st[:, b], mv[:, b]).then_inc(s_st, 1)
                c1.end()

            def finish(g, q, m):
                b = m % 2
                done(dve, s_sd, g)
                c2.begin(g)
                c2.inc(nc.vector.reciprocal(xo[:, m, :, D:D + 1], sd[:, b, :].unsqueeze(2)))
                c2.wait()
                nc.vector.scalar_tensor_tensor(xo[:, m, :, D + 1:XW], mv[:, b, :, 0:1], -1.0, xo[:, m, :, D:D + 1], ALU.mult, ALU.mult).then_inc(s_xo, 1)
                c2.end()
            pipelined(dve, [(evacuate, 2), (finish, 5), (add, 4), (combine, 1), (relu, 2)], NBLK, 4)

        @block.scalar
        def _(act):
            def node(g, q, m):
                b = m % 2
                act.wait_ge(loaded[m], q * 32 + 32)
                done(act, s_hh, g, 2)
                normalise4(nc, h[:, b], x[:, m], lambda j: x[:, m, j, D:D + 1], lambda j: x[:, m, j, D + 1:XW], ACT.Relu).then_inc(s_h, 1)

            def relu(g, q, m):
                b = m % 2
                act.wait_ge(up2, g + 1)
                done(act, s_mm, g, 2)
                for k in (0, 1):
                    last = nc.scalar.activation(r[:, b, k], psH[:, k], ACT.Relu, bias=w["b1"][:, k:k + 1])
                last.then_inc(s_ra, 1)

            def deviation(g, q, m):
                b = m % 2
                done(act, s_st, g)
                done(act, s_xo, g, 2)
                nc.scalar.activation(sd[:, b, :], mv[:, b, :, 1], ACT.Sqrt, bias=w["eps"][:, :]).then_inc(s_sd, 1)
            pipelined(act, [(node, 0), (deviation, 4), (relu, 2)], NBLK, 4)

        @block.tensor
        def _(pe):
            def turn(g, q, m):
                b = m % 2
                done(pe, s_hh, g)
                done(pe, s_hT, g, 2)
                transposes4(nc, psT[:, b], hh[:, b], w["ident"]).then_inc(s_tr, 1)

            def up(g, q, m):
                b = m % 2
                done(pe, s_hT, g)
                done(pe, s_ra, g, 1)
                for k in (0, 1):
                    last = nc.tensor.matmul(psH[:, k], w["w1"][:, k * P:(k + 1) * P], hT[:, b], start=True, stop=True)
                last.then_inc(up2, 1)
                done(pe, s_rv, g, 1)
                for k in (2, 3):
                    last = nc.tensor.matmul(psH[:, k], w["w1"][:, k * P:(k + 1) * P], hT[:, b], start=True, stop=True)
                last.then_inc(s_up, 1)

            def down(g, q, m):
                b = m % 2
                done(pe, s_ra, g)
                done(pe, s_rv, g)
                done(pe, s_st, g, 2)
                for j in range(SLOTS):
                    for k in range(4):
                        last = nc.tensor.matmul(psO[:, b, j * P:(j + 1) * P], r[:, b, k, j * P:(j + 1) * P], w["w2"][:, k, :],
                                                start=(k == 0), stop=(k == 3))
                last.then_inc(s_mm, 1)
            pipelined(pe, [(up, 2), (down, 3), (turn, 1)], NBLK, 4)


def factor_update(nc, a, w, t):
    with ExitStack() as c:
        ph = Phase(nc, c, "D")
        x, ag, xh = ph.sb("x", [P, 4, SLOTS, XW]), ph.sb("ag", [P, 4, SLOTS, D]), ph.sb("xh", [P, 4, SLOTS, D])
        h, hT, aT, o, xo = ph.sb("h", [P, 2, SLOTS, D]), ph.sb("hT", [P, 2, BLK]), ph.sb("aT", [P, 2, BLK]), ph.sb("o", [P, 2, SLOTS, D]), ph.sb("xo", [P, 4, SLOTS, XW])
        st, mv, sd = ph.sb("st", [P, 2, SLOTS, 6]), ph.sb("mv", [P, 2, SLOTS, 2]), ph.sb("sd", [P, 2, SLOTS])
        psT, psA, psO = ph.ps("psT", [P, 2, BLK]), ph.ps("psA", [P, 2, BLK]), ph.ps("psO", [P, 2, BLK])
        loaded, stored = ph.sems("loaded", 4), ph.dma(w, 4)
        s_h, s_xh, s_ta, s_th, s_aT, s_hT, s_mm, s_st, s_sd, s_xo = ph.step("h", "xh", "ta", "th", "aT", "hT", "mm", "st", "sd", "xo")
        ch1, ch2 = ph.sems("ch", 2)
        block = new_block(nc, c, ph.all)

        @block.sync
        def _(sp):
            ph.start(sp)

            def load(g, q, m):
                done(sp, s_xh, g, 4)
                done(sp, s_ta, g, 4)
                sp.dma_start(ag[:, m], blocks4(t["sum_src"], g * BLK)).then_inc(loaded[m], 16)
                sp.dma_start(x[:, m], blocks4(t["x2"], g * BLK)).then_inc(loaded[m], 16)
            pipelined(sp, [(load, 0)], NBLK, 4)

        @block.gpsimd
        def _(pool):
            def add(g, q, m):
                b = m % 2
                done(pool, s_h, g)
                done(pool, s_st, g, 4)
                nc.gpsimd.tensor_tensor(xh[:, m], x[:, m, :, 0:D], h[:, b], ALU.add).then_inc(s_xh, 1)

            def store(g, q, m):
                b = m % 2
                done(pool, s_xo, g)
                pool.dma_start(blocks4(t["x3"], g * BLK), xo[:, m]).then_inc(stored[m], 16)
            pipelined(pool, [(store, 4), (add, 1)], NBLK, 4)
            for m in range(4):
                pool.wait_ge(stored[m], 16 * ((NBLK + 3 - m) // 4))

        @block.vector
        def _(dve):
            c1, c2 = Tally(dve, ch1, 3), Tally(dve, ch2, 1)

            def evacuate(g, q, m):
                b = m % 2
                done(dve, s_ta, g)
                done(dve, s_mm, g, 2)
                nc.vector.tensor_copy(aT[:, b], psA[:, b]).then_inc(s_aT, 1)

            def add(g, q, m):
                b = m % 2
                done(dve, s_mm, g)
                done(dve, s_xh, g)
                done(dve, s_sd, g, 2)
                reused(dve, stored[m], q * 16)
                c1.begin(g)
                c1.inc(nc.vector.tensor_tensor(o[:, b], psO[:, b].rearrange("p (j d) -> p j d", j=SLOTS),
                                        w["bc"][:, :].unsqueeze(1).to_broadcast([P, SLOTS, D]), ALU.add))
                c1.wait()
                c1.inc(nc.vector.scalar_tensor_tensor(xo[:, m, :, 0:D], o[:, b], 0.0, xh[:, m], ALU.max, ALU.add))
                c1.wait()
                stats4(ph, c1, xo[:, m], st[:, b], mv[:, b]).then_inc(s_st, 1)
                c1.end()

            def finish(g, q, m):
                b = m % 2
                done(dve, s_sd, g)
                c2.begin(g)
                c2.inc(nc.vector.reciprocal(xo[:, m, :, D:D + 1], sd[:, b, :].unsqueeze(2)))
                c2.wait()
                nc.vector.scalar_tensor_tensor(xo[:, m, :, D + 1:XW], mv[:, b, :, 0:1], -1.0, xo[:, m, :, D:D + 1], ALU.mult, ALU.mult).then_inc(s_xo, 1)
                c2.end()
            pipelined(dve, [(finish, 4), (add, 3), (evacuate, 1)], NBLK, 4)

        @block.scalar
        def _(act):
            def node(g, q, m):
                b = m % 2
                act.wait_ge(loaded[m], q * 32 + 32)
                done(act, s_th, g, 2)
                done(act, s_xh, g, 2)
                normalise4(nc, h[:, b], x[:, m], lambda j: x[:, m, j, D:D + 1], lambda j: x[:, m, j, D + 1:XW], ACT.Relu).then_inc(s_h, 1)

            def evacuate(g, q, m):
                b = m % 2
                done(act, s_th, g)
                done(act, s_mm, g, 2)
                nc.scalar.activation(hT[:, b], psT[:, b], ACT.Copy).then_inc(s_hT, 1)

            def deviation(g, q, m):
                b = m % 2
                done(act, s_st, g)
                done(act, s_xo, g, 2)
                nc.scalar.activation(sd[:, b, :], mv[:, b, :, 1], ACT.Sqrt, bias=w["eps"][:, :]).then_inc(s_sd, 1)
            pipelined(act, [(evacuate, 2), (node, 0), (deviation, 3)], NBLK, 4)

        @block.tensor
        def _(pe):
            def turn_sums(g, q, m):
                b = m % 2
                pe.wait_ge(loaded[m], q * 32 + 32)
                done(pe, s_aT, g, 2)
                transposes4(nc, psA[:, b], ag[:, m], w["ident"]).then_inc(s_ta, 1)

            def turn(g, q, m):
                b = m % 2
                done(pe, s_h, g)
                done(pe, s_hT, g, 2)
                transposes4(nc, psT[:, b], h[:, b], w["ident"]).then_inc(s_th, 1)

            def combine(g, q, m):
                b = m % 2
                done(pe, s_hT, g)
                done(pe, s_aT, g)
                done(pe, s_st, g, 2)
                for j in range(SLOTS):
                    nc.tensor.matmul(psO[:, b, j * P:(j + 1) * P], hT[:, b, j * P:(j + 1) * P], w["wc"][:, 0, :], start=True, stop=False)
                    last = nc.tensor.matmul(psO[:, b, j * P:(j + 1) * P], aT[:, b, j * P:(j + 1) * P], w["wc"][:, 1, :], start=False, stop=True)
                last.then_inc(s_mm, 1)
            pipelined(pe, [(combine, 2), (turn, 1), (turn_sums, 0)], NBLK, 4)


def graph_output(nc, a, w, t, out):
    with ExitStack() as c:
        ph = Phase(nc, c, "E")
        x, ag, xb = ph.sb("x", [P, 4, SLOTS, D]), ph.sb("ag", [P, 4, SLOTS, D]), ph.sb("xb", [P, 2, SLOTS, D])
        aT, z, zm, e, rz = ph.sb("aT", [P, 2, BLK]), ph.sb("z", [P, 2, BLK]), ph.sb("zm", [P, 2, BLK]), ph.sb("e", [P, 2, BLK]), ph.sb("rz", [P, 2, BLK])
        u, y, xo = ph.sb("u", [P, 2, SLOTS, D]), ph.sb("y", [P, 2, SLOTS, D]), ph.sb("xo", [P, 4, SLOTS, D])
        st, mv, ve = ph.sb("st", [P, 2, SLOTS, 6]), ph.sb("mv", [P, 2, SLOTS, 2]), ph.sb("ve", [P, 2, SLOTS])
        rs, nm, half = ph.sb("rs", [P, 2, SLOTS]), ph.sb("nm", [P, 2, SLOTS]), ph.sb("half", [P, SLOTS])
        psT, psO = ph.ps("psT", [P, 2, BLK]), ph.ps("psO", [P, 2, BLK])
        loaded, loaded_x, stored = ph.sems("loaded", 4), ph.sems("loaded_x", 4), ph.dma(w, 4)
        s_xb, s_tr, s_aT, s_mm, s_z, s_zm, s_e, s_st, s_ve, s_rs, s_nm, s_y, s_xo = ph.step(
            "xb", "tr", "aT", "mm", "z", "zm", "e", "st", "ve", "rs", "nm", "y", "xo")
        ch1, ch2 = ph.sems("ch", 2)
        s_half = ph.sem("half")
        block = new_block(nc, c, ph.all)

        @block.sync
        def _(sp):
            ph.start(sp)

            def load(g, q, m):
                done(sp, s_tr, g, 4)
                sp.dma_start(ag[:, m], blocks4(t["sum_src"], g * BLK)).then_inc(loaded[m], 16)

            def load_x(g, q, m):
                done(sp, s_xb, g, 4)
                sp.dma_start(x[:, m], blocks4(t["x3"], g * BLK)[:, :, 0:D]).then_inc(loaded_x[m], 16)
            pipelined(sp, [(load, 0), (load_x, 3)], NBLK, 4)

        @block.gpsimd
        def _(pool):
            nc.gpsimd.memset(half[:, :], -0.5).then_inc(s_half, 1)
            pool.wait_ge(s_half, 1)

            def clip(g, q, m):
                b = m % 2
                done(pool, s_z, g)
                done(pool, s_e, g, 2)
                ph.apart(pool)
                nc.gpsimd.tensor_scalar(zm[:, b], z[:, b], 0.0, None, ALU.min).then_inc(s_zm, 1)

            def shift(g, q, m):
                b = m % 2
                pool.wait_ge(loaded_x[m], q * 16 + 16)
                done(pool, s_xo, g, 2)
                nc.gpsimd.tensor_tensor(xb[:, b], x[:, m], w["be3"][:, :].unsqueeze(1).to_broadcast([P, SLOTS, D]), ALU.add).then_inc(s_xb, 1)

            def power(g, q, m):
                b = m % 2
                done(pool, s_st, g)
                done(pool, s_rs, g, 2)
                ph.apart(pool)
                nc.gpsimd.tensor_scalar(ve[:, b, :], mv[:, b, :, 1], LN_EPS, None, ALU.add).then_inc(s_ve, 1)
                done(pool, s_ve, g)
                done(pool, s_nm, g, 2)
                done(pool, s_y, g, 2)
                nc.gpsimd.tensor_tensor(rs[:, b, :], ve[:, b, :], half[:, :], ALU.pow).then_inc(s_rs, 1)

            def store(g, q, m):
                b = m % 2
                done(pool, s_xo, g)
                pool.dma_start(blocks4(out, g * BLK), xo[:, m]).then_inc(stored[m], 16)
            pipelined(pool, [(store, 6), (shift, 5), (power, 4), (clip, 2)], NBLK, 4)
            for m in range(4):
                pool.wait_ge(stored[m], 16 * ((NBLK + 3 - m) // 4))

        @block.vector
        def _(dve):
            c1, c2 = Tally(dve, ch1, 2), Tally(dve, ch2, 1)

            def bias(g, q, m):
                b = m % 2
                done(dve, s_mm, g)
                done(dve, s_zm, g, 2)
                done(dve, s_e, g, 2)
                nc.vector.tensor_tensor(z[:, b].rearrange("p (j d) -> p j d", j=SLOTS), psO[:, b].rearrange("p (j d) -> p j d", j=SLOTS),
                                        w["b3"][:, :].unsqueeze(1).to_broadcast([P, SLOTS, D]), ALU.add).then_inc(s_z, 1)

            def elu(g, q, m):
                b = m % 2
                done(dve, s_e, g)
                done(dve, s_y, g, 2)
                done(dve, s_nm, g, 2)
                c1.begin(g)
                c1.inc(nc.vector.scalar_tensor_tensor(u[:, b], e[:, b].rearrange("p (j d) -> p j d", j=SLOTS), -1.0,
                                               rz[:, b].rearrange("p (j d) -> p j d", j=SLOTS), ALU.add, ALU.add))
                c1.wait()
                stats4(ph, c1, u[:, b], st[:, b], mv[:, b]).then_inc(s_st, 1)
                c1.end()

            def scale(g, q, m):
                b = m % 2
                done(dve, s_rs, g)
                nc.vector.scalar_tensor_tensor(nm[:, b, :], mv[:, b, :, 0], -1.0, rs[:, b, :], ALU.mult, ALU.mult).then_inc(s_nm, 1)

            def add(g, q, m):
                b = m % 2
                done(dve, s_y, g)
                done(dve, s_xb, g)
                reused(dve, stored[m], q * 16)
                c2.begin(g)
                c2.inc(nc.vector.tensor_tensor(y[:, b], y[:, b], w["g3"][:, :].unsqueeze(1).to_broadcast([P, SLOTS, D]), ALU.mult))
                c2.wait()
                nc.vector.tensor_tensor(xo[:, m], y[:, b], xb[:, b], ALU.add).then_inc(s_xo, 1)
                c2.end()
            pipelined(dve, [(add, 6), (scale, 5), (elu, 4), (bias, 2)], NBLK, 4)

        @block.scalar
        def _(act):
            def evacuate(g, q, m):
                b = m % 2
                done(act, s_tr, g)
                done(act, s_mm, g, 2)
                nc.scalar.activation(aT[:, b], psT[:, b], ACT.Copy).then_inc(s_aT, 1)

            def exponential(g, q, m):
                b = m % 2
                done(act, s_z, g)
                done(act, s_st, g, 2)
                nc.scalar.activation(rz[:, b], z[:, b], ACT.Relu)
                done(act, s_zm, g)
                nc.scalar.activation(e[:, b], zm[:, b], ACT.Exp).then_inc(s_e, 1)

            def normalise(g, q, m):
                b = m % 2
                done(act, s_nm, g)
                done(act, s_xo, g, 2)
                normalise4(nc, y[:, b], u[:, b], lambda j: rs[:, b, j:j + 1], lambda j: nm[:, b, j:j + 1], ACT.Identity).then_inc(s_y, 1)
            pipelined(act, [(evacuate, 1), (exponential, 3), (normalise, 5)], NBLK, 4)

        @block.tensor
        def _(pe):
            def turn(g, q, m):
                b = m % 2
                pe.wait_ge(loaded[m], q * 16 + 16)
                done(pe, s_aT, g, 2)
                transposes4(nc, psT[:, b], ag[:, m], w["ident"]).then_inc(s_tr, 1)

            def project(g, q, m):
                b = m % 2
                done(pe, s_aT, g)
                done(pe, s_z, g, 2)
                for j in range(SLOTS):
                    last = nc.tensor.matmul(psO[:, b, j * P:(j + 1) * P], aT[:, b, j * P:(j + 1) * P], w["w3"][:, :], start=True, stop=True)
                last.then_inc(s_mm, 1)
            pipelined(pe, [(turn, 0), (project, 1)], NBLK, 4)


def clear_sums(nc, t):
    with ExitStack() as c:
        zero = c.enter_context(nc.sbuf_tensor("z_zero", [P, 8 * D], F32))
        ready, cleared = c.enter_context(nc.semaphore("z_ready")), c.enter_context(nc.semaphore("z_cleared"))
        block = new_block(nc, c, [ready, cleared])

        @block.vector
        def _(dve):
            nc.vector.memset(zero[:, :], 0.0).then_inc(ready, 1)

        @block.sync
        def _(sp):
            sp.wait_ge(ready, 1)
            with sp.Fori(0, NPAD // (8 * P)) as i:
                for table in (t["sum_dst"], t["sum_src"]):
                    sp.dma_start(table[bass.ds(i * 8 * P, 8 * P), :].rearrange("(p j) d -> p (j d)", p=P),
                                 zero[:, :]).then_inc(cleared, 16)
            sp.wait_ge(cleared, 2 * 16 * (NPAD // (8 * P)))


class Edges(Phase):

    def __init__(self, nc, ctx, w, name, table, key, first, second, widths):
        super().__init__(nc, ctx, name)
        self.table, self.key, self.fields = table, key, (first, second)
        self.rec, self.nxt = self.sb("rec", [P, 4, SLOTS, 4]), self.sb("nxt", [P, 4, SLOTS])
        self.index, self.goal = self.sb("index", [P, 4, 2, SLOTS], I32), self.sb("goal", [P, 4, SLOTS], I32)
        self.same = self.sb("same", [P, 4, SLOTS])
        self.got = [self.sb(f"got{k}", [P, 4, SLOTS, n]) for k, n in enumerate(widths)]
        self.kr, self.flag = self.sb("kr", [P, 2, BLK + 1]), self.sb("flag", [P, 2, BLK])
        self.sums, self.rows = self.sb("sums", [P, 2, BLK]), self.sb("rows", [P, 2, SLOTS, D])
        self.psK, self.psB = self.ps("psK", [P, BLK]), self.ps("psB", [P, BLK])
        self.loaded, self.gathered, self.scattered = self.sems("loaded", 4), self.dma(w, 4), self.dma(w, 4)
        self.own, self.init = self.sem("own"), self.sem("init")
        self.s_idx, self.s_goal, self.s_k, self.s_kr, self.s_flag, self.s_msg, self.s_scan, self.s_back, self.s_rows = self.step(
            "idx", "goal", "k", "kr", "flag", "msg", "scan", "back", "rows")

    def load(self, sp, users):
        def stage(g, q, m):
            for s in users:
                done(sp, s, g, 4)
            sp.dma_start(self.rec[:, m], self.table[bass.ds(g * BLK, BLK), :].rearrange("(j p) f -> p j f", p=P)).then_inc(self.loaded[m], 16)
            sp.dma_start(self.nxt[:, m], self.table[bass.ds(g * BLK + 1, BLK), self.key:self.key + 1].rearrange("(j p) f -> p (j f)", p=P),
                         allow_slow_non_contiguous=True).then_inc(self.loaded[m], 16)
        return stage

    def indices(self, dve):
        def stage(g, q, m):
            dve.wait_ge(self.loaded[m], q * 32 + 32)
            reused(dve, self.gathered[m], q * 16 * SLOTS * sum(f is not None for f in self.fields))
            for k, field in enumerate(self.fields):
                if field is not None:
                    last = self.nc.vector.tensor_copy(self.index[:, m, k], self.rec[:, m, :, field])
            last.then_inc(self.s_idx, 1)
        return stage

    def goals(self, dve):
        nc, tally = self.nc, Tally(dve, self.own, 1)

        def stage(g, q, m):
            reused(dve, self.scattered[m], q * 16 * SLOTS)
            tally.begin(g)
            tally.inc(nc.vector.tensor_tensor(self.same[:, m], self.nxt[:, m], self.rec[:, m, :, self.key], ALU.is_equal))
            tally.wait()
            nc.vector.scalar_tensor_tensor(self.goal[:, m], self.same[:, m], SKIP, self.rec[:, m, :, self.key],
                                           ALU.mult, ALU.add).then_inc(self.s_goal, 1)
            tally.end()
        return stage

    def flags(self, dve, user):
        def stage(g, q, m):
            b = m % 2
            done(dve, self.s_kr, g)
            done(dve, user, g, 2)
            self.nc.vector.tensor_tensor(self.flag[:, b], self.kr[:, b, 1:BLK + 1], self.kr[:, b, 0:BLK], ALU.is_equal).then_inc(self.s_flag, 1)
        return stage

    def clear(self, dve):
        self.nc.vector.memset(self.kr[:, 1, BLK:BLK + 1], -1.0)
        self.nc.vector.memset(self.sums[:, 1, BLK - 1:BLK], 0.0).then_inc(self.init, 1)
        dve.wait_ge(self.init, 1)

    def evacuate(self, dve):
        def stage(g, q, m):
            b = m % 2
            done(dve, self.s_back, g)
            reused(dve, self.scattered[(m + 2) % 4], (q + m // 2) * 16 * SLOTS)
            self.nc.vector.tensor_copy(self.rows[:, b], self.psB[:, :].rearrange("p (j d) -> p j d", j=SLOTS)).then_inc(self.s_rows, 1)
        return stage

    def run_pool(self, pool, tables, target, users):
        nc = self.nc
        limits = [pool.to_reg(x.shape[0] - 1) for x in tables]
        last = pool.to_reg(NPAD - 1)

        def gather(g, q, m):
            done(pool, self.s_idx, g)
            for s in users:
                done(pool, s, g, 4)
            self.apart(pool)
            for k, x in enumerate(tables):
                for j in range(SLOTS):
                    nc.gpsimd.indirect_dma_start(self.got[k][:, m, j, :], None, x,
                                                 bass.IndirectOffsetOnAxis(ap=self.index[:, m, k, j:j + 1], axis=0),
                                                 bounds_check=limits[k], oob_is_err=True).then_inc(self.gathered[m], 16)

        def scatter(g, q, m):
            done(pool, self.s_rows, g)
            done(pool, self.s_goal, g)
            self.apart(pool)
            for j in range(SLOTS):
                nc.gpsimd.indirect_dma_start(target, bass.IndirectOffsetOnAxis(ap=self.goal[:, m, j:j + 1], axis=0),
                                             self.rows[:, m % 2, j, :], None, bounds_check=last, oob_is_err=False
                                             ).then_inc(self.scattered[m], 16)
        pipelined(pool, [(gather, 0), (scatter, 6)], GROUPS, 4)
        for m in range(4):
            pool.wait_ge(self.gathered[m], 16 * SLOTS * len(tables) * ((GROUPS + 3 - m) // 4))
            pool.wait_ge(self.scattered[m], 16 * SLOTS * ((GROUPS + 3 - m) // 4))

    def arrived(self, eng, q, m, tables):
        eng.wait_ge(self.gathered[m], (q + 1) * 16 * SLOTS * tables)

    def key_rows(self, pe):
        def stage(g, q, m):
            pe.wait_ge(self.loaded[m], q * 32 + 32)
            done(pe, self.s_kr, g, 1)
            for j in range(SLOTS):
                last = self.nc.tensor.transpose(self.psK[:, j * P:(j + 1) * P],
                                                self.rec[:, m, j, self.key:self.key + 1].to_broadcast([P, P]), self.ident[:, :])
            last.then_inc(self.s_k, 1)
        return stage

    def back(self, pe):
        def stage(g, q, m):
            done(pe, self.s_scan, g)
            done(pe, self.s_rows, g, 1)
            for j in range(SLOTS):
                last = self.nc.tensor.transpose(self.psB[:, j * P:(j + 1) * P], self.sums[:, m % 2, j * P:(j + 1) * P], self.ident[:, :])
            last.then_inc(self.s_back, 1)
        return stage

    def key_copy(self, act):
        def stage(g, q, m):
            b = m % 2
            done(act, self.s_k, g)
            done(act, self.s_kr, g, 1)
            done(act, self.s_flag, g, 2)
            act.wait_ge(self.init, 1)
            self.nc.scalar.activation(self.kr[:, b, 0:1], self.kr[:, 1 - b, BLK:BLK + 1], ACT.Copy)
            self.nc.scalar.activation(self.kr[:, b, 1:BLK + 1], self.psK[:, :], ACT.Copy).then_inc(self.s_kr, 1)
        return stage


def message_edges(nc, a, w, t, layer):
    with ExitStack() as c:
        if layer == 1:
            ph = Edges(nc, c, w, "F1", t["by_dst"], 1, 0, 2, [XW, D])
            tables, target = [t["x1"], a["edge_attr"]], t["sum_dst"]
        elif layer == 2:
            ph = Edges(nc, c, w, "F2", t["by_src"], 0, 0, 1, [XW, D])
            tables, target = [t["x2"], a["factors"]], t["sum_src"]
        else:
            ph = Edges(nc, c, w, "F3", t["by_src"], 0, 1, None, [XW])
            tables, target = [t["x3"]], t["sum_src"]
        ph.ident = w["ident"]
        nt = len(tables)
        h = ph.sb("h", [P, 2, SLOTS, D])
        bT, hT, msg = ph.sb("bT", [P, 2, BLK]), ph.sb("hT", [P, 2, BLK]), ph.sb("msg", [P, 2, BLK])
        zc, zb, ex, den, num = (ph.sb(n, [P, 2, BLK]) for n in ("zc", "zb", "ex", "den", "num"))
        psE, psH, psZ = ph.ps("psE", [P, BLK]), ph.ps("psH", [P, BLK]), ph.ps("psZ", [P, 2, BLK])
        s_h, s_hw, s_te, s_bT, s_th, s_hT, s_z, s_zb, s_zc, s_ex = ph.step("h", "hw", "te", "bT", "th", "hT", "z", "zb", "zc", "ex")
        ch = ph.sem("ch")
        block = new_block(nc, c, ph.all)

        @block.sync
        def _(sp):
            ph.start(sp)
            pipelined(sp, [(ph.load(sp, [ph.s_idx, ph.s_goal, ph.s_k] + ([s_hw] if layer == 3 else [])), 0)], GROUPS, 4)

        @block.gpsimd
        def _(pool):
            ph.run_pool(pool, tables, target, [s_h] + ([s_te] if nt == 2 else []))

        @block.vector
        def _(dve):
            ph.clear(dve)
            c1 = Tally(dve, ch, 4)

            def operand(g, q, m):
                done(dve, s_te, g)
                done(dve, s_z, g, 2)
                nc.vector.tensor_copy(bT[:, m % 2], psE[:, :]).then_inc(s_bT, 1)

            def weigh(g, q, m):
                done(dve, s_h, g)
                nc.vector.tensor_tensor(h[:, m % 2], h[:, m % 2], ph.rec[:, m, :, 3:4].to_broadcast([P, SLOTS, D]), ALU.mult).then_inc(s_hw, 1)

            def clip(g, q, m):
                done(dve, s_zb, g)
                done(dve, s_ex, g, 2)
                nc.vector.tensor_scalar(zc[:, m % 2], zb[:, m % 2], 30.0, None, ALU.min).then_inc(s_zc, 1)

            def mish(g, q, m):
                b = m % 2
                done(dve, s_ex, g)
                done(dve, ph.s_scan, g, 1)
                c1.begin(g)
                c1.inc(nc.vector.scalar_tensor_tensor(num[:, b], ex[:, b], 2.0, ex[:, b], ALU.add, ALU.mult))
                c1.wait()
                c1.inc(nc.vector.tensor_scalar(den[:, b], num[:, b], 2.0, None, ALU.add))
                c1.inc(nc.vector.tensor_tensor(num[:, b], num[:, b], zb[:, b], ALU.mult))
                c1.wait()
                c1.inc(nc.vector.reciprocal(den[:, b], den[:, b]))
                c1.wait()
                nc.vector.tensor_tensor(msg[:, b], num[:, b], den[:, b], ALU.mult).then_inc(ph.s_msg, 1)
                c1.end()

            def scan(g, q, m):
                b = m % 2
                done(dve, ph.s_msg if layer < 3 else s_z, g)
                done(dve, ph.s_flag, g)
                done(dve, ph.s_scan, g, 1)
                done(dve, ph.s_back, g, 2)
                nc.vector.tensor_tensor_scan(ph.sums[:, b], ph.flag[:, b], msg[:, b] if layer < 3 else psZ[:, b],
                                             ph.sums[:, 1 - b, BLK - 1:BLK], ALU.mult, ALU.add).then_inc(ph.s_scan, 1)
            index, goal, flags, evacuate = ph.indices(dve), ph.goals(dve), ph.flags(dve, ph.s_scan), ph.evacuate(dve)
            if layer == 1:
                stages = [(index, 0), (operand, 2), (clip, 3), (evacuate, 5), (flags, 3), (goal, 3), (mish, 4), (scan, 4)]
            elif layer == 2:
                stages = [(index, 0), (operand, 2), (scan, 4), (evacuate, 5), (flags, 3), (goal, 3)]
            else:
                stages = [(index, 0), (weigh, 2), (scan, 4), (evacuate, 5), (flags, 3), (goal, 3)]
            pipelined(dve, stages, GROUPS, 4)

        @block.scalar
        def _(act):
            def node(g, q, m):
                b = m % 2
                ph.arrived(act, q, m, nt)
                x = ph.got[0][:, m]
                done(act, {1: s_z, 2: s_th, 3: s_z}[layer], g, 2)
                normalise4(nc, h[:, b], x, lambda j: x[:, j, D:D + 1], lambda j: x[:, j, D + 1:XW], ACT.Relu).then_inc(s_h, 1)

            def argument(g, q, m):
                b = m % 2
                done(act, s_z, g)
                done(act, ph.s_msg, g, 2)
                nc.scalar.activation(zb[:, b], psZ[:, b], ACT.Identity, bias=w["bee"][:, :]).then_inc(s_zb, 1)

            def exponential(g, q, m):
                b = m % 2
                done(act, s_zc, g)
                done(act, ph.s_msg, g, 2)
                nc.scalar.activation(ex[:, b], zc[:, b], ACT.Exp).then_inc(s_ex, 1)

            def evacuate(g, q, m):
                done(act, s_th, g)
                done(act, s_z, g, 2)
                nc.scalar.activation(hT[:, m % 2], psH[:, :], ACT.Copy).then_inc(s_hT, 1)

            def message(g, q, m):
                done(act, s_z, g)
                done(act, ph.s_scan, g, 2)
                nc.scalar.activation(msg[:, m % 2], psZ[:, m % 2], ACT.Relu, bias=w["bm"][:, :]).then_inc(ph.s_msg, 1)
            keys = ph.key_copy(act)
            if layer == 1:
                stages = [(exponential, 4), (argument, 3), (keys, 3), (node, 1)]
            elif layer == 2:
                stages = [(evacuate, 2), (keys, 3), (message, 3), (node, 1)]
            else:
                stages = [(keys, 3), (node, 1)]
            pipelined(act, stages, GROUPS, 4)

        @block.tensor
        def _(pe):
            def turn(g, q, m):
                ph.arrived(pe, q, m, nt)
                done(pe, s_bT, g, 1)
                transposes4(nc, psE[:, :], ph.got[1][:, m], w["ident"]).then_inc(s_te, 1)

            def turn_node(g, q, m):
                done(pe, s_h, g)
                done(pe, s_hT, g, 1)
                transposes4(nc, psH[:, :], h[:, m % 2], w["ident"]).then_inc(s_th, 1)

            def product1(g, q, m):
                b = m % 2
                done(pe, s_bT, g)
                done(pe, s_h, g)
                done(pe, s_zb, g, 2)
                nc.tensor.matmul(psZ[:, b], w["we"][:, :], bT[:, b], start=True, stop=False)
                for j in range(SLOTS):
                    last = nc.tensor.matmul(psZ[:, b, j * P:(j + 1) * P], h[:, b, j, :], w["ident"][:, :], start=False,
                                            stop=(j == SLOTS - 1))
                last.then_inc(s_z, 1)

            def product2(g, q, m):
                b = m % 2
                done(pe, s_bT, g)
                done(pe, s_hT, g)
                done(pe, ph.s_msg, g, 2)
                nc.tensor.matmul(psZ[:, b], w["wm"][:, 0, :], hT[:, b], start=True, stop=False)
                nc.tensor.matmul(psZ[:, b], w["wm"][:, 1, :], bT[:, b], start=False, stop=True).then_inc(s_z, 1)

            def turn_weighed(g, q, m):
                done(pe, s_hw, g)
                done(pe, ph.s_scan, g, 2)
                transposes4(nc, psZ[:, m % 2], h[:, m % 2], w["ident"]).then_inc(s_z, 1)
            keys, back = ph.key_rows(pe), ph.back(pe)
            if layer == 1:
                stages = [(back, 5), (product1, 2), (keys, 2), (turn, 1)]
            elif layer == 2:
                stages = [(back, 5), (product2, 3), (turn_node, 2), (keys, 2), (turn, 1)]
            else:
                stages = [(back, 5), (turn_weighed, 3), (keys, 2)]
            pipelined(pe, stages, GROUPS, 4)


def attention_edges(nc, a, w, t):
    with ExitStack() as c:
        ph = Edges(nc, c, w, "F0", t["by_dst"], 1, 0, 1, [AW, AW])
        ph.ident = w["ident"]
        pre, lg, v = ph.sb("pre", [P, 2, 2, SLOTS, HEADS]), ph.sb("lg", [P, 4, 2, SLOTS, HEADS]), ph.sb("v", [P, 2, SLOTS, HEADS])
        pen, m_ = ph.sb("pen", [HEADS, 2, BLK]), ph.sb("m", [HEADS, 2, BLK + 1])
        d, r, dsum = ph.sb("d", [HEADS, 2, 2, BLK]), ph.sb("r", [HEADS, 4, BLK]), ph.sb("dsum", [HEADS, 2, BLK])
        lm, p_ = ph.sb("lm", [P, 2, 2, SLOTS, HEADS]), ph.sb("p", [P, 4, 2, SLOTS, HEADS])
        phs, rS = ph.sb("phs", [P, 2, SLOTS, D]), ph.sb("rS", [P, 2, BLK])
        dn, rd, t1, t2 = ph.sb("dn", [P, 2, SLOTS, HEADS]), ph.sb("rd", [P, 2, SLOTS, HEADS]), ph.sb("t1", [P, 4, SLOTS, D]), ph.sb("t2", [P, 2, SLOTS, D])
        psV, psP, psR, psM = ph.ps("psV", [P, BLK]), ph.ps("psP", [P, BLK]), ph.ps("psR", [P, BLK]), ph.ps("psM", [P, BLK])
        psS, psD = ph.ps("psS", [P, SLOTS, HEADS]), ph.ps("psD", [P, SLOTS, HEADS])
        s_v, s_vT, s_m, s_d, s_r, s_mT, s_lm, s_p, s_ph, s_mm, s_rS = ph.step("v", "vT", "m", "d", "r", "mT", "lm", "p", "phs", "mm", "rS")
        ch1, ch2, ch3 = ph.sems("ch", 3)
        block = new_block(nc, c, ph.all)

        def heads(x):
            return x.unsqueeze(3).to_broadcast([P, SLOTS, HEADS, HD])

        def split(x):
            return x.rearrange("p j (h f) -> p j h f", h=HEADS)

        @block.sync
        def _(sp):
            ph.start(sp)
            pipelined(sp, [(ph.load(sp, [ph.s_idx, ph.s_goal, ph.s_k]), 0)], GROUPS, 4)

        @block.gpsimd
        def _(pool):
            ph.run_pool(pool, [t["att"], t["att"]], t["gat"], [s_ph])

        @block.vector
        def _(dve):
            nc.vector.memset(m_[:, 1, BLK:BLK + 1], 0.0)
            nc.vector.memset(dsum[:, 1, BLK - 1:BLK], 0.0)
            ph.clear(dve)
            c1, c2, c3 = Tally(dve, ch1, 2), Tally(dve, ch2, 2), Tally(dve, ch3, 2)

            def logits(g, q, m):
                b = m % 2
                ph.arrived(dve, q, m, 2)
                done(dve, s_vT, g, 2)
                done(dve, s_lm, g, 2)
                c1.begin(g)
                ga, gb = ph.got[0][:, m], ph.got[1][:, m]
                nc.vector.tensor_tensor(pre[:, b, 0], ga[:, :, D:D + HEADS], gb[:, :, D + HEADS:AW], ALU.add)
                c1.inc(nc.vector.tensor_tensor(pre[:, b, 1], gb[:, :, D:D + HEADS], gb[:, :, D + HEADS:AW], ALU.add))
                c1.wait()
                c1.inc(nc.vector.scalar_tensor_tensor(lg[:, m].rearrange("p k j h -> p (k j h)"), pre[:, b].rearrange("p k j h -> p (k j h)"), 0.2,
                                                      pre[:, b].rearrange("p k j h -> p (k j h)"), ALU.mult, ALU.max))
                c1.wait()
                nc.vector.tensor_tensor(v[:, b], lg[:, m, 0], lg[:, m, 1], ALU.max).then_inc(s_v, 1)
                c1.end()

            def maximum(g, q, m):
                b = m % 2
                done(dve, ph.s_flag, g)
                done(dve, s_d, g, 2)
                c2.begin(g)
                c2.inc(nc.vector.tensor_scalar(pen[:, b], ph.flag[0:HEADS, b], 1.0, -LOWEST, ALU.subtract, ALU.mult))
                done(dve, s_vT, g)
                done(dve, s_mT, g, 2)
                done(dve, s_m, g, 1)
                c2.wait()
                nc.vector.tensor_copy(m_[:, b, 0:1], m_[:, 1 - b, BLK:BLK + 1])
                nc.vector.tensor_tensor_scan(m_[:, b, 1:BLK + 1], pen[:, b], psV[0:HEADS, :], m_[:, 1 - b, BLK:BLK + 1],
                                             ALU.add, ALU.max).then_inc(s_m, 1)
                done(dve, s_m, g)
                done(dve, s_r, g, 2)
                c2.inc(nc.vector.tensor_tensor(d[:, b, 0], m_[:, b, 0:BLK], m_[:, b, 1:BLK + 1], ALU.subtract))
                c2.wait()
                nc.vector.tensor_tensor(d[:, b, 1], d[:, b, 0], pen[:, b], ALU.add).then_inc(s_d, 1)
                c2.end()

            def exponents(g, q, m):
                b = m % 2
                done(dve, s_mT, g)
                done(dve, s_p, g, 2)
                for k in range(2):
                    last = nc.vector.tensor_tensor(lm[:, b, k], lg[:, m, k], psS[:, :, :], ALU.subtract)
                last.then_inc(s_lm, 1)

            def weighed(g, q, m):
                b = m % 2
                done(dve, s_p, g)
                done(dve, s_mm, g, 2)
                done(dve, ph.s_rows, g, 4)
                nc.vector.tensor_tensor(split(t1[:, m]), split(ph.got[1][:, m, :, 0:D]), heads(p_[:, m, 1]), ALU.mult)
                nc.vector.tensor_tensor(split(phs[:, b]), split(ph.got[0][:, m, :, 0:D]), heads(p_[:, m, 0]), ALU.mult).then_inc(s_ph, 1)

            def scan(g, q, m):
                b = m % 2
                done(dve, s_mm, g)
                done(dve, s_rS, g)
                done(dve, ph.s_scan, g, 1)
                done(dve, ph.s_back, g, 2)
                nc.vector.tensor_tensor_scan(dsum[:, b], r[:, m], psP[0:HEADS, :], dsum[:, 1 - b, BLK - 1:BLK], ALU.mult, ALU.add)
                nc.vector.tensor_tensor_scan(ph.sums[:, b], rS[:, b], psM[:, :], ph.sums[:, 1 - b, BLK - 1:BLK],
                                             ALU.mult, ALU.add).then_inc(ph.s_scan, 1)

            def finish(g, q, m):
                b = m % 2
                done(dve, ph.s_back, g)
                done(dve, ph.s_rows, g, 1)
                reused(dve, ph.scattered[(m + 2) % 4], (q + m // 2) * 16 * SLOTS)
                c3.begin(g)
                nc.vector.tensor_tensor(dn[:, b], psD[:, :, :], p_[:, m, 1], ALU.add)
                c3.inc(nc.vector.tensor_tensor(t2[:, b], t1[:, m], ph.psB[:, :].rearrange("p (j d) -> p j d", j=SLOTS), ALU.add))
                c3.wait()
                c3.inc(nc.vector.reciprocal(rd[:, b], dn[:, b]))
                c3.wait()
                nc.vector.tensor_tensor(split(ph.rows[:, b]), split(t2[:, b]), heads(rd[:, b]), ALU.mult).then_inc(ph.s_rows, 1)
                c3.end()
            pipelined(dve, [(ph.indices(dve), 0), (exponents, 3), (finish, 5), (logits, 1), (ph.flags(dve, s_d), 2), (maximum, 2), (weighed, 3),
                            (ph.goals(dve), 3), (scan, 4)], GROUPS, 4)

        @block.scalar
        def _(act):
            def decay(g, q, m):
                b = m % 2
                done(act, s_d, g)
                done(act, ph.s_scan, g, 4)
                nc.scalar.activation(r[:, m], d[:, b, 1], ACT.Exp).then_inc(s_r, 1)

            def weights(g, q, m):
                b = m % 2
                done(act, s_lm, g)
                done(act, ph.s_rows, g, 4)
                nc.scalar.activation(p_[:, m], lm[:, b], ACT.Exp).then_inc(s_p, 1)

            def spread(g, q, m):
                done(act, s_mm, g)
                done(act, ph.s_scan, g, 2)
                nc.scalar.activation(rS[:, m % 2], psR[:, :], ACT.Copy).then_inc(s_rS, 1)
            pipelined(act, [(ph.key_copy(act), 2), (weights, 3), (decay, 3), (spread, 4)], GROUPS, 4)

        @block.tensor
        def _(pe):
            def turn_logits(g, q, m):
                done(pe, s_v, g)
                done(pe, s_m, g, 1)
                ph.apart(pe)
                for j in range(SLOTS):
                    last = nc.tensor.transpose(psV[0:HEADS, j * P:(j + 1) * P], v[:, m % 2, j, :], w["ident"][:, :])
                last.then_inc(s_vT, 1)

            def turn_maximum(g, q, m):
                done(pe, s_m, g)
                done(pe, s_lm, g, 1)
                ph.apart(pe)
                for j in range(SLOTS):
                    last = nc.tensor.transpose(psS[:, j, :], m_[:, m % 2, 1 + j * P:1 + (j + 1) * P], w["ident"][0:HEADS, 0:HEADS])
                last.then_inc(s_mT, 1)

            def turn_rows(g, q, m):
                b = m % 2
                done(pe, s_r, g)
                done(pe, ph.s_scan, g, 1)
                done(pe, s_rS, g, 1)
                nc.tensor.matmul(psR[:, :], w["expand"][:, :], r[:, m], start=True, stop=True)
                done(pe, s_ph, g)
                transposes4(nc, psM[:, :], phs[:, b], w["ident"])
                for j in range(SLOTS):
                    last = nc.tensor.transpose(psP[0:HEADS, j * P:(j + 1) * P], p_[:, m, 0, j, :], w["ident"][:, :])
                last.then_inc(s_mm, 1)

            def back(g, q, m):
                done(pe, ph.s_scan, g)
                done(pe, ph.s_rows, g, 1)
                for j in range(SLOTS):
                    nc.tensor.transpose(ph.psB[:, j * P:(j + 1) * P], ph.sums[:, m % 2, j * P:(j + 1) * P], w["ident"][:, :])
                    last = nc.tensor.transpose(psD[:, j, :], dsum[:, m % 2, j * P:(j + 1) * P], w["ident"][0:HEADS, 0:HEADS])
                last.then_inc(ph.s_back, 1)
            pipelined(pe, [(back, 5), (turn_rows, 4), (turn_logits, 1), (ph.key_rows(pe), 1), (turn_maximum, 2)], GROUPS, 4)


def program(nc, a, out):
    t = tables(nc)
    with ExitStack() as c:
        def sb(name, shape):
            return c.enter_context(nc.sbuf_tensor("k_" + name, shape, F32))
        w = {n: sb(n, [P, k]) for n, k in (
            ("ident", P), ("hmask", HEADS), ("wl", AW), ("proj", D), ("c0", D), ("g0", D), ("be0", D), ("we", D), ("bee", 1),
            ("eps1", 1), ("eps", 1), ("w1", HID), ("b1", 4), ("b2", D), ("bm", 1), ("bc", D), ("w3", D), ("b3", D),
            ("g3", D), ("be3", D))}
        w["expand"] = sb("expand", [HEADS, P])
        w["w2"], w["wm"], w["wc"] = sb("w2", [P, 4, D]), sb("wm", [P, 2, D]), sb("wc", [P, 2, D])
        w["dma"] = [c.enter_context(nc.semaphore(f"pool_dma{k}")) for k in range(8)]
        prepare(nc, a, w)
        clear_sums(nc, t)
        sort_edges(nc, a, w, t, "dst")
        sort_edges(nc, a, w, t, "src")
        attention_inputs(nc, a, w, t)
        attention_edges(nc, a, w, t)
        attention_outputs(nc, a, w, t)
        message_edges(nc, a, w, t, 1)
        mlp(nc, a, w, t)
        message_edges(nc, a, w, t, 2)
        factor_update(nc, a, w, t)
        message_edges(nc, a, w, t, 3)
        graph_output(nc, a, w, t, out)


def kernel(**inputs):
    import numpy as np
    import concourse.bacc as bacc
    from concourse.bass_utils import run_bass_kernel_spmd

    v = {k: np.asarray(x) for k, x in inputs.items()}

    def rows(x, count, fill=0):
        full = np.full((count,) + x.shape[1:], fill, x.dtype)
        full[:x.shape[0]] = x
        return full

    def every(x):
        return np.ascontiguousarray(np.broadcast_to(x.reshape(1, -1), (P, x.size)))

    def tiles(x):
        return np.ascontiguousarray(np.moveaxis(x.reshape((TILES, P) + x.shape[1:]), 0, 1))
    i = np.arange(P)
    src, dst = rows(v["src"], EPAD, N), rows(v["dst"], EPAD, N)
    rec = np.zeros((EPAD, 2), np.float32)
    rec[:E, 0] = np.arange(E)
    rec[:E, 1] = v["edge_weight"]
    arrays = {
        "ident": np.eye(P, dtype=np.float32), "hmask": (i[:, None] // HD == np.arange(HEADS)[None, :]).astype(np.float32),
        "expand": (i[None, :] // HD == np.arange(HEADS)[:, None]).astype(np.float32),
        "iota": every(np.arange(LO, dtype=np.float32)), "iotap": np.stack([i, i + P], 1).astype(np.float32),
        "tri": np.stack([i[None, :] < i[:, None], i[:, None] < i[None, :], np.ones((P, P), bool)], 1).astype(np.float32),
        "sentinel": np.tile(np.array([[N, N, 0, 0]], np.float32), (PAD_ROWS, 1)),
        "x": rows(v["x"], NPAD), "factors": rows(v["L2_gnn_factors"], NPAD), "edge_attr": v["edge_attr_128"],
        "src_col": tiles(src), "dst_col": tiles(dst), "src_row": src[None], "dst_row": dst[None], "rec_col": tiles(rec),
        "linw": v["L0_gnn_lin_w"], "linwT": np.ascontiguousarray(v["L0_gnn_lin_w"].T),
        "projT": np.ascontiguousarray(v["L0_gnn_proj_w"].T),
        "att": np.stack([v["L0_gnn_att_src"].reshape(-1), v["L0_gnn_att_dst"].reshape(-1)], 1),
        "gatb": np.ascontiguousarray(every(v["L0_gnn_gat_bias"]).T), "projb": every(v["L0_gnn_proj_b"]),
        "g0": every(v["L0_gnn_ln_gamma"]), "be0": every(v["L0_gnn_ln_beta"]),
        "we": v["L1_gnn_W_e_k"], "bee": v["L1_gnn_W_e_b"].reshape(-1, 1), "eps1": every(v["L1_gnn_eps"]),
        "w1": v["L1_gnn_W1"], "glob": v["L1_gnn_globals_g"].reshape(-1, 1),
        "b1": np.ascontiguousarray(v["L1_gnn_b1"].reshape(4, P).T), "w2": v["L1_gnn_W2"], "b2": every(v["L1_gnn_b2"]),
        "wm": v["L2_gnn_Wm"], "bm": v["L2_gnn_bm"].reshape(-1, 1), "wc": v["L2_gnn_Wc"], "bc": every(v["L2_gnn_bc"]),
        "w3": v["L3_gnn_weight"], "b3": every(v["L3_gnn_bias"]), "g3": every(v["L3_gnn_ln_gamma"]), "be3": every(v["L3_gnn_ln_beta"]),
    }
    nc = bacc.Bacc("TRN2", target_bir_lowering=False, num_devices=1)
    a = {n: nc.dram_tensor(f"in_{n}", x.shape, mybir.dt.from_np(x.dtype), kind="ExternalInput").ap() for n, x in arrays.items()}
    out = nc.dram_tensor("out_x", (NPAD, D), F32, kind="ExternalOutput").ap()
    program(nc, a, out)
    r = run_bass_kernel_spmd(nc, [{f"in_{n}": x for n, x in arrays.items()}], core_ids=[0])
    return r.results[0]["out_x"][:N]
```

```python
import concourse.bass as bass
from concourse import mybir
from contextlib import ExitStack

F32, I32, BF16 = mybir.dt.float32, mybir.dt.int32, mybir.dt.bfloat16
ALU = mybir.AluOpType
ACT = mybir.ActivationFunctionType

P = 128
D = 128
N, E = 50000, 25000
HEADS, HD = 8, 16
HID = 512
SLOTS = 4
BLK = P * SLOTS
NBLK = 98
NPAD = NBLK * BLK
TILES = 196
EPAD = TILES * P
GROUPS = TILES // SLOTS
SROWS = EPAD + 16
PAD_ROWS = SROWS - EPAD
AW = D + 2 * HEADS
XW = D + 2
LO = 256
PAIR = TILES // NBLK
LN_EPS = 1e-5
SKIP = 1.0e6
LOWEST = -3.0e38


class Tally:

    def __init__(self, eng, sem, per):
        self.eng, self.sem, self.per = eng, sem, per

    def begin(self, turn):
        self.base, self.n = turn * self.per, 0

    def inc(self, instruction):
        self.n += 1
        instruction.then_inc(self.sem, 1)

    def wait(self):
        self.eng.wait_ge(self.sem, self.base + self.n)

    def end(self):
        assert self.n == self.per, f"per must be {self.n}"


def tables(nc):
    def dram(name, rows, cols):
        return nc.dram_tensor(name, (rows, cols), F32).ap()
    return {
        "att": dram("t_att", NPAD, AW), "gat": dram("t_gat", NPAD, D),
        "x1": dram("t_x1", NPAD, XW), "x2": dram("t_x2", NPAD, XW), "x3": dram("t_x3", NPAD, XW),
        "sum_dst": dram("t_sum_dst", NPAD, D), "sum_src": dram("t_sum_src", NPAD, D),
        "by_dst": dram("t_by_dst", SROWS, 4), "by_src": dram("t_by_src", SROWS, 4),
        "edge_attr": dram("t_edge_attr", EPAD, D), "factors": dram("t_factors", EPAD, D),
    }


def blocks4(table, row):
    return table[bass.ds(row, BLK), :].rearrange("(p j) d -> p j d", p=P)


def new_block(nc, ctx, sems):
    def zero():
        with nc.Block() as after:
            @after.gpsimd
            def _(pool):
                pool.dma_reset()
                for s in sems:
                    pool.sem_clear(s)
    ctx.callback(zero)
    return ctx.enter_context(nc.Block())


def prepare(nc, a, w):
    with ExitStack() as c:
        loaded, folded, vec, step = (c.enter_context(nc.semaphore(n)) for n in
                                     ("w_loaded", "w_folded", "w_vec", "w_step"))
        ps = c.enter_context(nc.psum_tensor("w_ps", [P, 4, 512], F32))
        att = c.enter_context(nc.sbuf_tensor("w_att", [P, 2], F32))
        attm = c.enter_context(nc.sbuf_tensor("w_attm", [P, 2 * HEADS], F32))
        linw = c.enter_context(nc.sbuf_tensor("w_linw", [P, D], F32))
        gatb = c.enter_context(nc.sbuf_tensor("w_gatb", [P, D], F32))
        projb = c.enter_context(nc.sbuf_tensor("w_projb", [P, D], F32))
        w1b = c.enter_context(nc.sbuf_tensor("w_w1b", [P, HID], F32))
        glob = c.enter_context(nc.sbuf_tensor("w_glob", [P, 1], F32))
        b1 = c.enter_context(nc.sbuf_tensor("w_b1", [P, 4], F32))
        block = new_block(nc, c, [loaded, folded, vec, step])
        loads = [(w["ident"][:, :], a["ident"]), (w["hmask"][:, :], a["hmask"]), (w["expand"][:, :], a["expand"]),
                 (w["wl"][:, 0:D], a["linwT"]), (w["proj"][:, :], a["projT"]), (linw[:, :], a["linw"]),
                 (att[:, :], a["att"]), (gatb[:, :], a["gatb"]), (projb[:, :], a["projb"]),
                 (w["g0"][:, :], a["g0"]), (w["be0"][:, :], a["be0"]), (w["we"][:, :], a["we"]), (w["bee"][:, :], a["bee"]),
                 (w["eps1"][:, :], a["eps1"]), (w["w1"][:, :], a["w1"][0:D, :]), (w1b[:, :], a["w1"][D:2 * D, :]),
                 (glob[:, :], a["glob"]), (b1[:, :], a["b1"]),
                 (w["w2"][:, :, :], a["w2"].rearrange("(c p) o -> p c o", p=P)), (w["b2"][:, :], a["b2"]),
                 (w["wm"][:, :, :], a["wm"].rearrange("(c p) o -> p c o", p=P)), (w["bm"][:, :], a["bm"]),
                 (w["wc"][:, :, :], a["wc"].rearrange("(c p) o -> p c o", p=P)), (w["bc"][:, :], a["bc"]),
                 (w["w3"][:, :], a["w3"]), (w["b3"][:, :], a["b3"]), (w["g3"][:, :], a["g3"]), (w["be3"][:, :], a["be3"])]

        @block.sync
        def _(sp):
            for dst, src in loads:
                sp.dma_start(dst, src).then_inc(loaded, 16)

        @block.vector
        def _(dve):
            nc.vector.memset(w["eps"][:, :], LN_EPS)
            dve.wait_ge(loaded, 16 * len(loads))
            for k in range(2):
                nc.vector.tensor_scalar(attm[:, k * HEADS:(k + 1) * HEADS], w["hmask"][:, :], att[:, k:k + 1], None,
                                        ALU.mult).then_inc(vec, 1)
            nc.vector.tensor_scalar(w["eps1"][:, :], w["eps1"][:, :], 1.0, None, ALU.add).then_inc(step, 1)
            dve.wait_ge(folded, 1)
            nc.vector.tensor_copy(w["wl"][:, D:AW], ps[:, 0, 0:2 * HEADS])
            nc.vector.tensor_tensor(w["c0"][:, :], ps[:, 1, 0:D], projb[:, :], ALU.add)
            nc.vector.tensor_tensor(w["b1"][:, :], ps[:, 2, 0:4], b1[:, :], ALU.add).then_inc(step, 1)
            dve.wait_ge(step, 2)

        @block.tensor
        def _(pe):
            pe.wait_ge(loaded, 16 * len(loads))
            pe.wait_ge(vec, 2)
            nc.tensor.matmul(ps[:, 0, 0:2 * HEADS], linw[:, :], attm[:, :], start=True, stop=True)
            nc.tensor.matmul(ps[:, 1, 0:D], gatb[:, :], w["proj"][:, :], start=True, stop=True)
            for k in range(4):
                last = nc.tensor.matmul(ps[:, 2, k:k + 1], w1b[:, k * D:(k + 1) * D], glob[:, :], start=True, stop=True)
            last.then_inc(folded, 1)



AHEAD = 4


def done(eng, sem, g, before=0):
    eng.wait_ge(sem, g + (AHEAD + 1 - before))


def reused(eng, sem, value):
    if not (isinstance(value, int) and value == 0):
        eng.wait_ge(sem, value)


def pipelined(eng, stages, count, unroll):
    longest = max(lag for _, lag in stages)
    head = longest + unroll
    turns = (count - head) // unroll

    def step(tau, i):
        for stage, lag in stages:
            at = tau - lag
            if i is None:
                if 0 <= at < count:
                    stage(at, at // unroll, at % unroll)
            else:
                stage(i * unroll + at, i + at // unroll, at % unroll)
    for tau in range(head):
        step(tau, None)
    with eng.Fori(0, turns) as i:
        for u in range(unroll):
            step(head + u, i)
    for tau in range(head + turns * unroll, count + longest):
        step(tau, None)


class Phase:

    def __init__(self, nc, ctx, name):
        self.nc, self.ctx, self.name, self.steps, self.all = nc, ctx, name, [], []
        self.gate = self.sem("gate")

    def sb(self, name, shape, dt=F32):
        return self.ctx.enter_context(self.nc.sbuf_tensor(f"{self.name}_{name}", shape, dt))

    def ps(self, name, shape):
        return self.ctx.enter_context(self.nc.psum_tensor(f"{self.name}_{name}", shape, F32))

    def sem(self, name):
        self.all.append(self.ctx.enter_context(self.nc.semaphore(f"{self.name}_{name}")))
        return self.all[-1]

    def dma(self, w, n):
        first = sum(s in w["dma"] for s in self.all)
        self.all += w["dma"][first:first + n]
        return w["dma"][first:first + n]

    def sems(self, name, n):
        return [self.sem(f"{name}{k}") for k in range(n)]

    def step(self, *names):
        made = [self.sem(n) for n in names]
        self.steps += made
        return made

    def apart(self, eng):
        eng.sem_inc(self.gate, 1)

    def start(self, eng):
        for s in self.steps:
            eng.sem_inc(s, AHEAD)


def transposes4(nc, out, src, ident):
    for j in range(SLOTS):
        last = nc.tensor.transpose(out[:, j * P:(j + 1) * P], src[:, j, 0:D], ident[:, :])
    return last


def stats4(ph, tally, src, st, mv):
    nc = ph.nc
    for j in range(SLOTS):
        last = nc.vector.bn_stats(st[:, j, :], src[:, j, 0:D])
    tally.inc(last)
    tally.wait()
    ph.apart(tally.eng)
    for j in range(SLOTS):
        last = nc.vector.bn_aggr(mv[:, j, :], st[:, j, :])
    return last


def normalise4(nc, out, src, scale, shift, func):
    for j in range(SLOTS):
        last = nc.scalar.activation(out[:, j, 0:D], src[:, j, 0:D], func, bias=shift(j), scale=scale(j))
    return last


def count_keys(nc, a, w, t, s):
    STEPS = TILES // SLOTS
    with ExitStack() as c:
        ph = Phase(nc, c, "H")
        ints, parts = ph.sb("ints", [P, 2, TILES], I32), ph.sb("parts", [P, 2, 2, TILES], I32)
        zero, zrow = ph.sb("zero", [P, 512], BF16), ph.sb("zrow", [P, 8 * D])
        hi, lo = ph.sb("hi", [P, 2, 2, SLOTS, LO], BF16), ph.sb("lo", [P, 2, 2, SLOTS, LO], BF16)
        incl, rowsum = ph.sb("incl", [P, 2, 2, LO]), ph.sb("rowsum", [P, 2, 2])
        psC, psB = [ph.ps(f"psC{k}", [P, 2, LO]) for k in range(2)], ph.ps("psB", [P, 512])
        loaded, cleared, zeroed, vec, based = (ph.sem(n) for n in ("loaded", "cleared", "zeroed", "vec", "based"))
        s_hot, s_cnt = ph.step("hot", "cnt")
        block = new_block(nc, c, ph.all)

        @block.sync
        def _(sp):
            ph.start(sp)
            loads = ((ints[:, 0, :], a["src_col"]), (ints[:, 1, :], a["dst_col"]), (s["rec"][:, :, 2:4], a["rec_col"]),
                     (s["iota"][:, :], a["iota"]), (s["iotap"][:, :], a["iotap"]), (s["tri"][:, :, :], a["tri"]))
            for dst, src in loads:
                sp.dma_start(dst, src).then_inc(loaded, 16)
            sp.wait_ge(zeroed, 1)
            for table in (t["by_dst"], t["by_src"]):
                sp.dma_start(table[EPAD:SROWS, :], a["sentinel"]).then_inc(cleared, 16)
            with sp.Fori(0, NPAD // (8 * P)) as i:
                for table in (t["sum_dst"], t["sum_src"]):
                    sp.dma_start(table[bass.ds(i * 8 * P, 8 * P), :].rearrange("(p j) d -> p (j d)", p=P),
                                 zrow[:, :]).then_inc(cleared, 16)
            sp.wait_ge(cleared, 2 * 16 * (NPAD // (8 * P) + 1))

        @block.vector
        def _(dve):
            nc.vector.memset(zrow[:, :], 0.0)
            nc.vector.memset(zero[:, :], 0.0).then_inc(zeroed, 1)
            dve.wait_ge(loaded, 16 * 6)
            nc.vector.tensor_copy(s["iotab"][:, :], s["iota"][:, :])
            for k in range(2):
                nc.vector.tensor_copy(s["rec"][:, :, k], ints[:, k, :])
                nc.vector.tensor_copy(s["key"][:, k, 0, :], ints[:, k, :])
                nc.vector.tensor_scalar(parts[:, k, 0, :], ints[:, k, :], 8, None, ALU.logical_shift_right)
                last = nc.vector.tensor_scalar(parts[:, k, 1, :], ints[:, k, :], LO - 1, None, ALU.bitwise_and)
            last.then_inc(vec, 1)
            dve.wait_ge(vec, 1)
            nc.vector.tensor_copy(s["key"][:, :, 1:3, :], parts[:, :, :, :]).then_inc(vec, 1)
            dve.wait_ge(vec, 2)

            def hots(g, q, b):
                done(dve, s_cnt, g, 2)
                for k in range(2):
                    for j in range(SLOTS):
                        last = one_hots(nc, s, k, g * SLOTS + j, hi[:, b, k, j, :], lo[:, b, k, j, :])
                last.then_inc(s_hot, 1)
            pipelined(dve, [(hots, 0)], STEPS, 2)
            done(dve, s_cnt, STEPS - 1)
            for k in range(2):
                for half in range(2):
                    nc.vector.tensor_tensor_scan(incl[:, k, half, :], zero[:, 0:LO], psC[k][:, half, :], 0.0, ALU.add, ALU.add)
                last = nc.vector.tensor_reduce(rowsum[:, k, :], psC[k][:, :, :], mybir.AxisListType.X, ALU.add)
            last.then_inc(vec, 1)
            dve.wait_ge(vec, 3)
            for k in range(2):
                last = nc.vector.tensor_tensor(incl[:, k], incl[:, k], psC[k][:, :, :], ALU.subtract)
            last.then_inc(vec, 1)
            dve.wait_ge(vec, 4)
            dve.wait_ge(based, 1)
            for k in range(2):
                for half in range(2):
                    last = nc.vector.tensor_scalar(s["start"][:, k, half, :], incl[:, k, half, :],
                                                   psB[:, 2 * k + half:2 * k + half + 1], None, ALU.add)
            last.then_inc(vec, 1)
            dve.wait_ge(vec, 5)

        @block.tensor
        def _(pe):
            pe.wait_ge(zeroed, 1)
            for k in range(2):
                nc.tensor.matmul(psC[k][:, :, :], zero[:, 0:P], zero[:, :], start=True, stop=True)

            def count(g, q, b):
                done(pe, s_hot, g)
                for k in range(2):
                    for j in range(SLOTS):
                        last = count_tile(nc, psC[k], hi[:, b, k, j, :], lo[:, b, k, j, :])
                last.then_inc(s_cnt, 1)
            pipelined(pe, [(count, 0)], STEPS, 2)
            pe.wait_ge(vec, 3)
            for k in range(2):
                nc.tensor.matmul(psB[:, 2 * k:2 * k + 2], s["tri"][:, 1, :], rowsum[:, k, :], start=True, stop=True)
                last = nc.tensor.matmul(psB[:, 2 * k + 1:2 * k + 2], s["tri"][:, 2, :], rowsum[:, k, 0:1], start=False, stop=True,
                                        skip_group_check=True)
            last.then_inc(based, 1)


def one_hots(nc, s, k, tile, hi, lo):
    nc.vector.tensor_scalar(hi, s["iotab"][:, :], s["key"][:, k, 1, bass.ds(tile, 1)], None, ALU.is_equal)
    return nc.vector.tensor_scalar(lo, s["iotab"][:, :], s["key"][:, k, 2, bass.ds(tile, 1)], None, ALU.is_equal)


def count_tile(nc, table, hi, lo):
    for half in range(2):
        last = nc.tensor.matmul(table[:, half, :], hi[:, half * P:(half + 1) * P], lo, start=False, stop=True,
                                skip_group_check=True)
    return last


class Places:

    def __init__(self, ph, w, a, s, k, table):
        self.ph, self.nc, self.w, self.s, self.k, self.table = ph, ph.nc, w, s, k, table
        self.row = a[("src_row", "dst_row")[k]]
        self.krow, self.hrow = ph.sb("krow", [P, 4, PAIR * P], I32), ph.sb("hrow", [P, 2, PAIR * P], I32)
        self.hot_t = ph.sb("hot_t", [P, 2, 2, PAIR * P])
        self.hi, self.lo = ph.sb("hi", [P, 2, PAIR, LO], BF16), ph.sb("lo", [P, 2, PAIR, LO], BF16)
        self.count = ph.sb("count", [P, PAIR, 2, LO])
        self.scr, self.scr2 = ph.sb("scr", [P, 2, PAIR, P], BF16), ph.sb("scr2", [P, 2, PAIR, LO], BF16)
        self.before, self.earlier = ph.sb("before", [P, 4, PAIR]), ph.sb("earlier", [P, 4, PAIR])
        self.place, self.rec = ph.sb("place", [P, 4, PAIR], I32), ph.sb("prec", [P, 4, PAIR, 4])
        self.psC, self.psL = ph.ps("psC", [P, 2, LO]), ph.ps("psL", [P, PAIR, 512])
        self.rows, self.scattered, self.own = ph.sems("rows", 4), ph.dma(w, 4), ph.sem("place_own")
        self.seeded = ph.sem("seeded")
        self.s_hot, self.s_copy, self.s_count, self.s_look, self.s_pick, self.s_place = ph.step(
            "hot", "copy", "count", "look", "pick", "place")

    def load(self, sp):
        def stage(g, q, m):
            done(sp, self.s_hot, g, 4)
            self.ph.apart(sp)
            sp.dma_start(self.krow[:, m], self.row[:, bass.ds(g * PAIR * P, PAIR * P)].to_broadcast([P, PAIR * P])).then_inc(self.rows[m], 16)
        return stage

    def hots(self, dve):
        nc, s, k, tally = self.nc, self.s, self.k, Tally(dve, self.own, 1)

        def stage(g, q, m):
            b = m % 2
            dve.wait_ge(self.rows[m], q * 16 + 16)
            done(dve, self.s_hot, g, 1)
            done(dve, self.s_count, g * PAIR, 3)
            tally.begin(g)
            tally.inc(nc.vector.tensor_scalar(self.hrow[:, b], self.krow[:, m], 8, None, ALU.logical_shift_right))
            for j in range(PAIR):
                one_hots(nc, s, k, g * PAIR + j, self.hi[:, b, j, :], self.lo[:, b, j, :])
            tally.wait()
            done(dve, self.s_look, g * PAIR, 3)
            for half in range(2):
                nc.vector.tensor_scalar(self.hot_t[:, b, half, :], self.hrow[:, b], s["iotap"][:, half:half + 1], None, ALU.is_equal)
            done(dve, self.s_place, g, 2)
            for j in range(PAIR):
                last = nc.vector.scalar_tensor_tensor(self.scr[:, b, j, :], self.krow[:, m, j * P:(j + 1) * P],
                                                      s["key"][:, k, 0, bass.ds(g * PAIR + j, 1)], s["tri"][:, 0, :],
                                                      ALU.is_equal, ALU.mult, accum_out=self.before[:, m, j:j + 1])
            last.then_inc(self.s_hot, 1)
            tally.end()
        return stage

    def picks(self, dve):
        nc, s, k = self.nc, self.s, self.k

        def stage(g, q, m):
            b = m % 2
            done(dve, self.s_place, g, 1)
            for j in range(PAIR):
                done(dve, self.s_look, g * PAIR + j)
                nc.vector.scalar_tensor_tensor(self.scr2[:, b, j, :], s["iota"][:, :], s["key"][:, k, 2, bass.ds(g * PAIR + j, 1)],
                                               self.psL[:, j, 0:LO], ALU.is_equal, ALU.mult,
                                               accum_out=self.earlier[:, m, j:j + 1]).then_inc(self.s_pick, 1)
            done(dve, self.s_pick, g * PAIR + PAIR - 1)
            reused(dve, self.scattered[m], q * 16 * PAIR)
            nc.vector.tensor_tensor(self.place[:, m], self.before[:, m], self.earlier[:, m], ALU.add)
            nc.vector.tensor_copy(self.rec[:, m], s["rec"][:, bass.ds(g * PAIR, PAIR), :]).then_inc(self.s_place, 1)
        return stage

    def copies(self, act, j):
        def stage(g, q, m):
            done(act, self.s_count, g * PAIR + j, 1)
            done(act, self.s_look, g * PAIR + j, 2)
            self.nc.scalar.activation(self.count[:, j], self.psC[:, :, :], ACT.Copy).then_inc(self.s_copy, 1)
        return stage

    def seed(self, pe):
        self.nc.tensor.matmul(self.psC[:, :, :], self.w["ident"][:, :], self.s["start"][:, self.k], start=True,
                              stop=True).then_inc(self.seeded, 1)

    def lookups(self, pe, j):
        nc = self.nc

        def stage(g, q, m):
            b = m % 2
            done(pe, self.s_hot, g)
            done(pe, self.s_copy, g * PAIR + j)
            count_tile(nc, self.psC, self.hi[:, b, j, :], self.lo[:, b, j, :]).then_inc(self.s_count, 1)
            done(pe, self.s_pick, g * PAIR + j, 2)
            for half in range(2):
                last = nc.tensor.matmul(self.psL[:, j, 0:LO], self.hot_t[:, b, half, j * P:(j + 1) * P],
                                        self.count[:, j, half, :], start=(half == 0), stop=(half == 1))
            last.then_inc(self.s_look, 1)
        return stage

    def scatter(self, pool, limit):
        def stage(g, q, m):
            done(pool, self.s_place, g)
            self.ph.apart(pool)
            for j in range(PAIR):
                self.nc.gpsimd.indirect_dma_start(self.table, bass.IndirectOffsetOnAxis(ap=self.place[:, m, j:j + 1], axis=0),
                                                  self.rec[:, m, j, :], None, bounds_check=limit,
                                                  oob_is_err=True).then_inc(self.scattered[m], 16)
        return stage

    def end(self, pool):
        for m in range(4):
            pool.wait_ge(self.scattered[m], 16 * PAIR * ((NBLK + 3 - m) // 4))


class Permute:

    def __init__(self, ph, w, order, field, table, out):
        self.ph, self.nc, self.order, self.field, self.table, self.out = ph, ph.nc, order, field, table, out
        self.recs, self.index = ph.sb("recs", [P, 4, PAIR, 4]), ph.sb("pindex", [P, 4, PAIR], I32)
        self.rows = ph.sb("prows", [P, 4, PAIR, D])
        self.listed, self.fetched, self.kept = ph.sems("listed", 4), ph.dma(w, 4), ph.sems("kept", 4)
        (self.s_index,) = ph.step("pindex")

    def load(self, sp):
        def stage(g, q, m):
            done(sp, self.s_index, g, 4)
            self.ph.apart(sp)
            sp.dma_start(self.recs[:, m], self.order[bass.ds(g * PAIR * P, PAIR * P), :].rearrange("(j p) f -> p j f", p=P)).then_inc(self.listed[m], 16)
        return stage

    def indices(self, dve):
        def stage(g, q, m):
            dve.wait_ge(self.listed[m], q * 16 + 16)
            reused(dve, self.fetched[m], q * 16 * PAIR)
            self.nc.vector.tensor_copy(self.index[:, m], self.recs[:, m, :, self.field]).then_inc(self.s_index, 1)
        return stage

    def gather(self, pool, limit):
        def stage(g, q, m):
            done(pool, self.s_index, g)
            reused(pool, self.kept[m], q * 16)
            self.ph.apart(pool)
            for j in range(PAIR):
                self.nc.gpsimd.indirect_dma_start(self.rows[:, m, j, :], None, self.table,
                                                  bass.IndirectOffsetOnAxis(ap=self.index[:, m, j:j + 1], axis=0),
                                                  bounds_check=limit, oob_is_err=True).then_inc(self.fetched[m], 16)
        return stage

    def store(self, sp):
        def stage(g, q, m):
            sp.wait_ge(self.fetched[m], (q + 1) * 16 * PAIR)
            self.ph.apart(sp)
            sp.dma_start(self.out[bass.ds(g * PAIR * P, PAIR * P), :].rearrange("(j p) d -> p j d", p=P), self.rows[:, m]).then_inc(self.kept[m], 16)
        return stage

    def end(self, sp, pool=None):
        for m in range(4):
            sp.wait_ge(self.kept[m], 16 * ((NBLK + 3 - m) // 4))

    def end_pool(self, pool):
        for m in range(4):
            pool.wait_ge(self.fetched[m], 16 * PAIR * ((NBLK + 3 - m) // 4))


def attention_inputs(nc, a, w, t, s):
    with ExitStack() as c:
        ph = Phase(nc, c, "A")
        x, st, mv, sd = ph.sb("x", [P, 4, SLOTS, D]), ph.sb("st", [P, 2, SLOTS, 6]), ph.sb("mv", [P, 2, SLOTS, 2]), ph.sb("sd", [P, 2, SLOTS])
        rs, nm = ph.sb("rs", [P, 2, SLOTS]), ph.sb("nm", [P, 2, SLOTS])
        h, hT, o = ph.sb("h", [P, 2, SLOTS, D]), ph.sb("hT", [P, 2, BLK]), ph.sb("o", [P, 4, SLOTS, AW])
        psT, psO = ph.ps("psT", [P, BLK]), ph.ps("psO", [P, 2, SLOTS, LO])
        loaded, stored = ph.sems("loaded", 4), ph.sems("stored", 4)
        s_stat, s_sd, s_rs, s_h, s_tr, s_hT, s_mm, s_o = ph.step("stat", "sd", "rs", "h", "tr", "hT", "mm", "o")
        ch1, ch2 = ph.sems("ch", 2)
        pl = Places(ph, w, a, s, 1, t["by_dst"])
        block = new_block(nc, c, ph.all)

        @block.sync
        def _(sp):
            ph.start(sp)

            def load(g, q, m):
                done(sp, s_h, g, 4)
                sp.dma_start(x[:, m], blocks4(a["x"], g * BLK)).then_inc(loaded[m], 16)

            def store(g, q, m):
                b = m % 2
                done(sp, s_o, g)
                sp.dma_start(blocks4(t["att"], g * BLK), o[:, m]).then_inc(stored[m], 16)
                sp.dma_start(blocks4(t["gat"], g * BLK), o[:, m, :, 0:D]).then_inc(stored[m], 16)
            pipelined(sp, [(load, 0), (pl.load(sp), 0), (store, 4)], NBLK, 4)
            for m in range(4):
                sp.wait_ge(stored[m], 32 * ((NBLK + 3 - m) // 4))

        @block.gpsimd
        def _(pool):
            limit = pool.to_reg(SROWS - 1)
            pipelined(pool, [(pl.scatter(pool, limit), 4)], NBLK, 4)
            pl.end(pool)

        @block.vector
        def _(dve):
            c1, c2 = Tally(dve, ch1, 1), Tally(dve, ch2, 1)

            def stats(g, q, m):
                b = m % 2
                dve.wait_ge(loaded[m], q * 16 + 16)
                done(dve, s_rs, g, 2)
                done(dve, s_sd, g, 2)
                c1.begin(g)
                stats4(ph, c1, x[:, m], st[:, b], mv[:, b]).then_inc(s_stat, 1)
                c1.end()

            def scale(g, q, m):
                b = m % 2
                done(dve, s_sd, g)
                done(dve, s_h, g, 2)
                c2.begin(g)
                c2.inc(nc.vector.reciprocal(rs[:, b, :], sd[:, b, :]))
                c2.wait()
                nc.vector.scalar_tensor_tensor(nm[:, b, :], mv[:, b, :, 0], -1.0, rs[:, b, :], ALU.mult, ALU.mult).then_inc(s_rs, 1)
                c2.end()

            def evacuate(g, q, m):
                b = m % 2
                done(dve, s_mm, g)
                reused(dve, stored[m], q * 32)
                nc.vector.tensor_copy(o[:, m], psO[:, b, :, 0:AW]).then_inc(s_o, 1)
            pipelined(dve, [(pl.picks(dve), 3), (evacuate, 3), (scale, 1), (stats, 0), (pl.hots(dve), 1)], NBLK, 4)

        @block.scalar
        def _(act):
            def deviation(g, q, m):
                b = m % 2
                done(act, s_stat, g)
                done(act, s_rs, g, 2)
                nc.scalar.activation(sd[:, b, :], mv[:, b, :, 1], ACT.Sqrt, bias=w["eps"][:, :]).then_inc(s_sd, 1)

            def relu(g, q, m):
                b = m % 2
                done(act, s_rs, g)
                done(act, s_tr, g, 2)
                normalise4(nc, h[:, b], x[:, m], lambda j: rs[:, b, j:j + 1], lambda j: nm[:, b, j:j + 1], ACT.Relu).then_inc(s_h, 1)

            def evacuate(g, q, m):
                b = m % 2
                done(act, s_tr, g)
                done(act, s_mm, g, 2)
                nc.scalar.activation(hT[:, b], psT[:, :], ACT.Copy).then_inc(s_hT, 1)
            act.wait_ge(pl.seeded, 1)
            pipelined(act, [(pl.copies(act, 0), 2), (evacuate, 2), (pl.copies(act, 1), 2), (relu, 1), (deviation, 0)], NBLK, 4)

        @block.tensor
        def _(pe):
            def turn(g, q, m):
                b = m % 2
                done(pe, s_h, g)
                done(pe, s_hT, g, 1)
                transposes4(nc, psT[:, :], h[:, b], w["ident"]).then_inc(s_tr, 1)

            def project(g, q, m):
                b = m % 2
                done(pe, s_hT, g)
                done(pe, s_o, g, 2)
                for j in range(SLOTS):
                    last = nc.tensor.matmul(psO[:, b, j, 0:AW], hT[:, b, j * P:(j + 1) * P], w["wl"][:, :], start=True, stop=True)
                last.then_inc(s_mm, 1)
            pl.seed(pe)
            pipelined(pe, [(pl.lookups(pe, 0), 2), (project, 2), (pl.lookups(pe, 1), 2), (turn, 1)], NBLK, 4)


def attention_outputs(nc, a, w, t, s):
    with ExitStack() as c:
        ph = Phase(nc, c, "B")
        x, ga, xb = ph.sb("x", [P, 4, SLOTS, D]), ph.sb("ga", [P, 4, SLOTS, D]), ph.sb("xb", [P, 2, SLOTS, D])
        gT, o, y, xo = ph.sb("gT", [P, 2, BLK]), ph.sb("o", [P, 2, SLOTS, D]), ph.sb("y", [P, 2, SLOTS, D]), ph.sb("xo", [P, 4, SLOTS, XW])
        st, mv, sd = ph.sb("st", [P, 2, 2, SLOTS, 6]), ph.sb("mv", [P, 2, 2, SLOTS, 2]), ph.sb("sd", [P, 2, 2, SLOTS])
        rs, nm = ph.sb("rs", [P, 2, SLOTS]), ph.sb("nm", [P, 2, SLOTS])
        psT, psO = ph.ps("psT", [P, 2, BLK]), ph.ps("psO", [P, 2, BLK])
        loaded, stored = ph.sems("loaded", 4), ph.sems("stored", 4)
        s_xb, s_tr, s_gT, s_mm, s_st1, s_sd1, s_rs1, s_y, s_st2, s_sd2, s_xo = ph.step(
            "xb", "tr", "gT", "mm", "st1", "sd1", "rs1", "y", "st2", "sd2", "xo")
        ch1, ch2, ch3, ch4 = ph.sems("ch", 4)
        pl = Places(ph, w, a, s, 0, t["by_src"])
        pm = Permute(ph, w, t["by_dst"], 2, a["edge_attr"], t["edge_attr"])
        block = new_block(nc, c, ph.all)

        @block.sync
        def _(sp):
            ph.start(sp)

            def load(g, q, m):
                done(sp, s_xb, g, 4)
                done(sp, s_tr, g, 4)
                sp.dma_start(ga[:, m], blocks4(t["gat"], g * BLK)).then_inc(loaded[m], 16)
                sp.dma_start(x[:, m], blocks4(a["x"], g * BLK)).then_inc(loaded[m], 16)

            def store(g, q, m):
                b = m % 2
                done(sp, s_xo, g)
                sp.dma_start(blocks4(t["x1"], g * BLK), xo[:, m]).then_inc(stored[m], 16)
            pipelined(sp, [(load, 0), (pl.load(sp), 0), (pm.load(sp), 0), (pm.store(sp), 4), (store, 6)], NBLK, 4)
            pm.end(sp)
            for m in range(4):
                sp.wait_ge(stored[m], 16 * ((NBLK + 3 - m) // 4))

        @block.gpsimd
        def _(pool):
            def shift(g, q, m):
                b = m % 2
                pool.wait_ge(loaded[m], q * 32 + 32)
                done(pool, s_st2, g, 2)
                nc.gpsimd.tensor_tensor(xb[:, b], x[:, m], w["be0"][:, :].unsqueeze(1).to_broadcast([P, SLOTS, D]), ALU.add).then_inc(s_xb, 1)

            limit, last = pool.to_reg(SROWS - 1), pool.to_reg(E - 1)
            pipelined(pool, [(pl.scatter(pool, limit), 4), (pm.gather(pool, last), 2), (shift, 3)], NBLK, 4)
            pl.end(pool)
            pm.end_pool(pool)

        @block.vector
        def _(dve):
            c1, c2, c3, c4 = Tally(dve, ch1, 2), Tally(dve, ch2, 1), Tally(dve, ch3, 3), Tally(dve, ch4, 1)

            def first(g, q, m):
                b = m % 2
                done(dve, s_mm, g)
                done(dve, s_y, g, 2)
                done(dve, s_rs1, g, 2)
                c1.begin(g)
                c1.inc(nc.vector.tensor_tensor(o[:, b], psO[:, b].rearrange("p (j d) -> p j d", j=SLOTS),
                                        w["c0"][:, :].unsqueeze(1).to_broadcast([P, SLOTS, D]), ALU.add))
                c1.wait()
                stats4(ph, c1, o[:, b], st[:, 0, b], mv[:, 0, b]).then_inc(s_st1, 1)
                c1.end()

            def scale(g, q, m):
                b = m % 2
                done(dve, s_sd1, g)
                c2.begin(g)
                c2.inc(nc.vector.reciprocal(rs[:, b, :], sd[:, 0, b, :]))
                c2.wait()
                nc.vector.scalar_tensor_tensor(nm[:, b, :], mv[:, 0, b, :, 0], -1.0, rs[:, b, :], ALU.mult, ALU.mult).then_inc(s_rs1, 1)
                c2.end()

            def second(g, q, m):
                b = m % 2
                done(dve, s_y, g)
                done(dve, s_xb, g)
                reused(dve, stored[m], q * 16)
                c3.begin(g)
                c3.inc(nc.vector.tensor_tensor(y[:, b], y[:, b], w["g0"][:, :].unsqueeze(1).to_broadcast([P, SLOTS, D]), ALU.mult))
                c3.wait()
                c3.inc(nc.vector.tensor_tensor(xo[:, m, :, 0:D], y[:, b], xb[:, b], ALU.add))
                c3.wait()
                stats4(ph, c3, xo[:, m], st[:, 1, b], mv[:, 1, b]).then_inc(s_st2, 1)
                c3.end()

            def finish(g, q, m):
                b = m % 2
                done(dve, s_sd2, g)
                c4.begin(g)
                c4.inc(nc.vector.reciprocal(xo[:, m, :, D:D + 1], sd[:, 1, b, :].unsqueeze(2)))
                c4.wait()
                nc.vector.scalar_tensor_tensor(xo[:, m, :, D + 1:XW], mv[:, 1, b, :, 0:1], -1.0, xo[:, m, :, D:D + 1], ALU.mult, ALU.mult).then_inc(s_xo, 1)
                c4.end()
            pipelined(dve, [(pm.indices(dve), 1), (pl.picks(dve), 3), (finish, 5), (second, 4), (scale, 3), (pl.hots(dve), 1), (first, 2)], NBLK, 4)

        @block.scalar
        def _(act):
            def evacuate(g, q, m):
                b = m % 2
                done(act, s_tr, g)
                done(act, s_mm, g, 2)
                nc.scalar.activation(gT[:, b], psT[:, b], ACT.Copy).then_inc(s_gT, 1)

            def deviation1(g, q, m):
                b = m % 2
                done(act, s_st1, g)
                nc.scalar.activation(sd[:, 0, b, :], mv[:, 0, b, :, 1], ACT.Sqrt, bias=w["eps"][:, :]).then_inc(s_sd1, 1)

            def normalise(g, q, m):
                b = m % 2
                done(act, s_rs1, g)
                done(act, s_st2, g, 2)
                normalise4(nc, y[:, b], o[:, b], lambda j: rs[:, b, j:j + 1], lambda j: nm[:, b, j:j + 1], ACT.Identity).then_inc(s_y, 1)

            def deviation2(g, q, m):
                b = m % 2
                done(act, s_st2, g)
                nc.scalar.activation(sd[:, 1, b, :], mv[:, 1, b, :, 1], ACT.Sqrt, bias=w["eps"][:, :]).then_inc(s_sd2, 1)
            act.wait_ge(pl.seeded, 1)
            pipelined(act, [(pl.copies(act, 0), 2), (evacuate, 1), (pl.copies(act, 1), 2), (deviation2, 4), (normalise, 3), (deviation1, 2)], NBLK, 4)

        @block.tensor
        def _(pe):
            def turn(g, q, m):
                b = m % 2
                pe.wait_ge(loaded[m], q * 32 + 32)
                done(pe, s_gT, g, 2)
                transposes4(nc, psT[:, b], ga[:, m], w["ident"]).then_inc(s_tr, 1)

            def project(g, q, m):
                b = m % 2
                done(pe, s_gT, g)
                done(pe, s_st1, g, 2)
                for j in range(SLOTS):
                    last = nc.tensor.matmul(psO[:, b, j * P:(j + 1) * P], gT[:, b, j * P:(j + 1) * P], w["proj"][:, :], start=True, stop=True)
                last.then_inc(s_mm, 1)
            pl.seed(pe)
            pipelined(pe, [(turn, 0), (pl.lookups(pe, 0), 2), (project, 1), (pl.lookups(pe, 1), 2)], NBLK, 4)


def mlp(nc, a, w, t):
    with ExitStack() as c:
        ph = Phase(nc, c, "C")
        x, ag, xb = ph.sb("x", [P, 4, SLOTS, XW]), ph.sb("ag", [P, 4, SLOTS, D]), ph.sb("xb", [P, 2, SLOTS, D])
        h, hh, hT, r, xo = ph.sb("h", [P, 2, SLOTS, D]), ph.sb("hh", [P, 2, SLOTS, D]), ph.sb("hT", [P, 2, BLK]), ph.sb("r", [P, 2, 4, BLK]), ph.sb("xo", [P, 4, SLOTS, XW])
        st, mv, sd = ph.sb("st", [P, 2, SLOTS, 6]), ph.sb("mv", [P, 2, SLOTS, 2]), ph.sb("sd", [P, 2, SLOTS])
        psT, psH, psO = ph.ps("psT", [P, 2, BLK]), ph.ps("psH", [P, 4, BLK]), ph.ps("psO", [P, 2, BLK])
        loaded, stored = ph.sems("loaded", 4), ph.sems("stored", 4)
        s_xb, s_h, s_hh, s_tr, s_hT, s_up, s_ra, s_rv, s_mm, s_st, s_sd, s_xo = ph.step(
            "xb", "h", "hh", "tr", "hT", "up", "ra", "rv", "mm", "st", "sd", "xo")
        up2 = ph.sem("up2")
        ch1, ch2 = ph.sems("ch", 2)
        pm = Permute(ph, w, t["by_src"], 1, a["factors"], t["factors"])
        block = new_block(nc, c, ph.all)

        @block.sync
        def _(sp):
            ph.start(sp)

            def load(g, q, m):
                done(sp, s_xb, g, 4)
                done(sp, s_h, g, 4)
                done(sp, s_hh, g, 4)
                sp.dma_start(x[:, m], blocks4(t["x1"], g * BLK)).then_inc(loaded[m], 16)
                sp.dma_start(ag[:, m], blocks4(t["sum_dst"], g * BLK)).then_inc(loaded[m], 16)

            def store(g, q, m):
                b = m % 2
                done(sp, s_xo, g)
                sp.dma_start(blocks4(t["x2"], g * BLK), xo[:, m]).then_inc(stored[m], 16)
            pipelined(sp, [(load, 0), (pm.load(sp), 0), (pm.store(sp), 4), (store, 6)], NBLK, 4)
            pm.end(sp)
            for m in range(4):
                sp.wait_ge(stored[m], 16 * ((NBLK + 3 - m) // 4))

        @block.gpsimd
        def _(pool):
            def shift(g, q, m):
                b = m % 2
                pool.wait_ge(loaded[m], q * 32 + 32)
                done(pool, s_st, g, 2)
                nc.gpsimd.tensor_tensor(xb[:, b], x[:, m, :, 0:D], w["b2"][:, :].unsqueeze(1).to_broadcast([P, SLOTS, D]), ALU.add).then_inc(s_xb, 1)

            last = pool.to_reg(NPAD - 1)
            pipelined(pool, [(pm.gather(pool, last), 2), (shift, 3)], NBLK, 4)
            pm.end_pool(pool)

        @block.vector
        def _(dve):
            c1, c2 = Tally(dve, ch1, 2), Tally(dve, ch2, 1)

            def combine(g, q, m):
                b = m % 2
                done(dve, s_h, g)
                done(dve, s_tr, g, 2)
                nc.vector.scalar_tensor_tensor(hh[:, b], h[:, b], w["eps1"][:, :], ag[:, m], ALU.mult, ALU.add).then_inc(s_hh, 1)

            def evacuate(g, q, m):
                b = m % 2
                done(dve, s_tr, g)
                done(dve, s_up, g, 2)
                nc.vector.tensor_copy(hT[:, b], psT[:, b]).then_inc(s_hT, 1)

            def relu(g, q, m):
                b = m % 2
                done(dve, s_up, g)
                done(dve, s_mm, g, 2)
                for k in (2, 3):
                    last = nc.vector.tensor_scalar(r[:, b, k], psH[:, k], w["b1"][:, k:k + 1], 0.0, ALU.add, ALU.max)
                last.then_inc(s_rv, 1)

            def add(g, q, m):
                b = m % 2
                done(dve, s_mm, g)
                done(dve, s_xb, g)
                done(dve, s_sd, g, 2)
                reused(dve, stored[m], q * 16)
                c1.begin(g)
                c1.inc(nc.vector.tensor_tensor(xo[:, m, :, 0:D], psO[:, b].rearrange("p (j d) -> p j d", j=SLOTS), xb[:, b], ALU.add))
                c1.wait()
                stats4(ph, c1, xo[:, m], st[:, b], mv[:, b]).then_inc(s_st, 1)
                c1.end()

            def finish(g, q, m):
                b = m % 2
                done(dve, s_sd, g)
                c2.begin(g)
                c2.inc(nc.vector.reciprocal(xo[:, m, :, D:D + 1], sd[:, b, :].unsqueeze(2)))
                c2.wait()
                nc.vector.scalar_tensor_tensor(xo[:, m, :, D + 1:XW], mv[:, b, :, 0:1], -1.0, xo[:, m, :, D:D + 1], ALU.mult, ALU.mult).then_inc(s_xo, 1)
                c2.end()
            pipelined(dve, [(pm.indices(dve), 1), (evacuate, 2), (finish, 5), (add, 4), (combine, 1), (relu, 2)], NBLK, 4)

        @block.scalar
        def _(act):
            def node(g, q, m):
                b = m % 2
                act.wait_ge(loaded[m], q * 32 + 32)
                done(act, s_hh, g, 2)
                normalise4(nc, h[:, b], x[:, m], lambda j: x[:, m, j, D:D + 1], lambda j: x[:, m, j, D + 1:XW], ACT.Relu).then_inc(s_h, 1)

            def relu(g, q, m):
                b = m % 2
                act.wait_ge(up2, g + 1)
                done(act, s_mm, g, 2)
                for k in (0, 1):
                    last = nc.scalar.activation(r[:, b, k], psH[:, k], ACT.Relu, bias=w["b1"][:, k:k + 1])
                last.then_inc(s_ra, 1)

            def deviation(g, q, m):
                b = m % 2
                done(act, s_st, g)
                done(act, s_xo, g, 2)
                nc.scalar.activation(sd[:, b, :], mv[:, b, :, 1], ACT.Sqrt, bias=w["eps"][:, :]).then_inc(s_sd, 1)
            pipelined(act, [(node, 0), (deviation, 4), (relu, 2)], NBLK, 4)

        @block.tensor
        def _(pe):
            def turn(g, q, m):
                b = m % 2
                done(pe, s_hh, g)
                done(pe, s_hT, g, 2)
                transposes4(nc, psT[:, b], hh[:, b], w["ident"]).then_inc(s_tr, 1)

            def up(g, q, m):
                b = m % 2
                done(pe, s_hT, g)
                done(pe, s_ra, g, 1)
                for k in (0, 1):
                    last = nc.tensor.matmul(psH[:, k], w["w1"][:, k * P:(k + 1) * P], hT[:, b], start=True, stop=True)
                last.then_inc(up2, 1)
                done(pe, s_rv, g, 1)
                for k in (2, 3):
                    last = nc.tensor.matmul(psH[:, k], w["w1"][:, k * P:(k + 1) * P], hT[:, b], start=True, stop=True)
                last.then_inc(s_up, 1)

            def down(g, q, m):
                b = m % 2
                done(pe, s_ra, g)
                done(pe, s_rv, g)
                done(pe, s_st, g, 2)
                for j in range(SLOTS):
                    for k in range(4):
                        last = nc.tensor.matmul(psO[:, b, j * P:(j + 1) * P], r[:, b, k, j * P:(j + 1) * P], w["w2"][:, k, :],
                                                start=(k == 0), stop=(k == 3))
                last.then_inc(s_mm, 1)
            pipelined(pe, [(up, 2), (down, 3), (turn, 1)], NBLK, 4)


def factor_update(nc, a, w, t):
    with ExitStack() as c:
        ph = Phase(nc, c, "D")
        x, ag, xh = ph.sb("x", [P, 4, SLOTS, XW]), ph.sb("ag", [P, 4, SLOTS, D]), ph.sb("xh", [P, 4, SLOTS, D])
        h, hT, aT, o, xo = ph.sb("h", [P, 2, SLOTS, D]), ph.sb("hT", [P, 2, BLK]), ph.sb("aT", [P, 2, BLK]), ph.sb("o", [P, 2, SLOTS, D]), ph.sb("xo", [P, 4, SLOTS, XW])
        st, mv, sd = ph.sb("st", [P, 2, SLOTS, 6]), ph.sb("mv", [P, 2, SLOTS, 2]), ph.sb("sd", [P, 2, SLOTS])
        psT, psA, psO = ph.ps("psT", [P, 2, BLK]), ph.ps("psA", [P, 2, BLK]), ph.ps("psO", [P, 2, BLK])
        loaded, stored = ph.sems("loaded", 4), ph.sems("stored", 4)
        s_h, s_xh, s_ta, s_th, s_aT, s_hT, s_mm, s_st, s_sd, s_xo = ph.step("h", "xh", "ta", "th", "aT", "hT", "mm", "st", "sd", "xo")
        ch1, ch2 = ph.sems("ch", 2)
        block = new_block(nc, c, ph.all)

        @block.sync
        def _(sp):
            ph.start(sp)

            def load(g, q, m):
                done(sp, s_xh, g, 4)
                done(sp, s_ta, g, 4)
                sp.dma_start(ag[:, m], blocks4(t["sum_src"], g * BLK)).then_inc(loaded[m], 16)
                sp.dma_start(x[:, m], blocks4(t["x2"], g * BLK)).then_inc(loaded[m], 16)

            def store(g, q, m):
                b = m % 2
                done(sp, s_xo, g)
                sp.dma_start(blocks4(t["x3"], g * BLK), xo[:, m]).then_inc(stored[m], 16)
            pipelined(sp, [(load, 0), (store, 5)], NBLK, 4)
            for m in range(4):
                sp.wait_ge(stored[m], 16 * ((NBLK + 3 - m) // 4))

        @block.gpsimd
        def _(pool):
            def add(g, q, m):
                b = m % 2
                done(pool, s_h, g)
                done(pool, s_st, g, 4)
                nc.gpsimd.tensor_tensor(xh[:, m], x[:, m, :, 0:D], h[:, b], ALU.add).then_inc(s_xh, 1)

            pipelined(pool, [(add, 1)], NBLK, 4)

        @block.vector
        def _(dve):
            c1, c2 = Tally(dve, ch1, 3), Tally(dve, ch2, 1)

            def evacuate(g, q, m):
                b = m % 2
                done(dve, s_ta, g)
                done(dve, s_mm, g, 2)
                nc.vector.tensor_copy(aT[:, b], psA[:, b]).then_inc(s_aT, 1)

            def add(g, q, m):
                b = m % 2
                done(dve, s_mm, g)
                done(dve, s_xh, g)
                done(dve, s_sd, g, 2)
                reused(dve, stored[m], q * 16)
                c1.begin(g)
                c1.inc(nc.vector.tensor_tensor(o[:, b], psO[:, b].rearrange("p (j d) -> p j d", j=SLOTS),
                                        w["bc"][:, :].unsqueeze(1).to_broadcast([P, SLOTS, D]), ALU.add))
                c1.wait()
                c1.inc(nc.vector.scalar_tensor_tensor(xo[:, m, :, 0:D], o[:, b], 0.0, xh[:, m], ALU.max, ALU.add))
                c1.wait()
                stats4(ph, c1, xo[:, m], st[:, b], mv[:, b]).then_inc(s_st, 1)
                c1.end()

            def finish(g, q, m):
                b = m % 2
                done(dve, s_sd, g)
                c2.begin(g)
                c2.inc(nc.vector.reciprocal(xo[:, m, :, D:D + 1], sd[:, b, :].unsqueeze(2)))
                c2.wait()
                nc.vector.scalar_tensor_tensor(xo[:, m, :, D + 1:XW], mv[:, b, :, 0:1], -1.0, xo[:, m, :, D:D + 1], ALU.mult, ALU.mult).then_inc(s_xo, 1)
                c2.end()
            pipelined(dve, [(finish, 4), (add, 3), (evacuate, 1)], NBLK, 4)

        @block.scalar
        def _(act):
            def node(g, q, m):
                b = m % 2
                act.wait_ge(loaded[m], q * 32 + 32)
                done(act, s_th, g, 2)
                done(act, s_xh, g, 2)
                normalise4(nc, h[:, b], x[:, m], lambda j: x[:, m, j, D:D + 1], lambda j: x[:, m, j, D + 1:XW], ACT.Relu).then_inc(s_h, 1)

            def evacuate(g, q, m):
                b = m % 2
                done(act, s_th, g)
                done(act, s_mm, g, 2)
                nc.scalar.activation(hT[:, b], psT[:, b], ACT.Copy).then_inc(s_hT, 1)

            def deviation(g, q, m):
                b = m % 2
                done(act, s_st, g)
                done(act, s_xo, g, 2)
                nc.scalar.activation(sd[:, b, :], mv[:, b, :, 1], ACT.Sqrt, bias=w["eps"][:, :]).then_inc(s_sd, 1)
            pipelined(act, [(evacuate, 2), (node, 0), (deviation, 3)], NBLK, 4)

        @block.tensor
        def _(pe):
            def turn_sums(g, q, m):
                b = m % 2
                pe.wait_ge(loaded[m], q * 32 + 32)
                done(pe, s_aT, g, 2)
                transposes4(nc, psA[:, b], ag[:, m], w["ident"]).then_inc(s_ta, 1)

            def turn(g, q, m):
                b = m % 2
                done(pe, s_h, g)
                done(pe, s_hT, g, 2)
                transposes4(nc, psT[:, b], h[:, b], w["ident"]).then_inc(s_th, 1)

            def combine(g, q, m):
                b = m % 2
                done(pe, s_hT, g)
                done(pe, s_aT, g)
                done(pe, s_st, g, 2)
                for j in range(SLOTS):
                    nc.tensor.matmul(psO[:, b, j * P:(j + 1) * P], hT[:, b, j * P:(j + 1) * P], w["wc"][:, 0, :], start=True, stop=False)
                    last = nc.tensor.matmul(psO[:, b, j * P:(j + 1) * P], aT[:, b, j * P:(j + 1) * P], w["wc"][:, 1, :], start=False, stop=True)
                last.then_inc(s_mm, 1)
            pipelined(pe, [(combine, 2), (turn, 1), (turn_sums, 0)], NBLK, 4)


def graph_output(nc, a, w, t, out):
    with ExitStack() as c:
        ph = Phase(nc, c, "E")
        x, ag, xb = ph.sb("x", [P, 4, SLOTS, D]), ph.sb("ag", [P, 4, SLOTS, D]), ph.sb("xb", [P, 2, SLOTS, D])
        aT, z, zm, e, rz = ph.sb("aT", [P, 2, BLK]), ph.sb("z", [P, 2, BLK]), ph.sb("zm", [P, 2, BLK]), ph.sb("e", [P, 2, BLK]), ph.sb("rz", [P, 2, BLK])
        u, y, xo = ph.sb("u", [P, 2, SLOTS, D]), ph.sb("y", [P, 2, SLOTS, D]), ph.sb("xo", [P, 4, SLOTS, D])
        st, mv, ve = ph.sb("st", [P, 2, SLOTS, 6]), ph.sb("mv", [P, 2, SLOTS, 2]), ph.sb("ve", [P, 2, SLOTS])
        rs, nm, half = ph.sb("rs", [P, 2, SLOTS]), ph.sb("nm", [P, 2, SLOTS]), ph.sb("half", [P, SLOTS])
        psT, psO = ph.ps("psT", [P, 2, BLK]), ph.ps("psO", [P, 2, BLK])
        loaded, loaded_x, stored = ph.sems("loaded", 4), ph.sems("loaded_x", 4), ph.sems("stored", 4)
        s_xb, s_tr, s_aT, s_mm, s_z, s_zm, s_e, s_st, s_ve, s_rs, s_nm, s_y, s_xo = ph.step(
            "xb", "tr", "aT", "mm", "z", "zm", "e", "st", "ve", "rs", "nm", "y", "xo")
        ch1, ch2 = ph.sems("ch", 2)
        s_half = ph.sem("half")
        block = new_block(nc, c, ph.all)

        @block.sync
        def _(sp):
            ph.start(sp)

            def load(g, q, m):
                done(sp, s_tr, g, 4)
                sp.dma_start(ag[:, m], blocks4(t["sum_src"], g * BLK)).then_inc(loaded[m], 16)

            def load_x(g, q, m):
                done(sp, s_xb, g, 4)
                sp.dma_start(x[:, m], blocks4(t["x3"], g * BLK)[:, :, 0:D]).then_inc(loaded_x[m], 16)

            def store(g, q, m):
                b = m % 2
                done(sp, s_xo, g)
                sp.dma_start(blocks4(out, g * BLK), xo[:, m]).then_inc(stored[m], 16)
            pipelined(sp, [(load, 0), (load_x, 3), (store, 7)], NBLK, 4)
            for m in range(4):
                sp.wait_ge(stored[m], 16 * ((NBLK + 3 - m) // 4))

        @block.gpsimd
        def _(pool):
            nc.gpsimd.memset(half[:, :], -0.5).then_inc(s_half, 1)
            pool.wait_ge(s_half, 1)

            def clip(g, q, m):
                b = m % 2
                done(pool, s_z, g)
                done(pool, s_e, g, 2)
                ph.apart(pool)
                nc.gpsimd.tensor_scalar(zm[:, b], z[:, b], 0.0, None, ALU.min).then_inc(s_zm, 1)

            def shift(g, q, m):
                b = m % 2
                pool.wait_ge(loaded_x[m], q * 16 + 16)
                done(pool, s_xo, g, 2)
                nc.gpsimd.tensor_tensor(xb[:, b], x[:, m], w["be3"][:, :].unsqueeze(1).to_broadcast([P, SLOTS, D]), ALU.add).then_inc(s_xb, 1)

            def power(g, q, m):
                b = m % 2
                done(pool, s_st, g)
                done(pool, s_rs, g, 2)
                ph.apart(pool)
                nc.gpsimd.tensor_scalar(ve[:, b, :], mv[:, b, :, 1], LN_EPS, None, ALU.add).then_inc(s_ve, 1)
                done(pool, s_ve, g)
                done(pool, s_nm, g, 2)
                done(pool, s_y, g, 2)
                nc.gpsimd.tensor_tensor(rs[:, b, :], ve[:, b, :], half[:, :], ALU.pow).then_inc(s_rs, 1)

            pipelined(pool, [(shift, 5), (power, 4), (clip, 2)], NBLK, 4)

        @block.vector
        def _(dve):
            c1, c2 = Tally(dve, ch1, 2), Tally(dve, ch2, 1)

            def bias(g, q, m):
                b = m % 2
                done(dve, s_mm, g)
                done(dve, s_zm, g, 2)
                done(dve, s_e, g, 2)
                nc.vector.tensor_tensor(z[:, b].rearrange("p (j d) -> p j d", j=SLOTS), psO[:, b].rearrange("p (j d) -> p j d", j=SLOTS),
                                        w["b3"][:, :].unsqueeze(1).to_broadcast([P, SLOTS, D]), ALU.add).then_inc(s_z, 1)

            def elu(g, q, m):
                b = m % 2
                done(dve, s_e, g)
                done(dve, s_y, g, 2)
                done(dve, s_nm, g, 2)
                c1.begin(g)
                c1.inc(nc.vector.scalar_tensor_tensor(u[:, b], e[:, b].rearrange("p (j d) -> p j d", j=SLOTS), -1.0,
                                               rz[:, b].rearrange("p (j d) -> p j d", j=SLOTS), ALU.add, ALU.add))
                c1.wait()
                stats4(ph, c1, u[:, b], st[:, b], mv[:, b]).then_inc(s_st, 1)
                c1.end()

            def scale(g, q, m):
                b = m % 2
                done(dve, s_rs, g)
                nc.vector.scalar_tensor_tensor(nm[:, b, :], mv[:, b, :, 0], -1.0, rs[:, b, :], ALU.mult, ALU.mult).then_inc(s_nm, 1)

            def add(g, q, m):
                b = m % 2
                done(dve, s_y, g)
                done(dve, s_xb, g)
                reused(dve, stored[m], q * 16)
                c2.begin(g)
                c2.inc(nc.vector.tensor_tensor(y[:, b], y[:, b], w["g3"][:, :].unsqueeze(1).to_broadcast([P, SLOTS, D]), ALU.mult))
                c2.wait()
                nc.vector.tensor_tensor(xo[:, m], y[:, b], xb[:, b], ALU.add).then_inc(s_xo, 1)
                c2.end()
            pipelined(dve, [(add, 6), (scale, 5), (elu, 4), (bias, 2)], NBLK, 4)

        @block.scalar
        def _(act):
            def evacuate(g, q, m):
                b = m % 2
                done(act, s_tr, g)
                done(act, s_mm, g, 2)
                nc.scalar.activation(aT[:, b], psT[:, b], ACT.Copy).then_inc(s_aT, 1)

            def exponential(g, q, m):
                b = m % 2
                done(act, s_z, g)
                done(act, s_st, g, 2)
                nc.scalar.activation(rz[:, b], z[:, b], ACT.Relu)
                done(act, s_zm, g)
                nc.scalar.activation(e[:, b], zm[:, b], ACT.Exp).then_inc(s_e, 1)

            def normalise(g, q, m):
                b = m % 2
                done(act, s_nm, g)
                done(act, s_xo, g, 2)
                normalise4(nc, y[:, b], u[:, b], lambda j: rs[:, b, j:j + 1], lambda j: nm[:, b, j:j + 1], ACT.Identity).then_inc(s_y, 1)
            pipelined(act, [(evacuate, 1), (exponential, 3), (normalise, 5)], NBLK, 4)

        @block.tensor
        def _(pe):
            def turn(g, q, m):
                b = m % 2
                pe.wait_ge(loaded[m], q * 16 + 16)
                done(pe, s_aT, g, 2)
                transposes4(nc, psT[:, b], ag[:, m], w["ident"]).then_inc(s_tr, 1)

            def project(g, q, m):
                b = m % 2
                done(pe, s_aT, g)
                done(pe, s_z, g, 2)
                for j in range(SLOTS):
                    last = nc.tensor.matmul(psO[:, b, j * P:(j + 1) * P], aT[:, b, j * P:(j + 1) * P], w["w3"][:, :], start=True, stop=True)
                last.then_inc(s_mm, 1)
            pipelined(pe, [(turn, 0), (project, 1)], NBLK, 4)


class Edges(Phase):

    def __init__(self, nc, ctx, w, name, table, key, first, second, widths):
        super().__init__(nc, ctx, name)
        self.table, self.key, self.fields = table, key, (first, second)
        self.rec, self.nxt = self.sb("rec", [P, 4, SLOTS, 4]), self.sb("nxt", [P, 4, SLOTS])
        self.index, self.goal = self.sb("index", [P, 4, 2, SLOTS], I32), self.sb("goal", [P, 4, SLOTS], I32)
        self.same = self.sb("same", [P, 4, SLOTS])
        self.got = [self.sb(f"got{k}", [P, 4, SLOTS, n]) for k, n in enumerate(widths)]
        self.kr, self.flag = self.sb("kr", [P, 2, BLK + 1]), self.sb("flag", [P, 2, BLK])
        self.sums, self.rows = self.sb("sums", [P, 2, BLK]), self.sb("rows", [P, 2, SLOTS, D])
        self.psK, self.psB = self.ps("psK", [P, BLK]), self.ps("psB", [P, BLK])
        self.loaded, self.gathered, self.scattered = self.sems("loaded", 4), self.dma(w, 4), self.dma(w, 4)
        self.own, self.init = self.sem("own"), self.sem("init")
        self.s_idx, self.s_goal, self.s_k, self.s_kr, self.s_flag, self.s_msg, self.s_scan, self.s_back, self.s_rows = self.step(
            "idx", "goal", "k", "kr", "flag", "msg", "scan", "back", "rows")

    def load(self, sp, users):
        def stage(g, q, m):
            for s in users:
                done(sp, s, g, 4)
            sp.dma_start(self.rec[:, m], self.table[bass.ds(g * BLK, BLK), :].rearrange("(j p) f -> p j f", p=P)).then_inc(self.loaded[m], 16)
            sp.dma_start(self.nxt[:, m], self.table[bass.ds(g * BLK + 1, BLK), self.key:self.key + 1].rearrange("(j p) f -> p (j f)", p=P),
                         allow_slow_non_contiguous=True).then_inc(self.loaded[m], 16)
        return stage

    def indices(self, dve):
        def stage(g, q, m):
            dve.wait_ge(self.loaded[m], q * 32 + 32)
            reused(dve, self.gathered[m], q * 16 * SLOTS * sum(f is not None for f in self.fields))
            for k, field in enumerate(self.fields):
                if field is not None:
                    last = self.nc.vector.tensor_copy(self.index[:, m, k], self.rec[:, m, :, field])
            last.then_inc(self.s_idx, 1)
        return stage

    def goals(self, dve):
        nc, tally = self.nc, Tally(dve, self.own, 1)

        def stage(g, q, m):
            reused(dve, self.scattered[m], q * 16 * SLOTS)
            tally.begin(g)
            tally.inc(nc.vector.tensor_tensor(self.same[:, m], self.nxt[:, m], self.rec[:, m, :, self.key], ALU.is_equal))
            tally.wait()
            nc.vector.scalar_tensor_tensor(self.goal[:, m], self.same[:, m], SKIP, self.rec[:, m, :, self.key],
                                           ALU.mult, ALU.add).then_inc(self.s_goal, 1)
            tally.end()
        return stage

    def flags(self, dve, user):
        def stage(g, q, m):
            b = m % 2
            done(dve, self.s_kr, g)
            done(dve, user, g, 2)
            self.nc.vector.tensor_tensor(self.flag[:, b], self.kr[:, b, 1:BLK + 1], self.kr[:, b, 0:BLK], ALU.is_equal).then_inc(self.s_flag, 1)
        return stage

    def clear(self, dve):
        self.nc.vector.memset(self.kr[:, 1, BLK:BLK + 1], -1.0)
        self.nc.vector.memset(self.sums[:, 1, BLK - 1:BLK], 0.0).then_inc(self.init, 1)
        dve.wait_ge(self.init, 1)

    def evacuate(self, dve):
        def stage(g, q, m):
            b = m % 2
            done(dve, self.s_back, g)
            reused(dve, self.scattered[(m + 2) % 4], (q + m // 2) * 16 * SLOTS)
            self.nc.vector.tensor_copy(self.rows[:, b], self.psB[:, :].rearrange("p (j d) -> p j d", j=SLOTS)).then_inc(self.s_rows, 1)
        return stage

    def run_pool(self, pool, tables, target, users):
        nc = self.nc
        limits = [pool.to_reg(x.shape[0] - 1) for x in tables]
        last = pool.to_reg(NPAD - 1)

        def gather(g, q, m):
            done(pool, self.s_idx, g)
            for s in users:
                done(pool, s, g, 4)
            self.apart(pool)
            for k, x in enumerate(tables):
                for j in range(SLOTS):
                    nc.gpsimd.indirect_dma_start(self.got[k][:, m, j, :], None, x,
                                                 bass.IndirectOffsetOnAxis(ap=self.index[:, m, k, j:j + 1], axis=0),
                                                 bounds_check=limits[k], oob_is_err=True).then_inc(self.gathered[m], 16)

        def scatter(g, q, m):
            done(pool, self.s_rows, g)
            done(pool, self.s_goal, g)
            self.apart(pool)
            for j in range(SLOTS):
                nc.gpsimd.indirect_dma_start(target, bass.IndirectOffsetOnAxis(ap=self.goal[:, m, j:j + 1], axis=0),
                                             self.rows[:, m % 2, j, :], None, bounds_check=last, oob_is_err=False
                                             ).then_inc(self.scattered[m], 16)
        pipelined(pool, [(gather, 0), (scatter, 6)], GROUPS, 4)
        for m in range(4):
            pool.wait_ge(self.gathered[m], 16 * SLOTS * len(tables) * ((GROUPS + 3 - m) // 4))
            pool.wait_ge(self.scattered[m], 16 * SLOTS * ((GROUPS + 3 - m) // 4))

    def arrived(self, eng, q, m, tables):
        eng.wait_ge(self.gathered[m], (q + 1) * 16 * SLOTS * tables)

    def key_rows(self, pe):
        def stage(g, q, m):
            pe.wait_ge(self.loaded[m], q * 32 + 32)
            done(pe, self.s_kr, g, 1)
            for j in range(SLOTS):
                last = self.nc.tensor.transpose(self.psK[:, j * P:(j + 1) * P],
                                                self.rec[:, m, j, self.key:self.key + 1].to_broadcast([P, P]), self.ident[:, :])
            last.then_inc(self.s_k, 1)
        return stage

    def back(self, pe):
        def stage(g, q, m):
            done(pe, self.s_scan, g)
            done(pe, self.s_rows, g, 1)
            for j in range(SLOTS):
                last = self.nc.tensor.transpose(self.psB[:, j * P:(j + 1) * P], self.sums[:, m % 2, j * P:(j + 1) * P], self.ident[:, :])
            last.then_inc(self.s_back, 1)
        return stage

    def key_copy(self, act):
        def stage(g, q, m):
            b = m % 2
            done(act, self.s_k, g)
            done(act, self.s_kr, g, 1)
            done(act, self.s_flag, g, 2)
            act.wait_ge(self.init, 1)
            self.nc.scalar.activation(self.kr[:, b, 0:1], self.kr[:, 1 - b, BLK:BLK + 1], ACT.Copy)
            self.nc.scalar.activation(self.kr[:, b, 1:BLK + 1], self.psK[:, :], ACT.Copy).then_inc(self.s_kr, 1)
        return stage


def message_edges(nc, a, w, t, layer):
    with ExitStack() as c:
        if layer == 1:
            ph = Edges(nc, c, w, "F1", t["by_dst"], 1, 0, None, [XW, D])
            tables, ordered, target = [t["x1"]], t["edge_attr"], t["sum_dst"]
        elif layer == 2:
            ph = Edges(nc, c, w, "F2", t["by_src"], 0, 0, None, [XW, D])
            tables, ordered, target = [t["x2"]], t["factors"], t["sum_src"]
        else:
            ph = Edges(nc, c, w, "F3", t["by_src"], 0, 1, None, [XW])
            tables, ordered, target = [t["x3"]], None, t["sum_src"]
        ph.ident = w["ident"]
        fetched = ph.sems("fetched", 4)
        h = ph.sb("h", [P, 2, SLOTS, D])
        bT, hT, msg = ph.sb("bT", [P, 2, BLK]), ph.sb("hT", [P, 2, BLK]), ph.sb("msg", [P, 2, BLK])
        zc, zb, ex, den, num = (ph.sb(n, [P, 2, BLK]) for n in ("zc", "zb", "ex", "den", "num"))
        psE, psH, psZ = ph.ps("psE", [P, BLK]), ph.ps("psH", [P, BLK]), ph.ps("psZ", [P, 2, BLK])
        s_h, s_hw, s_te, s_bT, s_th, s_hT, s_z, s_zb, s_zc, s_ex = ph.step("h", "hw", "te", "bT", "th", "hT", "z", "zb", "zc", "ex")
        ch = ph.sem("ch")
        block = new_block(nc, c, ph.all)

        @block.sync
        def _(sp):
            ph.start(sp)

            def second(g, q, m):
                done(sp, s_te, g, 4)
                ph.apart(sp)
                sp.dma_start(ph.got[1][:, m], ordered[bass.ds(g * BLK, BLK), :].rearrange("(j p) d -> p j d", p=P)).then_inc(fetched[m], 16)
            stages = [(ph.load(sp, [ph.s_idx, ph.s_goal, ph.s_k] + ([s_hw] if layer == 3 else [])), 0)]
            pipelined(sp, stages + ([(second, 0)] if layer < 3 else []), GROUPS, 4)

        @block.gpsimd
        def _(pool):
            ph.run_pool(pool, tables, target, [s_h])

        @block.vector
        def _(dve):
            ph.clear(dve)
            c1 = Tally(dve, ch, 4)

            def operand(g, q, m):
                done(dve, s_te, g)
                done(dve, s_z, g, 2)
                nc.vector.tensor_copy(bT[:, m % 2], psE[:, :]).then_inc(s_bT, 1)

            def weigh(g, q, m):
                done(dve, s_h, g)
                nc.vector.tensor_tensor(h[:, m % 2], h[:, m % 2], ph.rec[:, m, :, 3:4].to_broadcast([P, SLOTS, D]), ALU.mult).then_inc(s_hw, 1)

            def clip(g, q, m):
                done(dve, s_zb, g)
                done(dve, s_ex, g, 2)
                nc.vector.tensor_scalar(zc[:, m % 2], zb[:, m % 2], 30.0, None, ALU.min).then_inc(s_zc, 1)

            def mish(g, q, m):
                b = m % 2
                done(dve, s_ex, g)
                done(dve, ph.s_scan, g, 1)
                c1.begin(g)
                c1.inc(nc.vector.scalar_tensor_tensor(num[:, b], ex[:, b], 2.0, ex[:, b], ALU.add, ALU.mult))
                c1.wait()
                c1.inc(nc.vector.tensor_scalar(den[:, b], num[:, b], 2.0, None, ALU.add))
                c1.inc(nc.vector.tensor_tensor(num[:, b], num[:, b], zb[:, b], ALU.mult))
                c1.wait()
                c1.inc(nc.vector.reciprocal(den[:, b], den[:, b]))
                c1.wait()
                nc.vector.tensor_tensor(msg[:, b], num[:, b], den[:, b], ALU.mult).then_inc(ph.s_msg, 1)
                c1.end()

            def scan(g, q, m):
                b = m % 2
                done(dve, ph.s_msg if layer < 3 else s_z, g)
                done(dve, ph.s_flag, g)
                done(dve, ph.s_scan, g, 1)
                done(dve, ph.s_back, g, 2)
                nc.vector.tensor_tensor_scan(ph.sums[:, b], ph.flag[:, b], msg[:, b] if layer < 3 else psZ[:, b],
                                             ph.sums[:, 1 - b, BLK - 1:BLK], ALU.mult, ALU.add).then_inc(ph.s_scan, 1)
            index, goal, flags, evacuate = ph.indices(dve), ph.goals(dve), ph.flags(dve, ph.s_scan), ph.evacuate(dve)
            if layer == 1:
                stages = [(index, 0), (operand, 2), (clip, 3), (evacuate, 5), (flags, 3), (goal, 3), (mish, 4), (scan, 4)]
            elif layer == 2:
                stages = [(index, 0), (operand, 2), (scan, 4), (evacuate, 5), (flags, 3), (goal, 3)]
            else:
                stages = [(index, 0), (weigh, 2), (scan, 4), (evacuate, 5), (flags, 3), (goal, 3)]
            pipelined(dve, stages, GROUPS, 4)

        @block.scalar
        def _(act):
            def node(g, q, m):
                b = m % 2
                ph.arrived(act, q, m, 1)
                x = ph.got[0][:, m]
                done(act, {1: s_z, 2: s_th, 3: s_z}[layer], g, 2)
                normalise4(nc, h[:, b], x, lambda j: x[:, j, D:D + 1], lambda j: x[:, j, D + 1:XW], ACT.Relu).then_inc(s_h, 1)

            def argument(g, q, m):
                b = m % 2
                done(act, s_z, g)
                done(act, ph.s_msg, g, 2)
                nc.scalar.activation(zb[:, b], psZ[:, b], ACT.Identity, bias=w["bee"][:, :]).then_inc(s_zb, 1)

            def exponential(g, q, m):
                b = m % 2
                done(act, s_zc, g)
                done(act, ph.s_msg, g, 2)
                nc.scalar.activation(ex[:, b], zc[:, b], ACT.Exp).then_inc(s_ex, 1)

            def evacuate(g, q, m):
                done(act, s_th, g)
                done(act, s_z, g, 2)
                nc.scalar.activation(hT[:, m % 2], psH[:, :], ACT.Copy).then_inc(s_hT, 1)

            def message(g, q, m):
                done(act, s_z, g)
                done(act, ph.s_scan, g, 2)
                nc.scalar.activation(msg[:, m % 2], psZ[:, m % 2], ACT.Relu, bias=w["bm"][:, :]).then_inc(ph.s_msg, 1)
            keys = ph.key_copy(act)
            if layer == 1:
                stages = [(exponential, 4), (argument, 3), (keys, 3), (node, 1)]
            elif layer == 2:
                stages = [(evacuate, 2), (keys, 3), (message, 3), (node, 1)]
            else:
                stages = [(keys, 3), (node, 1)]
            pipelined(act, stages, GROUPS, 4)

        @block.tensor
        def _(pe):
            def turn(g, q, m):
                pe.wait_ge(fetched[m], q * 16 + 16)
                done(pe, s_bT, g, 1)
                transposes4(nc, psE[:, :], ph.got[1][:, m], w["ident"]).then_inc(s_te, 1)

            def turn_node(g, q, m):
                done(pe, s_h, g)
                done(pe, s_hT, g, 1)
                transposes4(nc, psH[:, :], h[:, m % 2], w["ident"]).then_inc(s_th, 1)

            def product1(g, q, m):
                b = m % 2
                done(pe, s_bT, g)
                done(pe, s_h, g)
                done(pe, s_zb, g, 2)
                nc.tensor.matmul(psZ[:, b], w["we"][:, :], bT[:, b], start=True, stop=False)
                for j in range(SLOTS):
                    last = nc.tensor.matmul(psZ[:, b, j * P:(j + 1) * P], h[:, b, j, :], w["ident"][:, :], start=False,
                                            stop=(j == SLOTS - 1))
                last.then_inc(s_z, 1)

            def product2(g, q, m):
                b = m % 2
                done(pe, s_bT, g)
                done(pe, s_hT, g)
                done(pe, ph.s_msg, g, 2)
                nc.tensor.matmul(psZ[:, b], w["wm"][:, 0, :], hT[:, b], start=True, stop=False)
                nc.tensor.matmul(psZ[:, b], w["wm"][:, 1, :], bT[:, b], start=False, stop=True).then_inc(s_z, 1)

            def turn_weighed(g, q, m):
                done(pe, s_hw, g)
                done(pe, ph.s_scan, g, 2)
                transposes4(nc, psZ[:, m % 2], h[:, m % 2], w["ident"]).then_inc(s_z, 1)
            keys, back = ph.key_rows(pe), ph.back(pe)
            if layer == 1:
                stages = [(back, 5), (product1, 2), (keys, 2), (turn, 1)]
            elif layer == 2:
                stages = [(back, 5), (product2, 3), (turn_node, 2), (keys, 2), (turn, 1)]
            else:
                stages = [(back, 5), (turn_weighed, 3), (keys, 2)]
            pipelined(pe, stages, GROUPS, 4)


def attention_edges(nc, a, w, t):
    with ExitStack() as c:
        ph = Edges(nc, c, w, "F0", t["by_dst"], 1, 0, 1, [AW, AW])
        ph.ident = w["ident"]
        pre, lg, v = ph.sb("pre", [P, 2, 2, SLOTS, HEADS]), ph.sb("lg", [P, 4, 2, SLOTS, HEADS]), ph.sb("v", [P, 2, SLOTS, HEADS])
        pen, m_ = ph.sb("pen", [HEADS, 2, BLK]), ph.sb("m", [HEADS, 2, BLK + 1])
        d, r, dsum = ph.sb("d", [HEADS, 2, 2, BLK]), ph.sb("r", [HEADS, 4, BLK]), ph.sb("dsum", [HEADS, 2, BLK])
        lm, p_ = ph.sb("lm", [P, 2, 2, SLOTS, HEADS]), ph.sb("p", [P, 4, 2, SLOTS, HEADS])
        phs, rS = ph.sb("phs", [P, 2, SLOTS, D]), ph.sb("rS", [P, 2, BLK])
        dn, rd, t1, t2 = ph.sb("dn", [P, 2, SLOTS, HEADS]), ph.sb("rd", [P, 2, SLOTS, HEADS]), ph.sb("t1", [P, 4, SLOTS, D]), ph.sb("t2", [P, 2, SLOTS, D])
        psV, psP, psR, psM = ph.ps("psV", [P, BLK]), ph.ps("psP", [P, BLK]), ph.ps("psR", [P, BLK]), ph.ps("psM", [P, BLK])
        psS, psD = ph.ps("psS", [P, SLOTS, HEADS]), ph.ps("psD", [P, SLOTS, HEADS])
        s_v, s_vT, s_m, s_d, s_r, s_mT, s_lm, s_p, s_ph, s_mm, s_rS = ph.step("v", "vT", "m", "d", "r", "mT", "lm", "p", "phs", "mm", "rS")
        ch1, ch2, ch3 = ph.sems("ch", 3)
        block = new_block(nc, c, ph.all)

        def heads(x):
            return x.unsqueeze(3).to_broadcast([P, SLOTS, HEADS, HD])

        def split(x):
            return x.rearrange("p j (h f) -> p j h f", h=HEADS)

        @block.sync
        def _(sp):
            ph.start(sp)
            pipelined(sp, [(ph.load(sp, [ph.s_idx, ph.s_goal, ph.s_k]), 0)], GROUPS, 4)

        @block.gpsimd
        def _(pool):
            ph.run_pool(pool, [t["att"], t["att"]], t["gat"], [s_ph])

        @block.vector
        def _(dve):
            nc.vector.memset(m_[:, 1, BLK:BLK + 1], 0.0)
            nc.vector.memset(dsum[:, 1, BLK - 1:BLK], 0.0)
            ph.clear(dve)
            c1, c2, c3 = Tally(dve, ch1, 2), Tally(dve, ch2, 2), Tally(dve, ch3, 2)

            def logits(g, q, m):
                b = m % 2
                ph.arrived(dve, q, m, 2)
                done(dve, s_vT, g, 2)
                done(dve, s_lm, g, 2)
                c1.begin(g)
                ga, gb = ph.got[0][:, m], ph.got[1][:, m]
                nc.vector.tensor_tensor(pre[:, b, 0], ga[:, :, D:D + HEADS], gb[:, :, D + HEADS:AW], ALU.add)
                c1.inc(nc.vector.tensor_tensor(pre[:, b, 1], gb[:, :, D:D + HEADS], gb[:, :, D + HEADS:AW], ALU.add))
                c1.wait()
                c1.inc(nc.vector.scalar_tensor_tensor(lg[:, m].rearrange("p k j h -> p (k j h)"), pre[:, b].rearrange("p k j h -> p (k j h)"), 0.2,
                                                      pre[:, b].rearrange("p k j h -> p (k j h)"), ALU.mult, ALU.max))
                c1.wait()
                nc.vector.tensor_tensor(v[:, b], lg[:, m, 0], lg[:, m, 1], ALU.max).then_inc(s_v, 1)
                c1.end()

            def maximum(g, q, m):
                b = m % 2
                done(dve, ph.s_flag, g)
                done(dve, s_d, g, 2)
                c2.begin(g)
                c2.inc(nc.vector.tensor_scalar(pen[:, b], ph.flag[0:HEADS, b], 1.0, -LOWEST, ALU.subtract, ALU.mult))
                done(dve, s_vT, g)
                done(dve, s_mT, g, 2)
                done(dve, s_m, g, 1)
                c2.wait()
                nc.vector.tensor_copy(m_[:, b, 0:1], m_[:, 1 - b, BLK:BLK + 1])
                nc.vector.tensor_tensor_scan(m_[:, b, 1:BLK + 1], pen[:, b], psV[0:HEADS, :], m_[:, 1 - b, BLK:BLK + 1],
                                             ALU.add, ALU.max).then_inc(s_m, 1)
                done(dve, s_m, g)
                done(dve, s_r, g, 2)
                c2.inc(nc.vector.tensor_tensor(d[:, b, 0], m_[:, b, 0:BLK], m_[:, b, 1:BLK + 1], ALU.subtract))
                c2.wait()
                nc.vector.tensor_tensor(d[:, b, 1], d[:, b, 0], pen[:, b], ALU.add).then_inc(s_d, 1)
                c2.end()

            def exponents(g, q, m):
                b = m % 2
                done(dve, s_mT, g)
                done(dve, s_p, g, 2)
                for k in range(2):
                    last = nc.vector.tensor_tensor(lm[:, b, k], lg[:, m, k], psS[:, :, :], ALU.subtract)
                last.then_inc(s_lm, 1)

            def weighed(g, q, m):
                b = m % 2
                done(dve, s_p, g)
                done(dve, s_mm, g, 2)
                done(dve, ph.s_rows, g, 4)
                nc.vector.tensor_tensor(split(t1[:, m]), split(ph.got[1][:, m, :, 0:D]), heads(p_[:, m, 1]), ALU.mult)
                nc.vector.tensor_tensor(split(phs[:, b]), split(ph.got[0][:, m, :, 0:D]), heads(p_[:, m, 0]), ALU.mult).then_inc(s_ph, 1)

            def scan(g, q, m):
                b = m % 2
                done(dve, s_mm, g)
                done(dve, s_rS, g)
                done(dve, ph.s_scan, g, 1)
                done(dve, ph.s_back, g, 2)
                nc.vector.tensor_tensor_scan(dsum[:, b], r[:, m], psP[0:HEADS, :], dsum[:, 1 - b, BLK - 1:BLK], ALU.mult, ALU.add)
                nc.vector.tensor_tensor_scan(ph.sums[:, b], rS[:, b], psM[:, :], ph.sums[:, 1 - b, BLK - 1:BLK],
                                             ALU.mult, ALU.add).then_inc(ph.s_scan, 1)

            def finish(g, q, m):
                b = m % 2
                done(dve, ph.s_back, g)
                done(dve, ph.s_rows, g, 1)
                reused(dve, ph.scattered[(m + 2) % 4], (q + m // 2) * 16 * SLOTS)
                c3.begin(g)
                nc.vector.tensor_tensor(dn[:, b], psD[:, :, :], p_[:, m, 1], ALU.add)
                c3.inc(nc.vector.tensor_tensor(t2[:, b], t1[:, m], ph.psB[:, :].rearrange("p (j d) -> p j d", j=SLOTS), ALU.add))
                c3.wait()
                c3.inc(nc.vector.reciprocal(rd[:, b], dn[:, b]))
                c3.wait()
                nc.vector.tensor_tensor(split(ph.rows[:, b]), split(t2[:, b]), heads(rd[:, b]), ALU.mult).then_inc(ph.s_rows, 1)
                c3.end()
            pipelined(dve, [(ph.indices(dve), 0), (exponents, 3), (finish, 5), (logits, 1), (ph.flags(dve, s_d), 2), (maximum, 2), (weighed, 3),
                            (ph.goals(dve), 3), (scan, 4)], GROUPS, 4)

        @block.scalar
        def _(act):
            def decay(g, q, m):
                b = m % 2
                done(act, s_d, g)
                done(act, ph.s_scan, g, 4)
                nc.scalar.activation(r[:, m], d[:, b, 1], ACT.Exp).then_inc(s_r, 1)

            def weights(g, q, m):
                b = m % 2
                done(act, s_lm, g)
                done(act, ph.s_rows, g, 4)
                nc.scalar.activation(p_[:, m], lm[:, b], ACT.Exp).then_inc(s_p, 1)

            def spread(g, q, m):
                done(act, s_mm, g)
                done(act, ph.s_scan, g, 2)
                nc.scalar.activation(rS[:, m % 2], psR[:, :], ACT.Copy).then_inc(s_rS, 1)
            pipelined(act, [(ph.key_copy(act), 2), (weights, 3), (decay, 3), (spread, 4)], GROUPS, 4)

        @block.tensor
        def _(pe):
            def turn_logits(g, q, m):
                done(pe, s_v, g)
                done(pe, s_m, g, 1)
                ph.apart(pe)
                for j in range(SLOTS):
                    last = nc.tensor.transpose(psV[0:HEADS, j * P:(j + 1) * P], v[:, m % 2, j, :], w["ident"][:, :])
                last.then_inc(s_vT, 1)

            def turn_maximum(g, q, m):
                done(pe, s_m, g)
                done(pe, s_lm, g, 1)
                ph.apart(pe)
                for j in range(SLOTS):
                    last = nc.tensor.transpose(psS[:, j, :], m_[:, m % 2, 1 + j * P:1 + (j + 1) * P], w["ident"][0:HEADS, 0:HEADS])
                last.then_inc(s_mT, 1)

            def turn_rows(g, q, m):
                b = m % 2
                done(pe, s_r, g)
                done(pe, ph.s_scan, g, 1)
                done(pe, s_rS, g, 1)
                nc.tensor.matmul(psR[:, :], w["expand"][:, :], r[:, m], start=True, stop=True)
                done(pe, s_ph, g)
                transposes4(nc, psM[:, :], phs[:, b], w["ident"])
                for j in range(SLOTS):
                    last = nc.tensor.transpose(psP[0:HEADS, j * P:(j + 1) * P], p_[:, m, 0, j, :], w["ident"][:, :])
                last.then_inc(s_mm, 1)

            def back(g, q, m):
                done(pe, ph.s_scan, g)
                done(pe, ph.s_rows, g, 1)
                for j in range(SLOTS):
                    nc.tensor.transpose(ph.psB[:, j * P:(j + 1) * P], ph.sums[:, m % 2, j * P:(j + 1) * P], w["ident"][:, :])
                    last = nc.tensor.transpose(psD[:, j, :], dsum[:, m % 2, j * P:(j + 1) * P], w["ident"][0:HEADS, 0:HEADS])
                last.then_inc(ph.s_back, 1)
            pipelined(pe, [(back, 5), (turn_rows, 4), (turn_logits, 1), (ph.key_rows(pe), 1), (turn_maximum, 2)], GROUPS, 4)


def program(nc, a, out):
    t = tables(nc)
    with ExitStack() as c:
        def sb(name, shape):
            return c.enter_context(nc.sbuf_tensor("k_" + name, shape, F32))
        w = {n: sb(n, [P, k]) for n, k in (
            ("ident", P), ("hmask", HEADS), ("wl", AW), ("proj", D), ("c0", D), ("g0", D), ("be0", D), ("we", D), ("bee", 1),
            ("eps1", 1), ("eps", 1), ("w1", HID), ("b1", 4), ("b2", D), ("bm", 1), ("bc", D), ("w3", D), ("b3", D),
            ("g3", D), ("be3", D))}
        w["expand"] = sb("expand", [HEADS, P])
        w["w2"], w["wm"], w["wc"] = sb("w2", [P, 4, D]), sb("wm", [P, 2, D]), sb("wc", [P, 2, D])
        w["dma"] = [c.enter_context(nc.semaphore(f"pool_dma{k}")) for k in range(8)]
        s = {n: sb(n, shape) for n, shape in (("iota", [P, LO]), ("iotap", [P, 2]), ("tri", [P, 3, P]), ("rec", [P, TILES, 4]),
                                              ("key", [P, 2, 3, TILES]), ("start", [P, 2, 2, LO]))}
        s["iotab"] = c.enter_context(nc.sbuf_tensor("k_iotab", [P, LO], BF16))
        prepare(nc, a, w)
        count_keys(nc, a, w, t, s)
        attention_inputs(nc, a, w, t, s)
        attention_edges(nc, a, w, t)
        attention_outputs(nc, a, w, t, s)
        message_edges(nc, a, w, t, 1)
        mlp(nc, a, w, t)
        message_edges(nc, a, w, t, 2)
        factor_update(nc, a, w, t)
        message_edges(nc, a, w, t, 3)
        graph_output(nc, a, w, t, out)


def kernel(**inputs):
    import numpy as np
    import concourse.bacc as bacc
    from concourse.bass_utils import run_bass_kernel_spmd

    v = {k: np.asarray(x) for k, x in inputs.items()}

    def rows(x, count, fill=0):
        full = np.full((count,) + x.shape[1:], fill, x.dtype)
        full[:x.shape[0]] = x
        return full

    def every(x):
        return np.ascontiguousarray(np.broadcast_to(x.reshape(1, -1), (P, x.size)))

    def tiles(x):
        return np.ascontiguousarray(np.moveaxis(x.reshape((TILES, P) + x.shape[1:]), 0, 1))
    i = np.arange(P)
    src, dst = rows(v["src"], EPAD, N), rows(v["dst"], EPAD, N)
    rec = np.zeros((EPAD, 2), np.float32)
    rec[:E, 0] = np.arange(E)
    rec[:E, 1] = v["edge_weight"]
    arrays = {
        "ident": np.eye(P, dtype=np.float32), "hmask": (i[:, None] // HD == np.arange(HEADS)[None, :]).astype(np.float32),
        "expand": (i[None, :] // HD == np.arange(HEADS)[:, None]).astype(np.float32),
        "iota": every(np.arange(LO, dtype=np.float32)), "iotap": np.stack([i, i + P], 1).astype(np.float32),
        "tri": np.stack([i[None, :] < i[:, None], i[:, None] < i[None, :], np.ones((P, P), bool)], 1).astype(np.float32),
        "sentinel": np.tile(np.array([[N, N, 0, 0]], np.float32), (PAD_ROWS, 1)),
        "x": rows(v["x"], NPAD), "factors": rows(v["L2_gnn_factors"], NPAD), "edge_attr": v["edge_attr_128"],
        "src_col": tiles(src), "dst_col": tiles(dst), "src_row": src[None], "dst_row": dst[None], "rec_col": tiles(rec),
        "linw": v["L0_gnn_lin_w"], "linwT": np.ascontiguousarray(v["L0_gnn_lin_w"].T),
        "projT": np.ascontiguousarray(v["L0_gnn_proj_w"].T),
        "att": np.stack([v["L0_gnn_att_src"].reshape(-1), v["L0_gnn_att_dst"].reshape(-1)], 1),
        "gatb": np.ascontiguousarray(every(v["L0_gnn_gat_bias"]).T), "projb": every(v["L0_gnn_proj_b"]),
        "g0": every(v["L0_gnn_ln_gamma"]), "be0": every(v["L0_gnn_ln_beta"]),
        "we": v["L1_gnn_W_e_k"], "bee": v["L1_gnn_W_e_b"].reshape(-1, 1), "eps1": every(v["L1_gnn_eps"]),
        "w1": v["L1_gnn_W1"], "glob": v["L1_gnn_globals_g"].reshape(-1, 1),
        "b1": np.ascontiguousarray(v["L1_gnn_b1"].reshape(4, P).T), "w2": v["L1_gnn_W2"], "b2": every(v["L1_gnn_b2"]),
        "wm": v["L2_gnn_Wm"], "bm": v["L2_gnn_bm"].reshape(-1, 1), "wc": v["L2_gnn_Wc"], "bc": every(v["L2_gnn_bc"]),
        "w3": v["L3_gnn_weight"], "b3": every(v["L3_gnn_bias"]), "g3": every(v["L3_gnn_ln_gamma"]), "be3": every(v["L3_gnn_ln_beta"]),
    }
    nc = bacc.Bacc("TRN2", target_bir_lowering=False, num_devices=1)
    a = {n: nc.dram_tensor(f"in_{n}", x.shape, mybir.dt.from_np(x.dtype), kind="ExternalInput").ap() for n, x in arrays.items()}
    out = nc.dram_tensor("out_x", (NPAD, D), F32, kind="ExternalOutput").ap()
    program(nc, a, out)
    r = run_bass_kernel_spmd(nc, [{f"in_{n}": x for n, x in arrays.items()}], core_ids=[0])
    return r.results[0]["out_x"][:N]
```

```python
import concourse.bass as bass
from concourse import mybir
from contextlib import ExitStack

F32, I32, BF16, F32R = mybir.dt.float32, mybir.dt.int32, mybir.dt.bfloat16, mybir.dt.float32r
ALU = mybir.AluOpType
ACT = mybir.ActivationFunctionType

P = 128
D = 128
N, E = 50000, 25000
HEADS, HD = 8, 16
HID = 512
SLOTS = 4
BLK = P * SLOTS
NBLK = 98
NPAD = NBLK * BLK
TILES = 196
EPAD = TILES * P
GROUPS = TILES // SLOTS
assert NPAD % (GROUPS * P) == 0
SROWS = EPAD + 16
REC = 4
PAD_ROWS = SROWS - EPAD
AW = D + 2 * HEADS
XW = D + 2
LO = 256
PAIR = TILES // NBLK
LN_EPS = 1e-5
SKIP = 1.0e6
LOWEST = -3.0e38


class Tally:

    def __init__(self, eng, sem, per):
        self.eng, self.sem, self.per = eng, sem, per

    def begin(self, turn):
        self.base, self.n = turn * self.per, 0

    def inc(self, instruction):
        self.n += 1
        instruction.then_inc(self.sem, 1)

    def wait(self):
        self.eng.wait_ge(self.sem, self.base + self.n)

    def end(self):
        assert self.n == self.per, f"per must be {self.n}"


def tables(nc):
    def dram(name, rows, cols):
        return nc.dram_tensor(name, (rows, cols), F32).ap()
    return {
        "att": dram("t_att", NPAD, AW), "gat": dram("t_gat", NPAD, D),
        "x1": dram("t_x1", NPAD, XW), "x2": dram("t_x2", NPAD, XW), "x3": dram("t_x3", NPAD, XW),
        "sum_dst": dram("t_sum_dst", NPAD, D), "sum_src": dram("t_sum_src", NPAD, D),
        "by_dst": dram("t_by_dst", SROWS, REC + D), "by_src": dram("t_by_src", SROWS, REC),
        "factors": dram("t_factors", EPAD, D), "hi_src": dram("t_hi_src", 1, EPAD), "hi_dst": dram("t_hi_dst", 1, EPAD),
    }


def blocks4(table, row):
    return table[bass.ds(row, BLK), :].rearrange("(p j) d -> p j d", p=P)


def new_block(nc, ctx, sems):
    def zero():
        with nc.Block() as after:
            @after.gpsimd
            def _(pool):
                pool.dma_reset()
                for s in sems:
                    pool.sem_clear(s)
    ctx.callback(zero)
    return ctx.enter_context(nc.Block())


def prepare(nc, a, w, s):
    with ExitStack() as c:
        loaded, folded, vec, step = (c.enter_context(nc.semaphore(n)) for n in
                                     ("w_loaded", "w_folded", "w_vec", "w_step"))
        ps = c.enter_context(nc.psum_tensor("w_ps", [P, 4, 512], F32))
        att = c.enter_context(nc.sbuf_tensor("w_att", [P, 2], F32))
        attm = c.enter_context(nc.sbuf_tensor("w_attm", [P, 2 * HEADS], F32))
        linw = c.enter_context(nc.sbuf_tensor("w_linw", [P, D], F32))
        gatb = c.enter_context(nc.sbuf_tensor("w_gatb", [P, D], F32))
        projb = c.enter_context(nc.sbuf_tensor("w_projb", [P, D], F32))
        w1b = c.enter_context(nc.sbuf_tensor("w_w1b", [P, HID], F32))
        glob = c.enter_context(nc.sbuf_tensor("w_glob", [P, 1], F32))
        b1 = c.enter_context(nc.sbuf_tensor("w_b1", [P, 4], F32))
        part, rest, placed = (c.enter_context(nc.sbuf_tensor("w_" + n, shape, dt)) for n, shape, dt in
                              (("part", [P, 2, D], BF16), ("rest", [P, 2, D], F32), ("placed", [P, D], F32)))
        block = new_block(nc, c, [loaded, folded, vec, step])
        loads = [(w["ident"][:, :], a["ident"]), (w["hmask"][:, :], a["hmask"]), (w["expand"][:, :], a["expand"]),
                 (w["wl"][:, 0:D], a["linwT"]), (w["proj"][:, :], a["projT"]), (linw[:, :], a["linw"]),
                 (att[:, :], a["att"]), (gatb[:, :], a["gatb"]), (projb[:, :], a["projb"]),
                 (w["g0"][:, :], a["g0"]), (w["be0"][:, :], a["be0"]), (w["we"][:, :], a["we"]), (w["bee"][:, :], a["bee"]),
                 (w["eps1"][:, :], a["eps1"]), (w["w1"][:, :], a["w1"][0:D, :]), (w1b[:, :], a["w1"][D:2 * D, :]),
                 (glob[:, :], a["glob"]), (b1[:, :], a["b1"]),
                 (w["w2"][:, :, :], a["w2"].rearrange("(c p) o -> p c o", p=P)), (w["b2"][:, :], a["b2"]),
                 (w["wm"][:, :, :], a["wm"].rearrange("(c p) o -> p c o", p=P)), (w["bm"][:, :], a["bm"]),
                 (w["wc"][:, :, :], a["wc"].rearrange("(c p) o -> p c o", p=P)), (w["bc"][:, :], a["bc"]),
                 (w["w3"][:, :], a["w3"]), (w["b3"][:, :], a["b3"]), (w["g3"][:, :], a["g3"]), (w["be3"][:, :], a["be3"]),
                 (s["ints"][:, 0, :], a["src_col"]), (s["ints"][:, 1, :], a["dst_col"]), (s["rec"][:, :, 2:4], a["rec_col"]),
                 (s["iota"][:, :], a["iota"]), (s["iotap"][:, :], a["iotap"]), (s["tri"][:, :, :], a["tri"])]

        @block.sync
        def _(sp):
            for dst, src in loads:
                sp.dma_start(dst, src).then_inc(loaded, 16)

        @block.vector
        def _(dve):
            nc.vector.memset(w["eps"][:, :], LN_EPS)
            nc.vector.memset(w["ones"][:, :], 1.0)
            nc.vector.memset(w["one"][:, :], 1.0)
            nc.vector.memset(w["zeros"][:, :], 0.0)
            dve.wait_ge(loaded, 16 * len(loads))
            for k in range(2):
                nc.vector.tensor_scalar(attm[:, k * HEADS:(k + 1) * HEADS], w["hmask"][:, :], att[:, k:k + 1], None,
                                        ALU.mult).then_inc(vec, 1)
            nc.vector.tensor_scalar(w["eps1"][:, :], w["eps1"][:, :], 1.0, None, ALU.add).then_inc(step, 1)
            dve.wait_ge(folded, 1)
            nc.vector.tensor_copy(w["wl"][:, D:AW], ps[:, 0, 0:2 * HEADS])
            nc.vector.tensor_tensor(w["c0"][:, :], ps[:, 1, 0:D], projb[:, :], ALU.add)
            nc.vector.tensor_tensor(w["b1"][:, :], ps[:, 2, 0:4], b1[:, :], ALU.add).then_inc(step, 1)
            dve.wait_ge(step, 2)
            count = 2

            def then(instruction):
                nonlocal count
                count += 1
                instruction.then_inc(step, 1)
                dve.wait_ge(step, count)
            then(nc.vector.tensor_copy(w["w1h"][:, :], w["w1"][:, :]))
            then(nc.vector.tensor_tensor(w["w1l"][:, :], w["w1"][:, :], w["w1h"][:, :].bitcast(F32), ALU.subtract))
            for name in ("c0", "bc", "b3"):
                bias = w[name][:, :]
                then(nc.vector.tensor_copy(part[:, 0], bias))
                then(nc.vector.tensor_tensor(rest[:, 0], bias, part[:, 0], ALU.subtract))
                then(nc.vector.tensor_copy(part[:, 1], rest[:, 0]))
                then(nc.vector.tensor_tensor(rest[:, 1], rest[:, 0], part[:, 1], ALU.subtract))
                then(nc.vector.tensor_scalar(placed[:, :], part[:, 0], w["ident"][:, 0:1], None, ALU.mult))
                then(nc.vector.scalar_tensor_tensor(placed[:, :], part[:, 1], w["ident"][:, 1:2], placed[:, :], ALU.mult, ALU.add))
                then(nc.vector.scalar_tensor_tensor(placed[:, :], rest[:, 1], w["ident"][:, 2:3], placed[:, :], ALU.mult, ALU.add))
                then(nc.vector.tensor_copy(w[name + "_parts"][:, :], placed[0:3, :]))

        @block.tensor
        def _(pe):
            pe.wait_ge(loaded, 16 * len(loads))
            pe.wait_ge(vec, 2)
            nc.tensor.matmul(ps[:, 0, 0:2 * HEADS], linw[:, :], attm[:, :], start=True, stop=True)
            nc.tensor.matmul(ps[:, 1, 0:D], gatb[:, :], w["proj"][:, :], start=True, stop=True)
            for k in range(4):
                last = nc.tensor.matmul(ps[:, 2, k:k + 1], w1b[:, k * D:(k + 1) * D], glob[:, :], start=True, stop=True)
            last.then_inc(folded, 1)



AHEAD = 4


def done(eng, sem, g, before=0):
    eng.wait_ge(sem, g + (AHEAD + 1 - before))


def reused(eng, sem, value):
    if not (isinstance(value, int) and value == 0):
        eng.wait_ge(sem, value)


def pipelined(eng, stages, count, unroll):
    longest = max(lag for _, lag in stages)
    head = longest + unroll
    turns = (count - head) // unroll

    def step(tau, i):
        for stage, lag in stages:
            at = tau - lag
            if i is None:
                if 0 <= at < count:
                    stage(at, at // unroll, at % unroll)
            else:
                stage(i * unroll + at, i + at // unroll, at % unroll)
    for tau in range(head):
        step(tau, None)
    with eng.Fori(0, turns) as i:
        for u in range(unroll):
            step(head + u, i)
    for tau in range(head + turns * unroll, count + longest):
        step(tau, None)


class Phase:

    def __init__(self, nc, ctx, name):
        self.nc, self.ctx, self.name, self.steps, self.all = nc, ctx, name, [], []
        self.gate = self.sem("gate")

    def sb(self, name, shape, dt=F32):
        return self.ctx.enter_context(self.nc.sbuf_tensor(f"{self.name}_{name}", shape, dt))

    def ps(self, name, shape):
        return self.ctx.enter_context(self.nc.psum_tensor(f"{self.name}_{name}", shape, F32))

    def sem(self, name):
        self.all.append(self.ctx.enter_context(self.nc.semaphore(f"{self.name}_{name}")))
        return self.all[-1]

    def dma(self, w, n):
        first = sum(s in w["dma"] for s in self.all)
        self.all += w["dma"][first:first + n]
        return w["dma"][first:first + n]

    def sems(self, name, n):
        return [self.sem(f"{name}{k}") for k in range(n)]

    def step(self, *names):
        made = [self.sem(n) for n in names]
        self.steps += made
        return made

    def apart(self, eng):
        eng.sem_inc(self.gate, 1)

    def start(self, eng):
        for s in self.steps:
            eng.sem_inc(s, AHEAD)


def transposes4(nc, out, src, ident):
    for j in range(SLOTS):
        last = nc.tensor.transpose(out[:, j * P:(j + 1) * P], src[:, j, 0:D], ident[:, :])
    return last


def biased4(nc, out, bias, ones):
    nc.tensor.matmul(out, ones[:, :], bias[:, :].unsqueeze(1).to_broadcast([3, SLOTS, D]), start=True, stop=False)


def stats4(ph, src, st):
    for j in range(SLOTS):
        last = ph.nc.vector.bn_stats(st[:, j, :], src[:, j, 0:D])
    return last


def aggregate4(ph, dve, st, mv):
    ph.apart(dve)
    for j in range(SLOTS):
        last = ph.nc.vector.bn_aggr(mv[:, j, :], st[:, j, :])
    return last


def normalise4(nc, out, src, scale, shift, func):
    for j in range(SLOTS):
        last = nc.scalar.activation(out[:, j, 0:D], src[:, j, 0:D], func, bias=shift(j), scale=scale(j))
    return last


def count_keys(nc, a, w, t, s):
    STEPS = TILES // SLOTS
    with ExitStack() as c:
        ph = Phase(nc, c, "H")
        ints, parts = s["ints"], ph.sb("parts", [P, 2, 2, TILES], I32)
        zero = ph.sb("zero", [P, 512], BF16)
        hi, lo = ph.sb("hi", [P, 2, 2, SLOTS, LO], BF16), ph.sb("lo", [P, 2, 2, SLOTS, LO], BF16)
        away, squares = ph.sb("away", [P, TILES]), ph.sb("squares", [P, 2, SLOTS, LO], BF16)
        incl, rowsum = ph.sb("incl", [P, 2, 2, LO]), ph.sb("rowsum", [P, 2, 2])
        psC, psB = [ph.ps(f"psC{k}", [P, 2, LO]) for k in range(2)], ph.ps("psB", [P, 512])
        HALF = TILES // 2
        psR, hirow = ph.ps("psR", [P, 2, 2, P]), ph.sb("hirow", [P, 2, 2, P])
        turned, kept = ph.sem("turned"), ph.sem("kept")
        cleared, zeroed, vec, based = (ph.sem(n) for n in ("cleared", "zeroed", "vec", "based"))
        s_hot, s_hot_a, s_squares, s_cnt = ph.step("hot", "hot_a", "squares", "cnt")
        block = new_block(nc, c, ph.all)

        @block.sync
        def _(sp):
            ph.start(sp)
            for table in (t["by_dst"], t["by_src"]):
                sp.dma_start(table[EPAD:SROWS, 0:REC], a["sentinel"]).then_inc(cleared, 16)
            sp.wait_ge(kept, 1)
            for k, table in enumerate((t["hi_src"], t["hi_dst"])):
                sp.dma_start(table.rearrange("o (h c p) -> c (o h) p", h=2, p=P), hirow[0:HALF, k]).then_inc(cleared, 16)
            sp.wait_ge(cleared, 2 * 16 * 2)

        @block.vector
        def _(dve):
            nc.vector.memset(zero[:, :], 0.0).then_inc(zeroed, 1)
            nc.vector.tensor_copy(s["iotab"][:, :], s["iota"][:, :])
            for k in range(2):
                nc.vector.tensor_copy(s["rec"][:, :, k], ints[:, k, :])
                nc.vector.tensor_copy(s["key"][:, k, 0, :], ints[:, k, :])
                nc.vector.tensor_scalar(parts[:, k, 0, :], ints[:, k, :], 8, None, ALU.logical_shift_right)
                last = nc.vector.tensor_scalar(parts[:, k, 1, :], ints[:, k, :], LO - 1, None, ALU.bitwise_and)
            last.then_inc(vec, 1)
            dve.wait_ge(vec, 1)
            nc.vector.tensor_copy(s["key"][:, :, 1:3, :], parts[:, :, :, :])
            nc.vector.tensor_scalar(away[:, :], parts[:, 1, 1, :], -1.0, None, ALU.mult).then_inc(vec, 1)
            dve.wait_ge(vec, 2)

            def hots(g, q, b):
                done(dve, s_cnt, g, 2)
                for k in range(2):
                    for j in range(SLOTS):
                        last = one_hot(nc, s, k, 1, g * SLOTS + j, hi[:, b, k, j, :])
                        if k == 0:
                            last = one_hot(nc, s, k, 2, g * SLOTS + j, lo[:, b, k, j, :])
                last.then_inc(s_hot, 1)
            pipelined(dve, [(hots, 0)], STEPS, 2)
            dve.wait_ge(turned, 1)
            nc.vector.tensor_copy(hirow[0:HALF], psR[0:HALF]).then_inc(kept, 1)
            done(dve, s_cnt, STEPS - 1)
            for k in range(2):
                for half in range(2):
                    nc.vector.tensor_tensor_scan(incl[:, k, half, :], zero[:, 0:LO], psC[k][:, half, :], 0.0, ALU.add, ALU.add)
                last = nc.vector.tensor_reduce(rowsum[:, k, :], psC[k][:, :, :], mybir.AxisListType.X, ALU.add)
            last.then_inc(vec, 1)
            dve.wait_ge(vec, 3)
            for k in range(2):
                last = nc.vector.tensor_tensor(incl[:, k], incl[:, k], psC[k][:, :, :], ALU.subtract)
            last.then_inc(vec, 1)
            dve.wait_ge(vec, 4)
            dve.wait_ge(based, 1)
            for k in range(2):
                for half in range(2):
                    last = nc.vector.tensor_scalar(s["start"][:, k, half, :], incl[:, k, half, :],
                                                   psB[:, 2 * k + half:2 * k + half + 1], None, ALU.add)
            last.then_inc(vec, 1)
            dve.wait_ge(vec, 5)

        @block.scalar
        def _(act):
            def square(g, q, b):
                done(act, s_hot_a, g, 2)
                for j in range(SLOTS):
                    last = nc.scalar.activation(squares[:, b, j, :], s["iotab"][:, :], ACT.Square, bias=away[:, bass.ds(g * SLOTS + j, 1)])
                last.then_inc(s_squares, 1)

            def hots(g, q, b):
                done(act, s_squares, g)
                done(act, s_cnt, g, 2)
                nc.scalar.activation(lo[:, b, 1], squares[:, b], ACT.Relu, bias=w["one"][:, :], scale=-1.0).then_inc(s_hot_a, 1)
            act.wait_ge(vec, 2)
            pipelined(act, [(hots, 1), (square, 0)], STEPS, 2)

        @block.tensor
        def _(pe):
            pe.wait_ge(zeroed, 1)
            for k in range(2):
                nc.tensor.matmul(psC[k][:, :, :], zero[:, 0:P], zero[:, :], start=True, stop=True)
            pe.wait_ge(vec, 2)
            for k in range(2):
                for half in range(2):
                    last = nc.tensor.transpose(psR[0:HALF, k, half, :], s["key"][:, k, 1, half * HALF:(half + 1) * HALF], w["ident"][:, :])
            last.then_inc(turned, 1)

            def count(g, q, b):
                done(pe, s_hot, g)
                done(pe, s_hot_a, g)
                for k in range(2):
                    for j in range(SLOTS):
                        last = count_tile(nc, psC[k], hi[:, b, k, j, :], lo[:, b, k, j, :])
                last.then_inc(s_cnt, 1)
            pipelined(pe, [(count, 0)], STEPS, 2)
            pe.wait_ge(vec, 3)
            for k in range(2):
                nc.tensor.matmul(psB[:, 2 * k:2 * k + 2], s["tri"][:, 1, :], rowsum[:, k, :], start=True, stop=True)
                last = nc.tensor.matmul(psB[:, 2 * k + 1:2 * k + 2], s["tri"][:, 2, :], rowsum[:, k, 0:1], start=False, stop=True,
                                        skip_group_check=True)
            last.then_inc(based, 1)


def one_hot(nc, s, k, part, tile, out):
    return nc.vector.tensor_scalar(out, s["iotab"][:, :], s["key"][:, k, part, bass.ds(tile, 1)], None, ALU.is_equal)


def count_tile(nc, table, hi, lo):
    for half in range(2):
        last = nc.tensor.matmul(table[:, half, :], hi[:, half * P:(half + 1) * P], lo, start=False, stop=True,
                                skip_group_check=True)
    return last


class Places:

    def __init__(self, ph, w, a, t, s, k, table, attributes=None, by_act=False):
        self.ph, self.nc, self.w, self.s, self.k, self.table = ph, ph.nc, w, s, k, table
        self.row, self.hi_row, self.attributes = a[("src_row", "dst_row")[k]], t[("hi_src", "hi_dst")[k]], attributes
        self.krow, self.hrow = ph.sb("krow", [P, 4, PAIR * P], I32), ph.sb("hrow", [P, 4, PAIR * P])
        self.hot_t = ph.sb("hot_t", [P, 2, 2, PAIR * P])
        self.hi, self.lo = ph.sb("hi", [P, 2, PAIR, LO], BF16), ph.sb("lo", [P, 2, PAIR, LO], BF16)
        self.count = ph.sb("count", [P, PAIR, 2, LO])
        self.scr, self.scr2 = ph.sb("scr", [P, 2, PAIR, P], BF16), ph.sb("scr2", [P, 2, PAIR, LO], BF16)
        self.before, self.earlier = ph.sb("before", [P, 4, PAIR]), ph.sb("earlier", [P, 4, PAIR])
        self.place, self.rec = ph.sb("place", [P, 4, PAIR], I32), ph.sb("prec", [P, 4, PAIR, table.shape[1]])
        self.psC, self.psL = ph.ps("psC", [P, 2, LO]), ph.ps("psL", [P, PAIR, 512])
        self.rows, self.scattered = ph.sems("rows", 4), ph.dma(w, 4)
        self.by_act, self.squared, self.squares = by_act, ph.sem("squared"), ph.sb("squares", [P, 2, PAIR * P]) if by_act else None
        self.seeded, self.attached = ph.sem("seeded"), ph.sems("attached", 4)
        self.s_hot, self.s_copy, self.s_count, self.s_look, self.s_pick, self.s_place, self.s_column = ph.step(
            "hot", "copy", "count", "look", "pick", "place", "column")

    def load(self, sp):
        def stage(g, q, m):
            done(sp, self.s_hot, g, 4)
            if self.by_act:
                done(sp, self.s_column, g, 4)
            self.ph.apart(sp)
            for out, row in ((self.krow, self.row), (self.hrow, self.hi_row)):
                sp.dma_start(out[:, m], row[:, bass.ds(g * PAIR * P, PAIR * P)].to_broadcast([P, PAIR * P])).then_inc(self.rows[m], 16)
        return stage

    def attach(self, sp):
        def stage(g, q, m):
            reused(sp, self.scattered[m], q * 16 * PAIR)
            self.ph.apart(sp)
            sp.dma_start(self.rec[:, m, :, REC:], self.attributes[bass.ds(g * PAIR * P, PAIR * P), :].rearrange("(j p) d -> p j d", p=P)
                         ).then_inc(self.attached[m], 16)
        return stage

    def hots(self, dve):
        nc, s, k = self.nc, self.s, self.k

        def stage(g, q, m):
            b = m % 2
            dve.wait_ge(self.rows[m], q * 32 + 32)
            done(dve, self.s_hot, g, 1)
            done(dve, self.s_count, g * PAIR, 3)
            for j in range(PAIR):
                one_hot(nc, s, k, 1, g * PAIR + j, self.hi[:, b, j, :])
                one_hot(nc, s, k, 2, g * PAIR + j, self.lo[:, b, j, :])
            if not self.by_act:
                done(dve, self.s_look, g * PAIR, 3)
                for half in range(2):
                    nc.vector.tensor_scalar(self.hot_t[:, b, half, :], self.hrow[:, m], s["iotap"][:, half:half + 1], None, ALU.is_equal)
            done(dve, self.s_place, g, 2)
            for j in range(PAIR):
                last = nc.vector.scalar_tensor_tensor(self.scr[:, b, j, :], self.krow[:, m, j * P:(j + 1) * P],
                                                      s["key"][:, k, 0, bass.ds(g * PAIR + j, 1)], s["tri"][:, 0, :],
                                                      ALU.is_equal, ALU.mult, accum_out=self.before[:, m, j:j + 1])
            last.then_inc(self.s_hot, 1)
        return stage

    def columns(self, act):
        nc, s = self.nc, self.s

        def stage(g, q, m):
            b = m % 2
            act.wait_ge(self.rows[m], q * 32 + 32)
            done(act, self.s_look, g * PAIR, 3)
            for half in range(2):
                last = nc.scalar.activation(self.squares[:, half], self.hrow[:, m], ACT.Square, bias=s["iotap"][:, 2 + half:3 + half])
            last.then_inc(self.squared, 1)
            act.wait_ge(self.squared, g + 1)
            nc.scalar.activation(self.hot_t[:, b], self.squares[:, :], ACT.Relu, bias=self.w["one"][:, :], scale=-1.0).then_inc(self.s_column, 1)
        return stage

    def picks(self, dve):
        nc, s, k = self.nc, self.s, self.k

        def stage(g, q, m):
            b = m % 2
            done(dve, self.s_place, g, 2)
            for j in range(PAIR):
                done(dve, self.s_look, g * PAIR + j)
                nc.vector.scalar_tensor_tensor(self.scr2[:, b, j, :], s["iota"][:, :], s["key"][:, k, 2, bass.ds(g * PAIR + j, 1)],
                                               self.psL[:, j, 0:LO], ALU.is_equal, ALU.mult,
                                               accum_out=self.earlier[:, m, j:j + 1]).then_inc(self.s_pick, 1)
        return stage

    def places(self, dve):
        nc, s = self.nc, self.s

        def stage(g, q, m):
            done(dve, self.s_pick, g * PAIR + PAIR - 1)
            reused(dve, self.scattered[m], q * 16 * PAIR)
            nc.vector.tensor_tensor(self.place[:, m], self.before[:, m], self.earlier[:, m], ALU.add)
            nc.vector.tensor_copy(self.rec[:, m, :, 0:REC], s["rec"][:, bass.ds(g * PAIR, PAIR), :]).then_inc(self.s_place, 1)
        return stage

    def copies(self, act, j):
        def stage(g, q, m):
            done(act, self.s_count, g * PAIR + j, 1)
            done(act, self.s_look, g * PAIR + j, 2)
            self.nc.scalar.activation(self.count[:, j], self.psC[:, :, :], ACT.Copy).then_inc(self.s_copy, 1)
        return stage

    def seed(self, pe):
        self.nc.tensor.matmul(self.psC[:, :, :], self.w["ident"][:, :], self.s["start"][:, self.k], start=True,
                              stop=True).then_inc(self.seeded, 1)

    def lookups(self, pe, j):
        nc = self.nc

        def stage(g, q, m):
            b = m % 2
            done(pe, self.s_hot, g)
            if self.by_act:
                done(pe, self.s_column, g)
            done(pe, self.s_copy, g * PAIR + j)
            count_tile(nc, self.psC, self.hi[:, b, j, :], self.lo[:, b, j, :]).then_inc(self.s_count, 1)
            done(pe, self.s_pick, g * PAIR + j, 2)
            for half in range(2):
                last = nc.tensor.matmul(self.psL[:, j, 0:LO], self.hot_t[:, b, half, j * P:(j + 1) * P],
                                        self.count[:, j, half, :], start=(half == 0), stop=(half == 1))
            last.then_inc(self.s_look, 1)
        return stage

    def scatter(self, pool, limit):
        def stage(g, q, m):
            done(pool, self.s_place, g)
            if self.attributes is not None:
                pool.wait_ge(self.attached[m], q * 16 + 16)
            self.ph.apart(pool)
            for j in range(PAIR):
                self.nc.gpsimd.indirect_dma_start(self.table, bass.IndirectOffsetOnAxis(ap=self.place[:, m, j:j + 1], axis=0),
                                                  self.rec[:, m, j, :], None, bounds_check=limit,
                                                  oob_is_err=True).then_inc(self.scattered[m], 16)
        return stage

    def end(self, pool):
        for m in range(4):
            pool.wait_ge(self.scattered[m], 16 * PAIR * ((NBLK + 3 - m) // 4))


class Permute:

    def __init__(self, ph, w, order, field, table, out):
        self.ph, self.nc, self.order, self.field, self.table, self.out = ph, ph.nc, order, field, table, out
        self.recs, self.index = ph.sb("recs", [P, 4, PAIR, 4]), ph.sb("pindex", [P, 4, PAIR], I32)
        self.rows = ph.sb("prows", [P, 4, PAIR, D])
        self.listed, self.fetched, self.kept = ph.sems("listed", 4), ph.dma(w, 4), ph.sems("kept", 4)
        (self.s_index,) = ph.step("pindex")

    def load(self, sp):
        def stage(g, q, m):
            done(sp, self.s_index, g, 4)
            self.ph.apart(sp)
            sp.dma_start(self.recs[:, m], self.order[bass.ds(g * PAIR * P, PAIR * P), :].rearrange("(j p) f -> p j f", p=P)).then_inc(self.listed[m], 16)
        return stage

    def indices(self, dve):
        def stage(g, q, m):
            dve.wait_ge(self.listed[m], q * 16 + 16)
            reused(dve, self.fetched[m], q * 16 * PAIR)
            self.nc.vector.tensor_copy(self.index[:, m], self.recs[:, m, :, self.field]).then_inc(self.s_index, 1)
        return stage

    def gather(self, pool, limit):
        def stage(g, q, m):
            done(pool, self.s_index, g)
            reused(pool, self.kept[m], q * 16)
            self.ph.apart(pool)
            for j in range(PAIR):
                self.nc.gpsimd.indirect_dma_start(self.rows[:, m, j, :], None, self.table,
                                                  bass.IndirectOffsetOnAxis(ap=self.index[:, m, j:j + 1], axis=0),
                                                  bounds_check=limit, oob_is_err=True).then_inc(self.fetched[m], 16)
        return stage

    def store(self, sp):
        def stage(g, q, m):
            sp.wait_ge(self.fetched[m], (q + 1) * 16 * PAIR)
            self.ph.apart(sp)
            sp.dma_start(self.out[bass.ds(g * PAIR * P, PAIR * P), :].rearrange("(j p) d -> p j d", p=P), self.rows[:, m]).then_inc(self.kept[m], 16)
        return stage

    def end(self, sp):
        for m in range(4):
            sp.wait_ge(self.kept[m], 16 * ((NBLK + 3 - m) // 4))

    def end_pool(self, pool):
        for m in range(4):
            pool.wait_ge(self.fetched[m], 16 * PAIR * ((NBLK + 3 - m) // 4))


def attention_inputs(nc, a, w, t, s):
    with ExitStack() as c:
        ph = Phase(nc, c, "A")
        x, st, mv, sd = ph.sb("x", [P, 4, SLOTS, D]), ph.sb("st", [P, 2, SLOTS, 6]), ph.sb("mv", [P, 2, SLOTS, 2]), ph.sb("sd", [P, 2, SLOTS])
        rs, nm = ph.sb("rs", [P, 2, SLOTS]), ph.sb("nm", [P, 2, SLOTS])
        h, hT, o = ph.sb("h", [P, 2, SLOTS, D]), ph.sb("hT", [P, 2, BLK]), ph.sb("o", [P, 4, SLOTS, AW])
        psT, psO = ph.ps("psT", [P, BLK]), ph.ps("psO", [P, 2, SLOTS, LO])
        loaded, stored = ph.sems("loaded", 4), ph.sems("stored", 4)
        s_raw, s_stat, s_sd, s_rs, s_h, s_tr, s_hT, s_mm, s_o, s_inv = ph.step("raw", "stat", "sd", "rs", "h", "tr", "hT", "mm", "o", "inv")
        pl = Places(ph, w, a, t, s, 1, t["by_dst"], a["edge_attr"])
        block = new_block(nc, c, ph.all)

        @block.sync
        def _(sp):
            ph.start(sp)

            def load(g, q, m):
                done(sp, s_h, g, 4)
                sp.dma_start(x[:, m], blocks4(a["x"], g * BLK)).then_inc(loaded[m], 16)

            def store(g, q, m):
                done(sp, s_o, g)
                sp.dma_start(blocks4(t["att"], g * BLK), o[:, m]).then_inc(stored[m], 16)
                sp.dma_start(blocks4(t["gat"], g * BLK), o[:, m, :, 0:D]).then_inc(stored[m], 16)
            pipelined(sp, [(load, 0), (pl.load(sp), 0), (pl.attach(sp), 2), (store, 4)], NBLK, 4)
            for m in range(4):
                sp.wait_ge(stored[m], 32 * ((NBLK + 3 - m) // 4))

        @block.gpsimd
        def _(pool):
            limit = pool.to_reg(SROWS - 1)
            pipelined(pool, [(pl.scatter(pool, limit), 4)], NBLK, 4)
            pl.end(pool)

        @block.vector
        def _(dve):
            def stats(g, q, m):
                b = m % 2
                dve.wait_ge(loaded[m], q * 16 + 16)
                done(dve, s_stat, g, 2)
                stats4(ph, x[:, m], st[:, b]).then_inc(s_raw, 1)

            def aggregate(g, q, m):
                b = m % 2
                done(dve, s_raw, g)
                done(dve, s_rs, g, 2)
                done(dve, s_sd, g, 2)
                aggregate4(ph, dve, st[:, b], mv[:, b]).then_inc(s_stat, 1)

            def scale(g, q, m):
                b = m % 2
                done(dve, s_sd, g)
                done(dve, s_h, g, 2)
                nc.vector.reciprocal(rs[:, b, :], sd[:, b, :]).then_inc(s_inv, 1)

            def offset(g, q, m):
                b = m % 2
                done(dve, s_inv, g)
                nc.vector.scalar_tensor_tensor(nm[:, b, :], mv[:, b, :, 0], -1.0, rs[:, b, :], ALU.mult, ALU.mult).then_inc(s_rs, 1)

            pipelined(dve, [(pl.picks(dve), 3), (scale, 1), (pl.places(dve), 3), (offset, 1), (stats, 0), (pl.hots(dve), 1), (aggregate, 0)], NBLK, 4)

        @block.scalar
        def _(act):
            def deviation(g, q, m):
                b = m % 2
                done(act, s_stat, g)
                done(act, s_rs, g, 2)
                nc.scalar.activation(sd[:, b, :], mv[:, b, :, 1], ACT.Sqrt, bias=w["eps"][:, :]).then_inc(s_sd, 1)

            def relu(g, q, m):
                b = m % 2
                done(act, s_rs, g)
                done(act, s_tr, g, 2)
                normalise4(nc, h[:, b], x[:, m], lambda j: rs[:, b, j:j + 1], lambda j: nm[:, b, j:j + 1], ACT.Relu).then_inc(s_h, 1)

            def evacuate(g, q, m):
                b = m % 2
                done(act, s_tr, g)
                done(act, s_mm, g, 2)
                nc.scalar.activation(hT[:, b], psT[:, :], ACT.Copy).then_inc(s_hT, 1)

            def output(g, q, m):
                b = m % 2
                done(act, s_mm, g)
                reused(act, stored[m], q * 32)
                nc.scalar.activation(o[:, m], psO[:, b, :, 0:AW], ACT.Copy).then_inc(s_o, 1)
            act.wait_ge(pl.seeded, 1)
            pipelined(act, [(pl.copies(act, 0), 2), (evacuate, 2), (pl.copies(act, 1), 2), (output, 3), (relu, 1), (deviation, 0)], NBLK, 4)

        @block.tensor
        def _(pe):
            def turn(g, q, m):
                b = m % 2
                done(pe, s_h, g)
                done(pe, s_hT, g, 1)
                transposes4(nc, psT[:, :], h[:, b], w["ident"]).then_inc(s_tr, 1)

            def project(g, q, m):
                b = m % 2
                done(pe, s_hT, g)
                done(pe, s_o, g, 2)
                for j in range(SLOTS):
                    last = nc.tensor.matmul(psO[:, b, j, 0:AW], hT[:, b, j * P:(j + 1) * P], w["wl"][:, :], start=True, stop=True)
                last.then_inc(s_mm, 1)
            pl.seed(pe)
            pipelined(pe, [(pl.lookups(pe, 0), 2), (project, 2), (pl.lookups(pe, 1), 2), (turn, 1)], NBLK, 4)


def attention_outputs(nc, a, w, t, s):
    with ExitStack() as c:
        ph = Phase(nc, c, "B")
        x, ga, xb = ph.sb("x", [P, 4, SLOTS, D]), ph.sb("ga", [P, 4, SLOTS, D]), ph.sb("xb", [P, 2, SLOTS, D])
        gT, y, yg, xo = ph.sb("gT", [P, 2, BLK]), ph.sb("y", [P, 2, SLOTS, D]), ph.sb("yg", [P, 2, SLOTS, D]), ph.sb("xo", [P, 4, SLOTS, XW])
        st, mv, sd = ph.sb("st", [P, 2, 2, SLOTS, 6]), ph.sb("mv", [P, 2, 2, SLOTS, 2]), ph.sb("sd", [P, 2, 2, SLOTS])
        rs, nm = ph.sb("rs", [P, 2, SLOTS]), ph.sb("nm", [P, 2, SLOTS])
        psT, psO = ph.ps("psT", [P, BLK]), ph.ps("psO", [P, 4, SLOTS, D])
        loaded, loaded_x, stored = ph.sems("loaded", 4), ph.sems("loaded_x", 4), ph.sems("stored", 4)
        s_xb, s_tr, s_gT, s_mm, s_st1, s_sd1, s_rs1, s_y, s_yg, s_st2, s_sd2, s_xo, s_raw1, s_x1, s_raw2, s_inv1, s_inv2 = ph.step(
            "xb", "tr", "gT", "mm", "st1", "sd1", "rs1", "y", "yg", "st2", "sd2", "xo", "raw1", "x1", "raw2", "inv1", "inv2")
        pl = Places(ph, w, a, t, s, 0, t["by_src"], by_act=True)
        block = new_block(nc, c, ph.all)

        @block.sync
        def _(sp):
            ph.start(sp)

            def load(g, q, m):
                done(sp, s_tr, g, 4)
                sp.dma_start(ga[:, m], blocks4(t["gat"], g * BLK)).then_inc(loaded[m], 16)

            def load_x(g, q, m):
                done(sp, s_xb, g, 4)
                sp.dma_start(x[:, m], blocks4(a["x"], g * BLK)).then_inc(loaded_x[m], 16)

            def store(g, q, m):
                done(sp, s_xo, g)
                sp.dma_start(blocks4(t["x1"], g * BLK), xo[:, m]).then_inc(stored[m], 16)
            pipelined(sp, [(load, 0), (pl.load(sp), 0), (load_x, 4), (store, 9)], NBLK, 4)
            for m in range(4):
                sp.wait_ge(stored[m], 16 * ((NBLK + 3 - m) // 4))

        @block.gpsimd
        def _(pool):
            def shift(g, q, m):
                b = m % 2
                pool.wait_ge(loaded_x[m], q * 16 + 16)
                done(pool, s_st2, g, 2)
                nc.gpsimd.tensor_tensor(xb[:, b], x[:, m], w["be0"][:, :].unsqueeze(1).to_broadcast([P, SLOTS, D]), ALU.add).then_inc(s_xb, 1)

            def gain(g, q, m):
                b = m % 2
                done(pool, s_y, g)
                done(pool, s_st2, g, 2)
                nc.gpsimd.tensor_tensor(yg[:, b], y[:, b], w["g0"][:, :].unsqueeze(1).to_broadcast([P, SLOTS, D]), ALU.mult).then_inc(s_yg, 1)

            limit = pool.to_reg(SROWS - 1)
            pipelined(pool, [(pl.scatter(pool, limit), 4), (shift, 6), (gain, 6)], NBLK, 4)
            pl.end(pool)

        @block.vector
        def _(dve):
            def first(g, q, m):
                b = m % 2
                done(dve, s_mm, g)
                done(dve, s_st1, g, 2)
                stats4(ph, psO[:, m], st[:, 0, b]).then_inc(s_raw1, 1)

            def aggregate1(g, q, m):
                b = m % 2
                done(dve, s_raw1, g)
                done(dve, s_rs1, g, 2)
                done(dve, s_sd1, g, 2)
                aggregate4(ph, dve, st[:, 0, b], mv[:, 0, b]).then_inc(s_st1, 1)

            def scale(g, q, m):
                b = m % 2
                done(dve, s_sd1, g)
                done(dve, s_y, g, 2)
                nc.vector.reciprocal(rs[:, b, :], sd[:, 0, b, :]).then_inc(s_inv1, 1)

            def offset(g, q, m):
                b = m % 2
                done(dve, s_inv1, g)
                nc.vector.scalar_tensor_tensor(nm[:, b, :], mv[:, 0, b, :, 0], -1.0, rs[:, b, :], ALU.mult, ALU.mult).then_inc(s_rs1, 1)

            def second(g, q, m):
                b = m % 2
                done(dve, s_yg, g)
                done(dve, s_xb, g)
                done(dve, s_sd2, g, 2)
                reused(dve, stored[m], q * 16)
                nc.vector.tensor_tensor(xo[:, m, :, 0:D], yg[:, b], xb[:, b], ALU.add).then_inc(s_x1, 1)

            def stats2(g, q, m):
                b = m % 2
                done(dve, s_x1, g)
                done(dve, s_st2, g, 2)
                stats4(ph, xo[:, m], st[:, 1, b]).then_inc(s_raw2, 1)

            def aggregate2(g, q, m):
                b = m % 2
                done(dve, s_raw2, g)
                done(dve, s_xo, g, 2)
                done(dve, s_sd2, g, 2)
                aggregate4(ph, dve, st[:, 1, b], mv[:, 1, b]).then_inc(s_st2, 1)

            def finish(g, q, m):
                b = m % 2
                done(dve, s_sd2, g)
                nc.vector.reciprocal(xo[:, m, :, D:D + 1], sd[:, 1, b, :].unsqueeze(2)).then_inc(s_inv2, 1)

            def finish_offset(g, q, m):
                b = m % 2
                done(dve, s_inv2, g)
                nc.vector.scalar_tensor_tensor(xo[:, m, :, D + 1:XW], mv[:, 1, b, :, 0:1], -1.0, xo[:, m, :, D:D + 1], ALU.mult, ALU.mult).then_inc(s_xo, 1)
            pipelined(dve, [(scale, 5), (finish, 8), (offset, 5), (finish_offset, 8), (pl.picks(dve), 3), (second, 7), (pl.places(dve), 3), (pl.hots(dve), 1), (stats2, 7), (first, 3), (aggregate2, 7), (aggregate1, 3)], NBLK, 4)

        @block.scalar
        def _(act):
            def evacuate(g, q, m):
                b = m % 2
                done(act, s_tr, g)
                done(act, s_mm, g, 2)
                nc.scalar.activation(gT[:, b], psT[:, :], ACT.Copy).then_inc(s_gT, 1)

            def deviation1(g, q, m):
                b = m % 2
                done(act, s_st1, g)
                nc.scalar.activation(sd[:, 0, b, :], mv[:, 0, b, :, 1], ACT.Sqrt, bias=w["eps"][:, :]).then_inc(s_sd1, 1)

            def normalise(g, q, m):
                b = m % 2
                done(act, s_rs1, g)
                done(act, s_yg, g, 2)
                normalise4(nc, y[:, b], psO[:, m], lambda j: rs[:, b, j:j + 1], lambda j: nm[:, b, j:j + 1], ACT.Identity).then_inc(s_y, 1)

            def deviation2(g, q, m):
                b = m % 2
                done(act, s_st2, g)
                nc.scalar.activation(sd[:, 1, b, :], mv[:, 1, b, :, 1], ACT.Sqrt, bias=w["eps"][:, :]).then_inc(s_sd2, 1)
            act.wait_ge(pl.seeded, 1)
            pipelined(act, [(deviation2, 8), (pl.copies(act, 0), 2), (evacuate, 1), (normalise, 5), (pl.copies(act, 1), 2), (pl.columns(act), 1), (deviation1, 4)], NBLK, 4)

        @block.tensor
        def _(pe):
            def turn(g, q, m):
                pe.wait_ge(loaded[m], q * 16 + 16)
                done(pe, s_gT, g, 1)
                transposes4(nc, psT[:, :], ga[:, m], w["ident"]).then_inc(s_tr, 1)

            def project(g, q, m):
                b = m % 2
                done(pe, s_gT, g)
                done(pe, s_st1, g, 4)
                done(pe, s_y, g, 4)
                biased4(nc, psO[:, m], w["c0_parts"], w["ones"])
                for j in range(SLOTS):
                    last = nc.tensor.matmul(psO[:, m, j], gT[:, b, j * P:(j + 1) * P], w["proj"][:, :], start=False, stop=(j == SLOTS - 1))
                last.then_inc(s_mm, 1)
            pl.seed(pe)
            pipelined(pe, [(pl.lookups(pe, 0), 2), (project, 2), (turn, 0), (pl.lookups(pe, 1), 2)], NBLK, 4)


def mlp(nc, a, w, t):
    with ExitStack() as c:
        ph = Phase(nc, c, "C")
        x, ag, xb = ph.sb("x", [P, 4, SLOTS, XW]), ph.sb("ag", [P, 4, SLOTS, D]), ph.sb("xb", [P, 4, SLOTS, D])
        h, hh, hT, r, xo = ph.sb("h", [P, 2, SLOTS, D]), ph.sb("hh", [P, 2, SLOTS, D]), ph.sb("hT", [P, 2, 2, BLK], F32R), ph.sb("r", [P, 2, 4, BLK]), ph.sb("xo", [P, 4, SLOTS, XW])
        st, mv, sd = ph.sb("st", [P, 2, SLOTS, 6]), ph.sb("mv", [P, 2, SLOTS, 2]), ph.sb("sd", [P, 2, SLOTS])
        psT, psH, psO = ph.ps("psT", [P, 2, BLK]), ph.ps("psH", [P, 4, BLK]), ph.ps("psO", [P, 2, BLK])
        loaded, stored = ph.sems("loaded", 4), ph.sems("stored", 4)
        s_xb, s_h, s_hh, s_tr, s_hT, s_up, s_ra, s_rv, s_mm, s_st, s_sd, s_xo, s_x2, s_raw, s_upper, s_inv = ph.step(
            "xb", "h", "hh", "tr", "hT", "up", "ra", "rv", "mm", "st", "sd", "xo", "x2", "raw", "upper", "inv")
        up2 = ph.sem("up2")
        pm = Permute(ph, w, t["by_src"], 1, a["factors"], t["factors"])
        block = new_block(nc, c, ph.all)

        @block.sync
        def _(sp):
            ph.start(sp)

            def load(g, q, m):
                done(sp, s_xb, g, 4)
                done(sp, s_h, g, 4)
                done(sp, s_hh, g, 4)
                sp.dma_start(x[:, m], blocks4(t["x1"], g * BLK)).then_inc(loaded[m], 16)
                sp.dma_start(ag[:, m], blocks4(t["sum_dst"], g * BLK)).then_inc(loaded[m], 16)

            def store(g, q, m):
                done(sp, s_xo, g)
                sp.dma_start(blocks4(t["x2"], g * BLK), xo[:, m]).then_inc(stored[m], 16)
            pipelined(sp, [(load, 0), (pm.load(sp), 0), (pm.store(sp), 4), (store, 7)], NBLK, 4)
            pm.end(sp)
            for m in range(4):
                sp.wait_ge(stored[m], 16 * ((NBLK + 3 - m) // 4))

        @block.gpsimd
        def _(pool):
            def shift(g, q, m):
                pool.wait_ge(loaded[m], q * 32 + 32)
                done(pool, s_st, g, 4)
                nc.gpsimd.tensor_tensor(xb[:, m], x[:, m, :, 0:D], w["b2"][:, :].unsqueeze(1).to_broadcast([P, SLOTS, D]), ALU.add).then_inc(s_xb, 1)

            last = pool.to_reg(NPAD - 1)
            pipelined(pool, [(pm.gather(pool, last), 2), (shift, 3)], NBLK, 4)
            pm.end_pool(pool)

        @block.vector
        def _(dve):
            def combine(g, q, m):
                b = m % 2
                done(dve, s_h, g)
                done(dve, s_tr, g, 2)
                nc.vector.scalar_tensor_tensor(hh[:, b], h[:, b], w["eps1"][:, :], ag[:, m], ALU.mult, ALU.add).then_inc(s_hh, 1)

            def remainder(g, q, m):
                b = m % 2
                done(dve, s_upper, g)
                nc.vector.tensor_tensor(hT[:, b, 1], psT[:, b], hT[:, b, 0].bitcast(F32), ALU.subtract).then_inc(s_hT, 1)

            def relu(g, q, m):
                b = m % 2
                done(dve, s_up, g)
                done(dve, s_mm, g, 2)
                for k in (2, 3):
                    last = nc.vector.tensor_scalar(r[:, b, k], psH[:, k], w["b1"][:, k:k + 1], 0.0, ALU.add, ALU.max)
                last.then_inc(s_rv, 1)

            def add(g, q, m):
                b = m % 2
                done(dve, s_mm, g)
                done(dve, s_xb, g)
                done(dve, s_sd, g, 2)
                reused(dve, stored[m], q * 16)
                nc.vector.tensor_tensor(xo[:, m, :, 0:D], psO[:, b].rearrange("p (j d) -> p j d", j=SLOTS), xb[:, m], ALU.add).then_inc(s_x2, 1)

            def stats(g, q, m):
                b = m % 2
                done(dve, s_x2, g)
                stats4(ph, xo[:, m], st[:, b]).then_inc(s_raw, 1)

            def aggregate(g, q, m):
                b = m % 2
                done(dve, s_raw, g)
                aggregate4(ph, dve, st[:, b], mv[:, b]).then_inc(s_st, 1)

            def finish(g, q, m):
                b = m % 2
                done(dve, s_sd, g)
                nc.vector.reciprocal(xo[:, m, :, D:D + 1], sd[:, b, :].unsqueeze(2)).then_inc(s_inv, 1)

            def offset(g, q, m):
                b = m % 2
                done(dve, s_inv, g)
                nc.vector.scalar_tensor_tensor(xo[:, m, :, D + 1:XW], mv[:, b, :, 0:1], -1.0, xo[:, m, :, D:D + 1], ALU.mult, ALU.mult).then_inc(s_xo, 1)
            pipelined(dve, [(pm.indices(dve), 1), (add, 5), (remainder, 2), (finish, 6), (combine, 1), (offset, 6), (stats, 5), (relu, 3), (aggregate, 5)], NBLK, 4)

        @block.scalar
        def _(act):
            def node(g, q, m):
                b = m % 2
                act.wait_ge(loaded[m], q * 32 + 32)
                done(act, s_hh, g, 2)
                normalise4(nc, h[:, b], x[:, m], lambda j: x[:, m, j, D:D + 1], lambda j: x[:, m, j, D + 1:XW], ACT.Relu).then_inc(s_h, 1)

            def relu(g, q, m):
                b = m % 2
                act.wait_ge(up2, g + 1)
                done(act, s_mm, g, 2)
                for k in (0, 1):
                    last = nc.scalar.activation(r[:, b, k], psH[:, k], ACT.Relu, bias=w["b1"][:, k:k + 1])
                last.then_inc(s_ra, 1)

            def evacuate(g, q, m):
                b = m % 2
                done(act, s_tr, g)
                done(act, s_up, g, 2)
                nc.scalar.activation(hT[:, b, 0], psT[:, b], ACT.Copy).then_inc(s_upper, 1)

            def deviation(g, q, m):
                b = m % 2
                done(act, s_st, g)
                done(act, s_xo, g, 2)
                nc.scalar.activation(sd[:, b, :], mv[:, b, :, 1], ACT.Sqrt, bias=w["eps"][:, :]).then_inc(s_sd, 1)
            pipelined(act, [(evacuate, 2), (deviation, 6), (node, 0), (relu, 3)], NBLK, 4)

        @block.tensor
        def _(pe):
            def turn(g, q, m):
                b = m % 2
                done(pe, s_hh, g)
                done(pe, s_hT, g, 2)
                transposes4(nc, psT[:, b], hh[:, b], w["ident"]).then_inc(s_tr, 1)

            def expand(k, b):
                for i, (left, right) in enumerate((("w1l", 0), ("w1h", 1), ("w1h", 0))):
                    last = nc.tensor.matmul(psH[:, k], w[left][:, k * P:(k + 1) * P], hT[:, b, right],
                                            start=(i == 0), stop=(i == 2))
                return last

            def up(g, q, m):
                b = m % 2
                done(pe, s_hT, g)
                done(pe, s_ra, g, 1)
                for k in (0, 1):
                    last = expand(k, b)
                last.then_inc(up2, 1)
                done(pe, s_rv, g, 1)
                for k in (2, 3):
                    last = expand(k, b)
                last.then_inc(s_up, 1)

            def down(g, q, m):
                b = m % 2
                done(pe, s_ra, g)
                done(pe, s_rv, g)
                done(pe, s_st, g, 2)
                for j in range(SLOTS):
                    for k in range(4):
                        last = nc.tensor.matmul(psO[:, b, j * P:(j + 1) * P], r[:, b, k, j * P:(j + 1) * P], w["w2"][:, k, :],
                                                start=(k == 0), stop=(k == 3))
                last.then_inc(s_mm, 1)
            pipelined(pe, [(up, 3), (turn, 1), (down, 4)], NBLK, 4)


def factor_update(nc, a, w, t):
    with ExitStack() as c:
        ph = Phase(nc, c, "D")
        x, ag, xh = ph.sb("x", [P, 4, SLOTS, XW]), ph.sb("ag", [P, 4, SLOTS, D]), ph.sb("xh", [P, 4, SLOTS, D])
        h, hT, aT, xo = ph.sb("h", [P, 2, SLOTS, D]), ph.sb("hT", [P, 2, BLK]), ph.sb("aT", [P, 2, BLK]), ph.sb("xo", [P, 4, SLOTS, XW])
        st, mv, sd = ph.sb("st", [P, 2, SLOTS, 6]), ph.sb("mv", [P, 2, SLOTS, 2]), ph.sb("sd", [P, 2, SLOTS])
        psT, psA, psO = ph.ps("psT", [P, 2, BLK]), ph.ps("psA", [P, 2, BLK]), ph.ps("psO", [P, 2, SLOTS, D])
        loaded, stored = ph.sems("loaded", 4), ph.sems("stored", 4)
        s_h, s_xh, s_ta, s_th, s_aT, s_hT, s_mm, s_st, s_sd, s_xo, s_x3, s_raw, s_inv = ph.step("h", "xh", "ta", "th", "aT", "hT", "mm", "st", "sd", "xo", "x3", "raw", "inv")
        block = new_block(nc, c, ph.all)

        @block.sync
        def _(sp):
            ph.start(sp)

            def load(g, q, m):
                done(sp, s_xh, g, 4)
                done(sp, s_ta, g, 4)
                sp.dma_start(ag[:, m], blocks4(t["sum_src"], g * BLK)).then_inc(loaded[m], 16)
                sp.dma_start(x[:, m], blocks4(t["x2"], g * BLK)).then_inc(loaded[m], 16)

            def store(g, q, m):
                done(sp, s_xo, g)
                sp.dma_start(blocks4(t["x3"], g * BLK), xo[:, m]).then_inc(stored[m], 16)
            pipelined(sp, [(load, 0), (store, 7)], NBLK, 4)
            for m in range(4):
                sp.wait_ge(stored[m], 16 * ((NBLK + 3 - m) // 4))

        @block.gpsimd
        def _(pool):
            def add(g, q, m):
                b = m % 2
                done(pool, s_h, g)
                done(pool, s_st, g, 4)
                nc.gpsimd.tensor_tensor(xh[:, m], x[:, m, :, 0:D], h[:, b], ALU.add).then_inc(s_xh, 1)

            pipelined(pool, [(add, 1)], NBLK, 4)

        @block.vector
        def _(dve):
            def evacuate(g, q, m):
                b = m % 2
                done(dve, s_ta, g)
                done(dve, s_mm, g, 2)
                nc.vector.tensor_copy(aT[:, b], psA[:, b]).then_inc(s_aT, 1)

            def add(g, q, m):
                b = m % 2
                done(dve, s_mm, g)
                done(dve, s_xh, g)
                done(dve, s_sd, g, 2)
                reused(dve, stored[m], q * 16)
                nc.vector.scalar_tensor_tensor(xo[:, m, :, 0:D], psO[:, b], 0.0, xh[:, m], ALU.max, ALU.add).then_inc(s_x3, 1)

            def stats(g, q, m):
                b = m % 2
                done(dve, s_x3, g)
                stats4(ph, xo[:, m], st[:, b]).then_inc(s_raw, 1)

            def aggregate(g, q, m):
                b = m % 2
                done(dve, s_raw, g)
                done(dve, s_xo, g, 2)
                aggregate4(ph, dve, st[:, b], mv[:, b]).then_inc(s_st, 1)

            def finish(g, q, m):
                b = m % 2
                done(dve, s_sd, g)
                nc.vector.reciprocal(xo[:, m, :, D:D + 1], sd[:, b, :].unsqueeze(2)).then_inc(s_inv, 1)

            def offset(g, q, m):
                b = m % 2
                done(dve, s_inv, g)
                nc.vector.scalar_tensor_tensor(xo[:, m, :, D + 1:XW], mv[:, b, :, 0:1], -1.0, xo[:, m, :, D:D + 1], ALU.mult, ALU.mult).then_inc(s_xo, 1)
            pipelined(dve, [(finish, 6), (add, 4), (offset, 6), (evacuate, 2), (stats, 4), (aggregate, 4)], NBLK, 4)

        @block.scalar
        def _(act):
            def node(g, q, m):
                b = m % 2
                act.wait_ge(loaded[m], q * 32 + 32)
                done(act, s_th, g, 2)
                done(act, s_xh, g, 2)
                normalise4(nc, h[:, b], x[:, m], lambda j: x[:, m, j, D:D + 1], lambda j: x[:, m, j, D + 1:XW], ACT.Relu).then_inc(s_h, 1)

            def evacuate(g, q, m):
                b = m % 2
                done(act, s_th, g)
                done(act, s_mm, g, 2)
                nc.scalar.activation(hT[:, b], psT[:, b], ACT.Copy).then_inc(s_hT, 1)

            def deviation(g, q, m):
                b = m % 2
                done(act, s_st, g)
                done(act, s_xo, g, 2)
                nc.scalar.activation(sd[:, b, :], mv[:, b, :, 1], ACT.Sqrt, bias=w["eps"][:, :]).then_inc(s_sd, 1)
            pipelined(act, [(evacuate, 2), (deviation, 5), (node, 0)], NBLK, 4)

        @block.tensor
        def _(pe):
            def turn_sums(g, q, m):
                b = m % 2
                pe.wait_ge(loaded[m], q * 32 + 32)
                done(pe, s_aT, g, 2)
                transposes4(nc, psA[:, b], ag[:, m], w["ident"]).then_inc(s_ta, 1)

            def turn(g, q, m):
                b = m % 2
                done(pe, s_h, g)
                done(pe, s_hT, g, 2)
                transposes4(nc, psT[:, b], h[:, b], w["ident"]).then_inc(s_th, 1)

            def combine(g, q, m):
                b = m % 2
                done(pe, s_hT, g)
                done(pe, s_aT, g)
                done(pe, s_st, g, 2)
                biased4(nc, psO[:, b], w["bc_parts"], w["ones"])
                for j in range(SLOTS):
                    nc.tensor.matmul(psO[:, b, j], hT[:, b, j * P:(j + 1) * P], w["wc"][:, 0, :], start=False, stop=False)
                    last = nc.tensor.matmul(psO[:, b, j], aT[:, b, j * P:(j + 1) * P], w["wc"][:, 1, :], start=False, stop=(j == SLOTS - 1))
                last.then_inc(s_mm, 1)
            pipelined(pe, [(combine, 3), (turn, 1), (turn_sums, 0)], NBLK, 4)


def graph_output(nc, a, w, t, out):
    with ExitStack() as c:
        ph = Phase(nc, c, "E")
        x, ag, xb = ph.sb("x", [P, 4, SLOTS, D]), ph.sb("ag", [P, 4, SLOTS, D]), ph.sb("xb", [P, 2, SLOTS, D])
        aT, zm, e, rz = ph.sb("aT", [P, 2, BLK]), ph.sb("zm", [P, 2, SLOTS, D]), ph.sb("e", [P, 2, SLOTS, D]), ph.sb("rz", [P, 2, SLOTS, D])
        u, y, xo = ph.sb("u", [P, 4, SLOTS, D]), ph.sb("y", [P, 2, SLOTS, D]), ph.sb("xo", [P, 4, SLOTS, D])
        st, mv, ve = ph.sb("st", [P, 2, SLOTS, 6]), ph.sb("mv", [P, 2, SLOTS, 2]), ph.sb("ve", [P, 2, SLOTS])
        rs, nm, half = ph.sb("rs", [P, 2, SLOTS]), ph.sb("nm", [P, 2, SLOTS]), ph.sb("half", [P, SLOTS])
        psT, psO = ph.ps("psT", [P, 2, BLK]), ph.ps("psO", [P, 2, SLOTS, D])
        loaded, loaded_x, stored = ph.sems("loaded", 4), ph.sems("loaded_x", 4), ph.sems("stored", 4)
        s_xb, s_tr, s_aT, s_mm, s_zm, s_e, s_st, s_ve, s_rs, s_nm, s_y, s_xo, s_u, s_raw, s_yg = ph.step(
            "xb", "tr", "aT", "mm", "zm", "e", "st", "ve", "rs", "nm", "y", "xo", "u", "raw", "yg")
        s_half = ph.sem("half")
        block = new_block(nc, c, ph.all)

        @block.sync
        def _(sp):
            ph.start(sp)

            def load(g, q, m):
                done(sp, s_tr, g, 4)
                sp.dma_start(ag[:, m], blocks4(t["sum_src"], g * BLK)).then_inc(loaded[m], 16)

            def load_x(g, q, m):
                done(sp, s_xb, g, 4)
                sp.dma_start(x[:, m], blocks4(t["x3"], g * BLK)[:, :, 0:D]).then_inc(loaded_x[m], 16)

            def store(g, q, m):
                done(sp, s_xo, g)
                sp.dma_start(blocks4(out, g * BLK), xo[:, m]).then_inc(stored[m], 16)
            pipelined(sp, [(load, 0), (load_x, 4), (store, 8)], NBLK, 4)
            for m in range(4):
                sp.wait_ge(stored[m], 16 * ((NBLK + 3 - m) // 4))

        @block.gpsimd
        def _(pool):
            nc.gpsimd.memset(half[:, :], -0.5).then_inc(s_half, 1)
            pool.wait_ge(s_half, 1)

            def shift(g, q, m):
                b = m % 2
                pool.wait_ge(loaded_x[m], q * 16 + 16)
                done(pool, s_xo, g, 2)
                nc.gpsimd.tensor_tensor(xb[:, b], x[:, m], w["be3"][:, :].unsqueeze(1).to_broadcast([P, SLOTS, D]), ALU.add).then_inc(s_xb, 1)

            def power(g, q, m):
                b = m % 2
                done(pool, s_st, g)
                done(pool, s_rs, g, 2)
                ph.apart(pool)
                nc.gpsimd.tensor_scalar(ve[:, b, :], mv[:, b, :, 1], LN_EPS, None, ALU.add).then_inc(s_ve, 1)
                done(pool, s_ve, g)
                done(pool, s_nm, g, 2)
                done(pool, s_y, g, 2)
                nc.gpsimd.tensor_tensor(rs[:, b, :], ve[:, b, :], half[:, :], ALU.pow).then_inc(s_rs, 1)

            pipelined(pool, [(shift, 6), (power, 5)], NBLK, 4)

        @block.vector
        def _(dve):
            def elu(g, q, m):
                b = m % 2
                done(dve, s_e, g)
                done(dve, s_y, g, 4)
                nc.vector.scalar_tensor_tensor(u[:, m], e[:, b], -1.0, rz[:, b], ALU.add, ALU.add).then_inc(s_u, 1)

            def stats(g, q, m):
                b = m % 2
                done(dve, s_u, g)
                done(dve, s_st, g, 2)
                stats4(ph, u[:, m], st[:, b]).then_inc(s_raw, 1)

            def aggregate(g, q, m):
                b = m % 2
                done(dve, s_raw, g)
                done(dve, s_nm, g, 2)
                aggregate4(ph, dve, st[:, b], mv[:, b]).then_inc(s_st, 1)

            def scale(g, q, m):
                b = m % 2
                done(dve, s_rs, g)
                nc.vector.scalar_tensor_tensor(nm[:, b, :], mv[:, b, :, 0], -1.0, rs[:, b, :], ALU.mult, ALU.mult).then_inc(s_nm, 1)

            def gain(g, q, m):
                b = m % 2
                done(dve, s_y, g)
                nc.vector.tensor_tensor(y[:, b], y[:, b], w["g3"][:, :].unsqueeze(1).to_broadcast([P, SLOTS, D]), ALU.mult).then_inc(s_yg, 1)

            def add(g, q, m):
                b = m % 2
                done(dve, s_yg, g)
                done(dve, s_xb, g)
                reused(dve, stored[m], q * 16)
                nc.vector.tensor_tensor(xo[:, m], y[:, b], xb[:, b], ALU.add).then_inc(s_xo, 1)
            pipelined(dve, [(scale, 6), (gain, 7), (elu, 4), (add, 7), (stats, 4), (aggregate, 4)], NBLK, 4)

        @block.scalar
        def _(act):
            def evacuate(g, q, m):
                b = m % 2
                done(act, s_tr, g)
                done(act, s_mm, g, 2)
                nc.scalar.activation(aT[:, b], psT[:, b], ACT.Copy).then_inc(s_aT, 1)

            def exponential(g, q, m):
                b = m % 2
                done(act, s_mm, g)
                done(act, s_st, g, 2)
                nc.scalar.activation(zm[:, b], psO[:, b], ACT.Relu, scale=-1.0).then_inc(s_zm, 1)
                nc.scalar.activation(rz[:, b], psO[:, b], ACT.Relu)
                done(act, s_zm, g)
                nc.scalar.activation(e[:, b], zm[:, b], ACT.Exp, scale=-1.0).then_inc(s_e, 1)

            def normalise(g, q, m):
                b = m % 2
                done(act, s_nm, g)
                done(act, s_xo, g, 2)
                normalise4(nc, y[:, b], u[:, m], lambda j: rs[:, b, j:j + 1], lambda j: nm[:, b, j:j + 1], ACT.Identity).then_inc(s_y, 1)
            pipelined(act, [(evacuate, 1), (exponential, 3), (normalise, 6)], NBLK, 4)

        @block.tensor
        def _(pe):
            def turn(g, q, m):
                b = m % 2
                pe.wait_ge(loaded[m], q * 16 + 16)
                done(pe, s_aT, g, 2)
                transposes4(nc, psT[:, b], ag[:, m], w["ident"]).then_inc(s_tr, 1)

            def project(g, q, m):
                b = m % 2
                done(pe, s_aT, g)
                done(pe, s_e, g, 2)
                biased4(nc, psO[:, b], w["b3_parts"], w["ones"])
                for j in range(SLOTS):
                    last = nc.tensor.matmul(psO[:, b, j], aT[:, b, j * P:(j + 1) * P], w["w3"][:, :], start=False, stop=(j == SLOTS - 1))
                last.then_inc(s_mm, 1)
            pipelined(pe, [(turn, 0), (project, 1)], NBLK, 4)


class Edges(Phase):

    def __init__(self, nc, ctx, w, name, table, key, first, second, widths):
        super().__init__(nc, ctx, name)
        self.table, self.key, self.fields = table, key, (first, second)
        self.rec, self.nxt = self.sb("rec", [P, 4, SLOTS, 4]), self.sb("nxt", [P, 4, SLOTS])
        self.index, self.goal = self.sb("index", [P, 4, 2, SLOTS], I32), self.sb("goal", [P, 4, SLOTS], I32)
        self.same = self.sb("same", [P, 4, SLOTS])
        self.got = [self.sb(f"got{k}", [P, 4, SLOTS, n]) for k, n in enumerate(widths)]
        self.kr, self.flag = self.sb("kr", [P, 2, BLK + 1]), self.sb("flag", [P, 2, BLK])
        self.sums, self.rows = self.sb("sums", [P, 2, BLK]), self.sb("rows", [P, 4, SLOTS, D])
        self.psK, self.psB = self.ps("psK", [P, BLK]), self.ps("psB", [P, BLK])
        self.loaded, self.gathered, self.scattered = self.sems("loaded", 4), self.dma(w, 4), self.dma(w, 4)
        self.own, self.init, self.zeroed = self.sem("own"), self.sem("init"), self.sem("zeroed")
        self.s_idx, self.s_goal, self.s_k, self.s_kr, self.s_flag, self.s_msg, self.s_scan, self.s_back, self.s_rows = self.step(
            "idx", "goal", "k", "kr", "flag", "msg", "scan", "back", "rows")

    def load(self, sp, users):
        def stage(g, q, m):
            for s in users:
                done(sp, s, g, 4)
            sp.dma_start(self.rec[:, m], self.table[bass.ds(g * BLK, BLK), 0:REC].rearrange("(j p) f -> p j f", p=P)).then_inc(self.loaded[m], 16)
            sp.dma_start(self.nxt[:, m], self.table[bass.ds(g * BLK + 1, BLK), self.key:self.key + 1].rearrange("(j p) f -> p (j f)", p=P),
                         allow_slow_non_contiguous=True).then_inc(self.loaded[m], 16)
        return stage

    def zero(self, sp, table, zeros):
        rows = NPAD // GROUPS

        def stage(g, q, m):
            sp.dma_start(table[bass.ds(g * rows, rows), :].rearrange("(p j) d -> p (j d)", p=P), zeros[:, :]).then_inc(self.zeroed, 16)
        return stage

    def indices(self, dve):
        def stage(g, q, m):
            dve.wait_ge(self.loaded[m], q * 32 + 32)
            reused(dve, self.gathered[m], q * 16 * SLOTS * sum(f is not None for f in self.fields))
            for k, field in enumerate(self.fields):
                if field is not None:
                    last = self.nc.vector.tensor_copy(self.index[:, m, k], self.rec[:, m, :, field])
            last.then_inc(self.s_idx, 1)
        return stage

    def goals(self, dve):
        nc, tally = self.nc, Tally(dve, self.own, 1)

        def stage(g, q, m):
            reused(dve, self.scattered[m], q * 16 * SLOTS)
            tally.begin(g)
            tally.inc(nc.vector.tensor_tensor(self.same[:, m], self.nxt[:, m], self.rec[:, m, :, self.key], ALU.is_equal))
            tally.wait()
            nc.vector.scalar_tensor_tensor(self.goal[:, m], self.same[:, m], SKIP, self.rec[:, m, :, self.key],
                                           ALU.mult, ALU.add).then_inc(self.s_goal, 1)
            tally.end()
        return stage

    def flags(self, dve, user):
        def stage(g, q, m):
            b = m % 2
            done(dve, self.s_kr, g)
            done(dve, user, g, 2)
            self.nc.vector.tensor_tensor(self.flag[:, b], self.kr[:, b, 1:BLK + 1], self.kr[:, b, 0:BLK], ALU.is_equal).then_inc(self.s_flag, 1)
        return stage

    def clear(self, dve):
        self.nc.vector.memset(self.kr[:, 1, BLK:BLK + 1], -1.0)
        self.nc.vector.memset(self.sums[:, 1, BLK - 1:BLK], 0.0).then_inc(self.init, 1)
        dve.wait_ge(self.init, 1)

    def evacuate(self, dve):
        def stage(g, q, m):
            done(dve, self.s_back, g)
            reused(dve, self.scattered[m], q * 16 * SLOTS)
            self.nc.vector.tensor_copy(self.rows[:, m], self.psB[:, :].rearrange("p (j d) -> p j d", j=SLOTS)).then_inc(self.s_rows, 1)
        return stage

    def evacuate_act(self, act):
        def stage(g, q, m):
            done(act, self.s_back, g)
            reused(act, self.scattered[m], q * 16 * SLOTS)
            self.nc.scalar.activation(self.rows[:, m], self.psB[:, :].rearrange("p (j d) -> p j d", j=SLOTS), ACT.Copy).then_inc(self.s_rows, 1)
        return stage

    def run_pool(self, pool, tables, target, users):
        nc = self.nc
        limits = [pool.to_reg(x.shape[0] - 1) for x in tables]
        last = pool.to_reg(NPAD - 1)

        def gather(g, q, m):
            done(pool, self.s_idx, g)
            for s in users:
                done(pool, s, g, 4)
            self.apart(pool)
            for k, x in enumerate(tables):
                for j in range(SLOTS):
                    nc.gpsimd.indirect_dma_start(self.got[k][:, m, j, :], None, x,
                                                 bass.IndirectOffsetOnAxis(ap=self.index[:, m, k, j:j + 1], axis=0),
                                                 bounds_check=limits[k], oob_is_err=True).then_inc(self.gathered[m], 16)

        def scatter(g, q, m):
            done(pool, self.s_rows, g)
            done(pool, self.s_goal, g)
            self.apart(pool)
            for j in range(SLOTS):
                nc.gpsimd.indirect_dma_start(target, bass.IndirectOffsetOnAxis(ap=self.goal[:, m, j:j + 1], axis=0),
                                             self.rows[:, m, j, :], None, bounds_check=last, oob_is_err=False
                                             ).then_inc(self.scattered[m], 16)
        pipelined(pool, [(gather, 0), (scatter, 6)], GROUPS, 4)
        for m in range(4):
            pool.wait_ge(self.gathered[m], 16 * SLOTS * len(tables) * ((GROUPS + 3 - m) // 4))
            pool.wait_ge(self.scattered[m], 16 * SLOTS * ((GROUPS + 3 - m) // 4))

    def arrived(self, eng, q, m, tables):
        eng.wait_ge(self.gathered[m], (q + 1) * 16 * SLOTS * tables)

    def key_rows(self, pe):
        def stage(g, q, m):
            pe.wait_ge(self.loaded[m], q * 32 + 32)
            done(pe, self.s_kr, g, 1)
            for j in range(SLOTS):
                last = self.nc.tensor.transpose(self.psK[:, j * P:(j + 1) * P],
                                                self.rec[:, m, j, self.key:self.key + 1].to_broadcast([P, P]), self.ident[:, :])
            last.then_inc(self.s_k, 1)
        return stage

    def back(self, pe):
        def stage(g, q, m):
            done(pe, self.s_scan, g)
            done(pe, self.s_rows, g, 1)
            for j in range(SLOTS):
                last = self.nc.tensor.transpose(self.psB[:, j * P:(j + 1) * P], self.sums[:, m % 2, j * P:(j + 1) * P], self.ident[:, :])
            last.then_inc(self.s_back, 1)
        return stage

    def key_copy(self, act):
        def stage(g, q, m):
            b = m % 2
            done(act, self.s_k, g)
            done(act, self.s_kr, g, 1)
            done(act, self.s_flag, g, 2)
            act.wait_ge(self.init, 1)
            self.nc.scalar.activation(self.kr[:, b, 0:1], self.kr[:, 1 - b, BLK:BLK + 1], ACT.Copy)
            self.nc.scalar.activation(self.kr[:, b, 1:BLK + 1], self.psK[:, :], ACT.Copy).then_inc(self.s_kr, 1)
        return stage


def message_edges(nc, a, w, t, layer):
    with ExitStack() as c:
        if layer == 1:
            ph = Edges(nc, c, w, "F1", t["by_dst"], 1, 0, None, [XW, D])
            tables, ordered, target = [t["x1"]], t["by_dst"], t["sum_dst"]
        elif layer == 2:
            ph = Edges(nc, c, w, "F2", t["by_src"], 0, 0, None, [XW, D])
            tables, ordered, target = [t["x2"]], t["factors"], t["sum_src"]
        else:
            ph = Edges(nc, c, w, "F3", t["by_src"], 0, 1, None, [XW])
            tables, ordered, target = [t["x3"]], None, t["sum_src"]
        ph.ident = w["ident"]
        first = REC if layer == 1 else 0
        fetched = ph.sems("fetched", 4)
        h = ph.sb("h", [P, 2, SLOTS, D])
        bT, hT, msg = ph.sb("bT", [P, 2, BLK]), ph.sb("hT", [P, 2, BLK]), ph.sb("msg", [P, 2, BLK])
        zc, zb, ex, den, num = (ph.sb(n, [P, 2, BLK]) for n in ("zc", "zb", "ex", "den", "num"))
        psE, psH, psZ = ph.ps("psE", [P, BLK]), ph.ps("psH", [P, BLK]), ph.ps("psZ", [P, 2, BLK])
        s_h, s_hw, s_te, s_bT, s_th, s_hT, s_z, s_zb, s_zc, s_ex = ph.step("h", "hw", "te", "bT", "th", "hT", "z", "zb", "zc", "ex")
        ch = ph.sem("ch")
        block = new_block(nc, c, ph.all)

        @block.sync
        def _(sp):
            ph.start(sp)

            def second(g, q, m):
                done(sp, s_te, g, 4)
                ph.apart(sp)
                sp.dma_start(ph.got[1][:, m], ordered[bass.ds(g * BLK, BLK), first:].rearrange("(j p) d -> p j d", p=P)).then_inc(fetched[m], 16)
            stages = [(ph.load(sp, [ph.s_idx, ph.s_goal, ph.s_k] + ([s_hw] if layer == 3 else [])), 0)]
            if layer < 3:
                stages.append((second, 0))
            if layer == 1:
                stages.append((ph.zero(sp, t["sum_src"], w["zeros"]), 0))
            pipelined(sp, stages, GROUPS, 4)
            if layer == 1:
                sp.wait_ge(ph.zeroed, 16 * GROUPS)

        @block.gpsimd
        def _(pool):
            ph.run_pool(pool, tables, target, [s_h])

        @block.vector
        def _(dve):
            ph.clear(dve)
            c1 = Tally(dve, ch, 4)

            def operand(g, q, m):
                done(dve, s_te, g)
                done(dve, s_z, g, 2)
                nc.vector.tensor_copy(bT[:, m % 2], psE[:, :]).then_inc(s_bT, 1)

            def weigh(g, q, m):
                done(dve, s_h, g)
                nc.vector.tensor_tensor(h[:, m % 2], h[:, m % 2], ph.rec[:, m, :, 3:4].to_broadcast([P, SLOTS, D]), ALU.mult).then_inc(s_hw, 1)

            def clip(g, q, m):
                done(dve, s_zb, g)
                done(dve, s_ex, g, 2)
                nc.vector.tensor_scalar(zc[:, m % 2], zb[:, m % 2], 30.0, None, ALU.min).then_inc(s_zc, 1)

            def mish(g, q, m):
                b = m % 2
                done(dve, s_ex, g)
                done(dve, ph.s_scan, g, 1)
                c1.begin(g)
                c1.inc(nc.vector.scalar_tensor_tensor(num[:, b], ex[:, b], 2.0, ex[:, b], ALU.add, ALU.mult))
                c1.wait()
                c1.inc(nc.vector.tensor_scalar(den[:, b], num[:, b], 2.0, None, ALU.add))
                c1.inc(nc.vector.tensor_tensor(num[:, b], num[:, b], zb[:, b], ALU.mult))
                c1.wait()
                c1.inc(nc.vector.reciprocal(den[:, b], den[:, b]))
                c1.wait()
                nc.vector.tensor_tensor(msg[:, b], num[:, b], den[:, b], ALU.mult).then_inc(ph.s_msg, 1)
                c1.end()

            def scan(g, q, m):
                b = m % 2
                done(dve, ph.s_msg if layer < 3 else s_z, g)
                done(dve, ph.s_flag, g)
                done(dve, ph.s_scan, g, 1)
                done(dve, ph.s_back, g, 2)
                nc.vector.tensor_tensor_scan(ph.sums[:, b], ph.flag[:, b], msg[:, b] if layer < 3 else psZ[:, b],
                                             ph.sums[:, 1 - b, BLK - 1:BLK], ALU.mult, ALU.add).then_inc(ph.s_scan, 1)
            index, goal, flags, evacuate = ph.indices(dve), ph.goals(dve), ph.flags(dve, ph.s_scan), ph.evacuate(dve)
            if layer == 1:
                stages = [(index, 0), (clip, 3), (flags, 3), (goal, 3), (mish, 4), (scan, 4)]
            elif layer == 2:
                stages = [(index, 0), (operand, 2), (scan, 4), (evacuate, 5), (flags, 3), (goal, 3)]
            else:
                stages = [(index, 0), (weigh, 2), (scan, 4), (evacuate, 5), (flags, 3), (goal, 3)]
            pipelined(dve, stages, GROUPS, 4)

        @block.scalar
        def _(act):
            def node(g, q, m):
                b = m % 2
                ph.arrived(act, q, m, 1)
                x = ph.got[0][:, m]
                done(act, {1: s_z, 2: s_th, 3: s_z}[layer], g, 2)
                normalise4(nc, h[:, b], x, lambda j: x[:, j, D:D + 1], lambda j: x[:, j, D + 1:XW], ACT.Relu).then_inc(s_h, 1)

            def argument(g, q, m):
                b = m % 2
                done(act, s_z, g)
                done(act, ph.s_msg, g, 2)
                nc.scalar.activation(zb[:, b], psZ[:, b], ACT.Identity, bias=w["bee"][:, :]).then_inc(s_zb, 1)

            def exponential(g, q, m):
                b = m % 2
                done(act, s_zc, g)
                done(act, ph.s_msg, g, 2)
                nc.scalar.activation(ex[:, b], zc[:, b], ACT.Exp).then_inc(s_ex, 1)

            def evacuate(g, q, m):
                done(act, s_th, g)
                done(act, s_z, g, 2)
                nc.scalar.activation(hT[:, m % 2], psH[:, :], ACT.Copy).then_inc(s_hT, 1)

            def message(g, q, m):
                done(act, s_z, g)
                done(act, ph.s_scan, g, 2)
                nc.scalar.activation(msg[:, m % 2], psZ[:, m % 2], ACT.Relu, bias=w["bm"][:, :]).then_inc(ph.s_msg, 1)
            def operand(g, q, m):
                done(act, s_te, g)
                done(act, s_z, g, 2)
                nc.scalar.activation(bT[:, m % 2], psE[:, :], ACT.Copy).then_inc(s_bT, 1)
            keys = ph.key_copy(act)
            if layer == 1:
                stages = [(operand, 2), (exponential, 4), (argument, 3), (keys, 3), (node, 1), (ph.evacuate_act(act), 5)]
            elif layer == 2:
                stages = [(evacuate, 2), (keys, 3), (message, 3), (node, 1)]
            else:
                stages = [(keys, 3), (node, 1)]
            pipelined(act, stages, GROUPS, 4)

        @block.tensor
        def _(pe):
            def turn(g, q, m):
                pe.wait_ge(fetched[m], q * 16 + 16)
                done(pe, s_bT, g, 1)
                transposes4(nc, psE[:, :], ph.got[1][:, m], w["ident"]).then_inc(s_te, 1)

            def turn_node(g, q, m):
                done(pe, s_h, g)
                done(pe, s_hT, g, 1)
                transposes4(nc, psH[:, :], h[:, m % 2], w["ident"]).then_inc(s_th, 1)

            def product1(g, q, m):
                b = m % 2
                done(pe, s_bT, g)
                done(pe, s_h, g)
                done(pe, s_zb, g, 2)
                nc.tensor.matmul(psZ[:, b], w["we"][:, :], bT[:, b], start=True, stop=False)
                for j in range(SLOTS):
                    last = nc.tensor.matmul(psZ[:, b, j * P:(j + 1) * P], h[:, b, j, :], w["ident"][:, :], start=False,
                                            stop=(j == SLOTS - 1))
                last.then_inc(s_z, 1)

            def product2(g, q, m):
                b = m % 2
                done(pe, s_bT, g)
                done(pe, s_hT, g)
                done(pe, ph.s_msg, g, 2)
                nc.tensor.matmul(psZ[:, b], w["wm"][:, 0, :], hT[:, b], start=True, stop=False)
                nc.tensor.matmul(psZ[:, b], w["wm"][:, 1, :], bT[:, b], start=False, stop=True).then_inc(s_z, 1)

            def turn_weighed(g, q, m):
                done(pe, s_hw, g)
                done(pe, ph.s_scan, g, 2)
                transposes4(nc, psZ[:, m % 2], h[:, m % 2], w["ident"]).then_inc(s_z, 1)
            keys, back = ph.key_rows(pe), ph.back(pe)
            if layer == 1:
                stages = [(product1, 2), (keys, 2), (turn, 1), (back, 5)]
            elif layer == 2:
                stages = [(back, 5), (product2, 3), (turn_node, 2), (keys, 2), (turn, 1)]
            else:
                stages = [(back, 5), (turn_weighed, 3), (keys, 2)]
            pipelined(pe, stages, GROUPS, 4)


def attention_edges(nc, a, w, t):
    with ExitStack() as c:
        ph = Edges(nc, c, w, "F0", t["by_dst"], 1, 0, 1, [AW, AW])
        ph.ident = w["ident"]
        pre, lg, v = ph.sb("pre", [P, 2, 2, SLOTS, HEADS]), ph.sb("lg", [P, 4, 2, SLOTS, HEADS]), ph.sb("v", [P, 2, SLOTS, HEADS])
        pen, m_ = ph.sb("pen", [HEADS, 2, BLK]), ph.sb("m", [HEADS, 2, BLK + 1])
        d, r, dsum = ph.sb("d", [HEADS, 2, 2, BLK]), ph.sb("r", [HEADS, 4, BLK]), ph.sb("dsum", [HEADS, 2, BLK])
        lm, p_ = ph.sb("lm", [P, 2, 2, SLOTS, HEADS]), ph.sb("p", [P, 4, 2, SLOTS, HEADS])
        phs, rS = ph.sb("phs", [P, 2, SLOTS, D]), ph.sb("rS", [P, 2, BLK])
        dn, rd, t1, t2 = ph.sb("dn", [P, 2, SLOTS, HEADS]), ph.sb("rd", [P, 2, SLOTS, HEADS]), ph.sb("t1", [P, 4, SLOTS, D]), ph.sb("t2", [P, 2, SLOTS, D])
        psV, psP, psR, psM = ph.ps("psV", [P, BLK]), ph.ps("psP", [P, BLK]), ph.ps("psR", [P, BLK]), ph.ps("psM", [P, BLK])
        psS, psD = ph.ps("psS", [P, SLOTS, HEADS]), ph.ps("psD", [P, SLOTS, HEADS])
        s_v, s_vT, s_m, s_d, s_r, s_mT, s_lm, s_p, s_ph, s_mm, s_rS = ph.step("v", "vT", "m", "d", "r", "mT", "lm", "p", "phs", "mm", "rS")
        ch1, ch2, ch3 = ph.sems("ch", 3)
        block = new_block(nc, c, ph.all)

        def heads(x):
            return x.unsqueeze(3).to_broadcast([P, SLOTS, HEADS, HD])

        def split(x):
            return x.rearrange("p j (h f) -> p j h f", h=HEADS)

        @block.sync
        def _(sp):
            ph.start(sp)
            pipelined(sp, [(ph.load(sp, [ph.s_idx, ph.s_goal, ph.s_k]), 0), (ph.zero(sp, t["sum_dst"], w["zeros"]), 0)], GROUPS, 4)
            sp.wait_ge(ph.zeroed, 16 * GROUPS)

        @block.gpsimd
        def _(pool):
            ph.run_pool(pool, [t["att"], t["att"]], t["gat"], [s_ph])

        @block.vector
        def _(dve):
            nc.vector.memset(m_[:, 1, BLK:BLK + 1], 0.0)
            nc.vector.memset(dsum[:, 1, BLK - 1:BLK], 0.0)
            ph.clear(dve)
            c1, c2, c3 = Tally(dve, ch1, 2), Tally(dve, ch2, 2), Tally(dve, ch3, 2)

            def logits(g, q, m):
                b = m % 2
                ph.arrived(dve, q, m, 2)
                done(dve, s_vT, g, 2)
                done(dve, s_lm, g, 2)
                c1.begin(g)
                ga, gb = ph.got[0][:, m], ph.got[1][:, m]
                nc.vector.tensor_tensor(pre[:, b, 0], ga[:, :, D:D + HEADS], gb[:, :, D + HEADS:AW], ALU.add)
                c1.inc(nc.vector.tensor_tensor(pre[:, b, 1], gb[:, :, D:D + HEADS], gb[:, :, D + HEADS:AW], ALU.add))
                c1.wait()
                c1.inc(nc.vector.scalar_tensor_tensor(lg[:, m].rearrange("p k j h -> p (k j h)"), pre[:, b].rearrange("p k j h -> p (k j h)"), 0.2,
                                                      pre[:, b].rearrange("p k j h -> p (k j h)"), ALU.mult, ALU.max))
                c1.wait()
                nc.vector.tensor_tensor(v[:, b], lg[:, m, 0], lg[:, m, 1], ALU.max).then_inc(s_v, 1)
                c1.end()

            def maximum(g, q, m):
                b = m % 2
                done(dve, ph.s_flag, g)
                done(dve, s_d, g, 2)
                c2.begin(g)
                c2.inc(nc.vector.tensor_scalar(pen[:, b], ph.flag[0:HEADS, b], 1.0, -LOWEST, ALU.subtract, ALU.mult))
                done(dve, s_vT, g)
                done(dve, s_mT, g, 2)
                done(dve, s_m, g, 1)
                c2.wait()
                nc.vector.tensor_copy(m_[:, b, 0:1], m_[:, 1 - b, BLK:BLK + 1])
                nc.vector.tensor_tensor_scan(m_[:, b, 1:BLK + 1], pen[:, b], psV[0:HEADS, :], m_[:, 1 - b, BLK:BLK + 1],
                                             ALU.add, ALU.max).then_inc(s_m, 1)
                done(dve, s_m, g)
                done(dve, s_r, g, 2)
                c2.inc(nc.vector.tensor_tensor(d[:, b, 0], m_[:, b, 0:BLK], m_[:, b, 1:BLK + 1], ALU.subtract))
                c2.wait()
                nc.vector.tensor_tensor(d[:, b, 1], d[:, b, 0], pen[:, b], ALU.add).then_inc(s_d, 1)
                c2.end()

            def exponents(g, q, m):
                b = m % 2
                done(dve, s_mT, g)
                done(dve, s_p, g, 2)
                for k in range(2):
                    last = nc.vector.tensor_tensor(lm[:, b, k], lg[:, m, k], psS[:, :, :], ALU.subtract)
                last.then_inc(s_lm, 1)

            def weighed(g, q, m):
                b = m % 2
                done(dve, s_p, g)
                done(dve, s_mm, g, 2)
                done(dve, ph.s_rows, g, 4)
                nc.vector.tensor_tensor(split(t1[:, m]), split(ph.got[1][:, m, :, 0:D]), heads(p_[:, m, 1]), ALU.mult)
                nc.vector.tensor_tensor(split(phs[:, b]), split(ph.got[0][:, m, :, 0:D]), heads(p_[:, m, 0]), ALU.mult).then_inc(s_ph, 1)

            def scan(g, q, m):
                b = m % 2
                done(dve, s_mm, g)
                done(dve, s_rS, g)
                done(dve, ph.s_scan, g, 1)
                done(dve, ph.s_back, g, 2)
                nc.vector.tensor_tensor_scan(dsum[:, b], r[:, m], psP[0:HEADS, :], dsum[:, 1 - b, BLK - 1:BLK], ALU.mult, ALU.add)
                nc.vector.tensor_tensor_scan(ph.sums[:, b], rS[:, b], psM[:, :], ph.sums[:, 1 - b, BLK - 1:BLK],
                                             ALU.mult, ALU.add).then_inc(ph.s_scan, 1)

            def finish(g, q, m):
                b = m % 2
                done(dve, ph.s_back, g)
                done(dve, ph.s_rows, g, 1)
                reused(dve, ph.scattered[m], q * 16 * SLOTS)
                c3.begin(g)
                nc.vector.tensor_tensor(dn[:, b], psD[:, :, :], p_[:, m, 1], ALU.add)
                c3.inc(nc.vector.tensor_tensor(t2[:, b], t1[:, m], ph.psB[:, :].rearrange("p (j d) -> p j d", j=SLOTS), ALU.add))
                c3.wait()
                c3.inc(nc.vector.reciprocal(rd[:, b], dn[:, b]))
                c3.wait()
                nc.vector.tensor_tensor(split(ph.rows[:, m]), split(t2[:, b]), heads(rd[:, b]), ALU.mult).then_inc(ph.s_rows, 1)
                c3.end()
            pipelined(dve, [(ph.indices(dve), 0), (exponents, 3), (finish, 5), (logits, 1), (ph.flags(dve, s_d), 2), (maximum, 2), (weighed, 3),
                            (ph.goals(dve), 3), (scan, 4)], GROUPS, 4)

        @block.scalar
        def _(act):
            def decay(g, q, m):
                b = m % 2
                done(act, s_d, g)
                done(act, ph.s_scan, g, 4)
                nc.scalar.activation(r[:, m], d[:, b, 1], ACT.Exp).then_inc(s_r, 1)

            def weights(g, q, m):
                b = m % 2
                done(act, s_lm, g)
                done(act, ph.s_rows, g, 4)
                nc.scalar.activation(p_[:, m], lm[:, b], ACT.Exp).then_inc(s_p, 1)

            def spread(g, q, m):
                done(act, s_mm, g)
                done(act, ph.s_scan, g, 2)
                nc.scalar.activation(rS[:, m % 2], psR[:, :], ACT.Copy).then_inc(s_rS, 1)
            pipelined(act, [(ph.key_copy(act), 2), (weights, 3), (decay, 3), (spread, 4)], GROUPS, 4)

        @block.tensor
        def _(pe):
            def turn_logits(g, q, m):
                done(pe, s_v, g)
                done(pe, s_m, g, 1)
                ph.apart(pe)
                for j in range(SLOTS):
                    last = nc.tensor.transpose(psV[0:HEADS, j * P:(j + 1) * P], v[:, m % 2, j, :], w["ident"][:, :])
                last.then_inc(s_vT, 1)

            def turn_maximum(g, q, m):
                done(pe, s_m, g)
                done(pe, s_lm, g, 1)
                ph.apart(pe)
                for j in range(SLOTS):
                    last = nc.tensor.transpose(psS[:, j, :], m_[:, m % 2, 1 + j * P:1 + (j + 1) * P], w["ident"][0:HEADS, 0:HEADS])
                last.then_inc(s_mT, 1)

            def turn_rows(g, q, m):
                b = m % 2
                done(pe, s_r, g)
                done(pe, ph.s_scan, g, 1)
                done(pe, s_rS, g, 1)
                nc.tensor.matmul(psR[:, :], w["expand"][:, :], r[:, m], start=True, stop=True)
                done(pe, s_ph, g)
                transposes4(nc, psM[:, :], phs[:, b], w["ident"])
                for j in range(SLOTS):
                    last = nc.tensor.transpose(psP[0:HEADS, j * P:(j + 1) * P], p_[:, m, 0, j, :], w["ident"][:, :])
                last.then_inc(s_mm, 1)

            def back(g, q, m):
                done(pe, ph.s_scan, g)
                done(pe, ph.s_rows, g, 1)
                for j in range(SLOTS):
                    nc.tensor.transpose(ph.psB[:, j * P:(j + 1) * P], ph.sums[:, m % 2, j * P:(j + 1) * P], w["ident"][:, :])
                    last = nc.tensor.transpose(psD[:, j, :], dsum[:, m % 2, j * P:(j + 1) * P], w["ident"][0:HEADS, 0:HEADS])
                last.then_inc(ph.s_back, 1)
            pipelined(pe, [(back, 5), (turn_rows, 4), (turn_logits, 1), (ph.key_rows(pe), 1), (turn_maximum, 2)], GROUPS, 4)


def program(nc, a, out):
    t = tables(nc)
    with ExitStack() as c:
        def sb(name, shape):
            return c.enter_context(nc.sbuf_tensor("k_" + name, shape, F32))
        w = {n: sb(n, [P, k]) for n, k in (
            ("ident", P), ("hmask", HEADS), ("wl", AW), ("proj", D), ("c0", D), ("g0", D), ("be0", D), ("we", D), ("bee", 1),
            ("eps1", 1), ("eps", 1), ("one", 1), ("zeros", NPAD // GROUPS // P * D), ("w1", HID), ("b1", 4), ("b2", D), ("bm", 1), ("bc", D), ("w3", D), ("b3", D),
            ("g3", D), ("be3", D))}
        w["expand"] = sb("expand", [HEADS, P])
        for n, k in (("ones", P), ("c0_parts", D), ("bc_parts", D), ("b3_parts", D)):
            w[n] = c.enter_context(nc.sbuf_tensor("k_" + n, [3, k], BF16))
        w["w2"], w["wm"], w["wc"] = sb("w2", [P, 4, D]), sb("wm", [P, 2, D]), sb("wc", [P, 2, D])
        w["w1h"], w["w1l"] = (c.enter_context(nc.sbuf_tensor("k_" + n, [P, HID], F32R)) for n in ("w1h", "w1l"))
        w["dma"] = [c.enter_context(nc.semaphore(f"pool_dma{k}")) for k in range(8)]
        s = {n: sb(n, shape) for n, shape in (("iota", [P, LO]), ("iotap", [P, 4]), ("tri", [P, 3, P]), ("rec", [P, TILES, 4]),
                                              ("key", [P, 2, 3, TILES]), ("start", [P, 2, 2, LO]))}
        s["ints"] = c.enter_context(nc.sbuf_tensor("k_ints", [P, 2, TILES], I32))
        s["iotab"] = c.enter_context(nc.sbuf_tensor("k_iotab", [P, LO], BF16))
        prepare(nc, a, w, s)
        count_keys(nc, a, w, t, s)
        attention_inputs(nc, a, w, t, s)
        attention_edges(nc, a, w, t)
        attention_outputs(nc, a, w, t, s)
        message_edges(nc, a, w, t, 1)
        mlp(nc, a, w, t)
        message_edges(nc, a, w, t, 2)
        factor_update(nc, a, w, t)
        message_edges(nc, a, w, t, 3)
        graph_output(nc, a, w, t, out)


def kernel(**inputs):
    import numpy as np
    import concourse.bacc as bacc
    from concourse.bass_utils import run_bass_kernel_spmd

    v = {k: np.asarray(x) for k, x in inputs.items()}

    def rows(x, count, fill=0):
        full = np.full((count,) + x.shape[1:], fill, x.dtype)
        full[:x.shape[0]] = x
        return full

    def every(x):
        return np.ascontiguousarray(np.broadcast_to(x.reshape(1, -1), (P, x.size)))

    def tiles(x):
        return np.ascontiguousarray(np.moveaxis(x.reshape((TILES, P) + x.shape[1:]), 0, 1))
    i = np.arange(P)
    src, dst = rows(v["src"], EPAD, N), rows(v["dst"], EPAD, N)
    rec = np.zeros((EPAD, 2), np.float32)
    rec[:E, 0] = np.arange(E)
    rec[:E, 1] = v["edge_weight"]
    arrays = {
        "ident": np.eye(P, dtype=np.float32), "hmask": (i[:, None] // HD == np.arange(HEADS)[None, :]).astype(np.float32),
        "expand": (i[None, :] // HD == np.arange(HEADS)[:, None]).astype(np.float32),
        "iota": every(np.arange(LO, dtype=np.float32)), "iotap": np.stack([i, i + P, -i, -i - P], 1).astype(np.float32),
        "tri": np.stack([i[None, :] < i[:, None], i[:, None] < i[None, :], np.ones((P, P), bool)], 1).astype(np.float32),
        "sentinel": np.tile(np.array([[N, N, 0, 0]], np.float32), (PAD_ROWS, 1)),
        "x": rows(v["x"], NPAD), "factors": rows(v["L2_gnn_factors"], NPAD), "edge_attr": rows(v["edge_attr_128"], EPAD),
        "src_col": tiles(src), "dst_col": tiles(dst), "src_row": src[None], "dst_row": dst[None], "rec_col": tiles(rec),
        "linw": v["L0_gnn_lin_w"], "linwT": np.ascontiguousarray(v["L0_gnn_lin_w"].T),
        "projT": np.ascontiguousarray(v["L0_gnn_proj_w"].T),
        "att": np.stack([v["L0_gnn_att_src"].reshape(-1), v["L0_gnn_att_dst"].reshape(-1)], 1),
        "gatb": np.ascontiguousarray(every(v["L0_gnn_gat_bias"]).T), "projb": every(v["L0_gnn_proj_b"]),
        "g0": every(v["L0_gnn_ln_gamma"]), "be0": every(v["L0_gnn_ln_beta"]),
        "we": v["L1_gnn_W_e_k"], "bee": v["L1_gnn_W_e_b"].reshape(-1, 1), "eps1": every(v["L1_gnn_eps"]),
        "w1": v["L1_gnn_W1"], "glob": v["L1_gnn_globals_g"].reshape(-1, 1),
        "b1": np.ascontiguousarray(v["L1_gnn_b1"].reshape(4, P).T), "w2": v["L1_gnn_W2"], "b2": every(v["L1_gnn_b2"]),
        "wm": v["L2_gnn_Wm"], "bm": v["L2_gnn_bm"].reshape(-1, 1), "wc": v["L2_gnn_Wc"], "bc": every(v["L2_gnn_bc"]),
        "w3": v["L3_gnn_weight"], "b3": every(v["L3_gnn_bias"]), "g3": every(v["L3_gnn_ln_gamma"]), "be3": every(v["L3_gnn_ln_beta"]),
    }
    nc = bacc.Bacc("TRN2", target_bir_lowering=False, num_devices=1)
    a = {n: nc.dram_tensor(f"in_{n}", x.shape, mybir.dt.from_np(x.dtype), kind="ExternalInput").ap() for n, x in arrays.items()}
    out = nc.dram_tensor("out_x", (NPAD, D), F32, kind="ExternalOutput").ap()
    program(nc, a, out)
    r = run_bass_kernel_spmd(nc, [{f"in_{n}": x for n, x in arrays.items()}], core_ids=[0])
    return r.results[0]["out_x"][:N]
```
